# Optimizing a Trainium2 kernel written in Bass

```python
import numpy as np
import jax
import jax.numpy as jnp

def _softmax(x, axis=-1):
    return jax.nn.softmax(x, axis=axis)

def _gelu(x):
    return jax.nn.gelu(x, approximate=True)

def _silu(x):
    return jax.nn.silu(x)

def _sigmoid(x):
    return jax.nn.sigmoid(x)

def _layernorm(x, axis=-1, eps=1e-05):
    m = jnp.mean(x, axis=axis, keepdims=True)
    v = jnp.var(x, axis=axis, keepdims=True)
    return (x - m) / jnp.sqrt(v + eps)

def _scatter_add(tgt, idx, src, axis=0):
    return tgt.at[idx].add(src)

def _segment_sum(src, seg, n):
    return jax.ops.segment_sum(src, seg, n)
kernel_name = 'mk_gnn_resnorm_d2_gnn_r32_fb142f'

def setup_inputs(seed: int=0):
    np.random.seed(seed)
    _w = jnp.asarray

    def _rec_inputs():
        import jax
        import jax.numpy as jnp
        _gk = jax.random.key(seed)
        x = -0.0009044 + 1 * jax.random.normal(jax.random.fold_in(_gk, 1), (3125, 160), jnp.float32)
        src = jax.random.randint(jax.random.fold_in(_gk, 2), (100000,), 0, 3125, jnp.int32)
        dst = jax.random.randint(jax.random.fold_in(_gk, 3), (100000,), 0, 3125, jnp.int32)
        _o = jnp.argsort(dst, stable=True)
        src = src[_o]
        dst = dst[_o]
        edge_attr_3 = 0.00047201 + 1.00023 * jax.random.normal(jax.random.fold_in(_gk, 12), (100000, 3), jnp.float32)
        edge_attr_4 = -0.000149047 + 1.00006 * jax.random.normal(jax.random.fold_in(_gk, 13), (100000, 4), jnp.float32)
        edge_attr_64 = 0.000279952 + 1.00013 * jax.random.normal(jax.random.fold_in(_gk, 14), (100000, 64), jnp.float32)
        edge_attr_8 = 0.000735704 + 1.0001 * jax.random.normal(jax.random.fold_in(_gk, 15), (100000, 8), jnp.float32)
        node_vec1 = jax.random.uniform(jax.random.fold_in(_gk, 17), (3125, 1), jnp.float32, 0.0, 1)
        return (x, src, dst, edge_attr_3, edge_attr_4, edge_attr_64, edge_attr_8, node_vec1)
    x, src, dst, edge_attr_3, edge_attr_4, edge_attr_64, edge_attr_8, node_vec1 = _rec_inputs()

    def _L0_gnn_setup():
        import jax, jax.numpy as jnp
        import numpy as np
        N_NODES = 10000
        N_EDGES = 10000
        NUM_NEIGHBORS = 32.0
        INV_SQRT3 = 1.0 / np.sqrt(3.0)

        def _fctp_scalar_attr(xs, xv, Ws, Wv, a):
            out_s = xs @ Ws * (a / np.sqrt(xs.shape[1]))[:, None]
            out_v = jnp.einsum('nuc,uw->nwc', xv, Wv) * (a / np.sqrt(xv.shape[1]))[:, None, None]
            return (out_s, out_v)
        key = jax.random.key(seed)
        ks = jax.random.split(key, 16)
        f32 = jnp.float32
        return {'node_input': jax.random.normal(ks[0], (N_NODES, 160), f32), 'node_attr': jnp.ones((N_NODES, 1), f32), 'edge_attr': jax.random.normal(ks[1], (N_EDGES, 4), f32), 'edge_scalar_attr': jax.random.normal(ks[2], (N_EDGES, 8), f32), 'Wsc0': jax.random.normal(ks[3], (64, 64), f32), 'Wsc1': jax.random.normal(ks[4], (32, 32), f32), 'Wl1_0': jax.random.normal(ks[5], (64, 64), f32), 'Wl1_1': jax.random.normal(ks[6], (32, 32), f32), 'Wfc1': jax.random.normal(ks[7], (8, 64), f32), 'Wfc2': jax.random.normal(ks[8], (64, 64), f32), 'Wfc3': jax.random.normal(ks[9], (64, 192), f32), 'Wl2_s': jax.random.normal(ks[10], (96, 64), f32), 'Wl2_v': jax.random.normal(ks[11], (96, 32), f32), 'Wa': jax.random.normal(ks[12], (96, 1), f32), 'edge_src': jax.random.randint(ks[13], (N_EDGES,), 0, N_NODES), 'edge_dst': jax.random.randint(ks[14], (N_EDGES,), 0, N_NODES)}
    _L0_gnn_all = _L0_gnn_setup()
    _L0_gnn_in = {k: v for k, v in _L0_gnn_all.items() if k in ('Wsc0', 'Wsc1', 'Wl1_0', 'Wl1_1', 'Wfc1', 'Wfc2', 'Wfc3', 'Wl2_s', 'Wl2_v', 'Wa')}
    del _L0_gnn_all

    def _L1_gnn_setup():
        import jax, jax.numpy as jnp
        import numpy as np
        N_NODES = 10000
        N_EDGES = 10000
        MUL0, MUL1 = (64, 32)
        EDGE_DIM = 64
        W_NUMEL = 224
        DENOM = 32.0
        SQRT3 = 3.0 ** 0.5
        INV_SQRT3 = 1.0 / SQRT3
        INV_SQRT2 = 2.0 ** (-0.5)

        def _forward(node_feature, edge_attr, edge_feature, W_skip0, W_skip1, W_nl0, W_nl1, W_fc1, W_fc2, W_out_s, W_out_v, edge_index):
            N = node_feature.shape[0]
            E = edge_attr.shape[0]
            s = node_feature[:, :MUL0]
            v = node_feature[:, MUL0:].reshape(N, MUL1, 3)
            skip_s = s @ W_skip0
            skip_v = jnp.einsum('nmi,mk->nki', v, W_skip1)
            s = s @ W_nl0
            v = jnp.einsum('nmi,mk->nki', v, W_nl1)
            rhat = edge_attr / jnp.linalg.norm(edge_attr, axis=-1, keepdims=True)
            sh1 = SQRT3 * rhat
            w = jax.nn.relu(edge_feature @ W_fc1) @ W_fc2
            w0, w1, w2, w3, w4 = jnp.split(w, [64, 128, 160, 192], axis=-1)
            src, dst = (edge_index[0], edge_index[1])
            xs = s[dst]
            xv = v[dst]
            out0a = w0 * xs
            out0b = w3 * (jnp.einsum('emi,ei->em', xv, sh1) * INV_SQRT3)
            out1a = (w1 * xs)[:, :, None] * sh1[:, None, :]
            out1b = w2[:, :, None] * xv
            out1c = w4[:, :, None] * (jnp.cross(xv, sh1[:, None, :]) * INV_SQRT2)
            tp = jnp.concatenate([out0a, out0b, out1a.reshape(E, -1), out1b.reshape(E, -1), out1c.reshape(E, -1)], axis=-1)
            agg = jax.ops.segment_sum(tp, src, num_segments=N) / DENOM
            agg_s = agg[:, :96]
            agg_v = agg[:, 96:].reshape(N, 128, 3)
            out_s = agg_s @ W_out_s + skip_s
            out_v = jnp.einsum('nmi,mk->nki', agg_v, W_out_v) + skip_v
            fs = jax.nn.silu(out_s[:, :MUL0])
            gate = jax.nn.sigmoid(out_s[:, MUL0:MUL0 + 32])
            gv = gate[:, :, None] * out_v
            return jnp.concatenate([fs, gv.reshape(N, -1)], axis=-1)
        key = jax.random.key(seed)
        ks = jax.random.split(key, 12)

        def lin(k, fi, fo):
            return jax.random.normal(k, (fi, fo), jnp.float32) / np.float32(np.sqrt(fi))
        return {'node_feature': jax.random.normal(ks[0], (N_NODES, MUL0 + 3 * MUL1), jnp.float32), 'edge_attr': jax.random.normal(ks[1], (N_EDGES, 3), jnp.float32), 'edge_feature': jax.random.normal(ks[2], (N_EDGES, EDGE_DIM), jnp.float32), 'W_skip0': lin(ks[3], MUL0, 96), 'W_skip1': lin(ks[4], MUL1, 32), 'W_nl0': lin(ks[5], MUL0, MUL0), 'W_nl1': lin(ks[6], MUL1, MUL1), 'W_fc1': lin(ks[7], EDGE_DIM, 64), 'W_fc2': lin(ks[8], 64, W_NUMEL), 'W_out_s': lin(ks[9], 96, 96), 'W_out_v': lin(ks[10], 128, 32), 'edge_index': jax.random.randint(ks[11], (2, N_EDGES), 0, N_NODES)}
    _L1_gnn_all = _L1_gnn_setup()
    _L1_gnn_in = {k: v for k, v in _L1_gnn_all.items() if k in ('W_skip0', 'W_skip1', 'W_nl0', 'W_nl1', 'W_fc1', 'W_fc2', 'W_out_s', 'W_out_v')}
    del _L1_gnn_all
    return {'x': x, 'src': src, 'dst': dst, 'edge_attr_3': edge_attr_3, 'edge_attr_4': edge_attr_4, 'edge_attr_64': edge_attr_64, 'edge_attr_8': edge_attr_8, 'node_vec1': node_vec1, 'L0_gnn_Wsc0': _L0_gnn_in['Wsc0'], 'L0_gnn_Wsc1': _L0_gnn_in['Wsc1'], 'L0_gnn_Wl1_0': _L0_gnn_in['Wl1_0'], 'L0_gnn_Wl1_1': _L0_gnn_in['Wl1_1'], 'L0_gnn_Wfc1': _L0_gnn_in['Wfc1'], 'L0_gnn_Wfc2': _L0_gnn_in['Wfc2'], 'L0_gnn_Wfc3': _L0_gnn_in['Wfc3'], 'L0_gnn_Wl2_s': _L0_gnn_in['Wl2_s'], 'L0_gnn_Wl2_v': _L0_gnn_in['Wl2_v'], 'L0_gnn_Wa': _L0_gnn_in['Wa'], 'L1_gnn_W_skip0': _L1_gnn_in['W_skip0'], 'L1_gnn_W_skip1': _L1_gnn_in['W_skip1'], 'L1_gnn_W_nl0': _L1_gnn_in['W_nl0'], 'L1_gnn_W_nl1': _L1_gnn_in['W_nl1'], 'L1_gnn_W_fc1': _L1_gnn_in['W_fc1'], 'L1_gnn_W_fc2': _L1_gnn_in['W_fc2'], 'L1_gnn_W_out_s': _L1_gnn_in['W_out_s'], 'L1_gnn_W_out_v': _L1_gnn_in['W_out_v']}

def reference(x, src, dst, edge_attr_3, edge_attr_4, edge_attr_64, edge_attr_8, node_vec1, L0_gnn_Wsc0, L0_gnn_Wsc1, L0_gnn_Wl1_0, L0_gnn_Wl1_1, L0_gnn_Wfc1, L0_gnn_Wfc2, L0_gnn_Wfc3, L0_gnn_Wl2_s, L0_gnn_Wl2_v, L0_gnn_Wa, L1_gnn_W_skip0, L1_gnn_W_skip1, L1_gnn_W_nl0, L1_gnn_W_nl1, L1_gnn_W_fc1, L1_gnn_W_fc2, L1_gnn_W_out_s, L1_gnn_W_out_v):
    import jax
    import jax.numpy as jnp

    def _L0_gnn_ref(node_input, node_attr, edge_attr, edge_scalar_attr, Wsc0, Wsc1, Wl1_0, Wl1_1, Wfc1, Wfc2, Wfc3, Wl2_s, Wl2_v, Wa, edge_src, edge_dst):
        import jax, jax.numpy as jnp
        import numpy as np
        N_NODES = 10000
        N_EDGES = 10000
        NUM_NEIGHBORS = 32.0
        INV_SQRT3 = 1.0 / np.sqrt(3.0)

        def _fctp_scalar_attr(xs, xv, Ws, Wv, a):
            out_s = xs @ Ws * (a / np.sqrt(xs.shape[1]))[:, None]
            out_v = jnp.einsum('nuc,uw->nwc', xv, Wv) * (a / np.sqrt(xv.shape[1]))[:, None, None]
            return (out_s, out_v)
        N = node_input.shape[0]
        a = node_attr[:, 0]
        xs = node_input[:, :64]
        xv = node_input[:, 64:].reshape(N, 32, 3)
        sc_s, sc_v = _fctp_scalar_attr(xs, xv, Wsc0, Wsc1, a)
        f_s, f_v = _fctp_scalar_attr(xs, xv, Wl1_0, Wl1_1, a)
        h = jax.nn.gelu(edge_scalar_attr @ Wfc1 / np.sqrt(8.0))
        h = jax.nn.gelu(h @ Wfc2 / np.sqrt(64.0))
        w = h @ Wfc3 / np.sqrt(64.0)
        w0, w1, w2, w3 = (w[:, :64], w[:, 64:128], w[:, 128:160], w[:, 160:192])
        gs = f_s[edge_src]
        gv = f_v[edge_src]
        y0 = edge_attr[:, 0]
        y1 = edge_attr[:, 1:4]
        mid0 = w0 * gs * y0[:, None]
        mid1 = w3 * jnp.einsum('euc,ec->eu', gv, y1) * INV_SQRT3
        mid2 = (w1 * gs)[:, :, None] * y1[:, None, :]
        mid3 = w2[:, :, None] * gv * y0[:, None, None]
        inv = 1.0 / np.sqrt(NUM_NEIGHBORS)
        seg = lambda x: jax.ops.segment_sum(x, edge_dst, num_segments=N) * inv
        ns0, ns1, nv2, nv3 = (seg(mid0), seg(mid1), seg(mid2), seg(mid3))
        mid_s = jnp.concatenate([ns0, ns1], axis=1)
        mid_v = jnp.concatenate([nv2, nv3], axis=1)
        out_s = mid_s @ Wl2_s * (a / np.sqrt(96.0))[:, None]
        out_v = jnp.einsum('nuc,uw->nwc', mid_v, Wl2_v) * (a / np.sqrt(96.0))[:, None, None]
        alpha = mid_s @ Wa * (a / np.sqrt(96.0))[:, None]
        res_s = sc_s + alpha * out_s
        res_v = sc_v + alpha[:, :, None] * out_v
        return jnp.concatenate([res_s, res_v.reshape(N, 96)], axis=1)

    def _L1_gnn_ref(node_feature, edge_attr, edge_feature, W_skip0, W_skip1, W_nl0, W_nl1, W_fc1, W_fc2, W_out_s, W_out_v, edge_index):
        import jax, jax.numpy as jnp
        import numpy as np
        N_NODES = 10000
        N_EDGES = 10000
        MUL0, MUL1 = (64, 32)
        EDGE_DIM = 64
        W_NUMEL = 224
        DENOM = 32.0
        SQRT3 = 3.0 ** 0.5
        INV_SQRT3 = 1.0 / SQRT3
        INV_SQRT2 = 2.0 ** (-0.5)

        def _forward(node_feature, edge_attr, edge_feature, W_skip0, W_skip1, W_nl0, W_nl1, W_fc1, W_fc2, W_out_s, W_out_v, edge_index):
            N = node_feature.shape[0]
            E = edge_attr.shape[0]
            s = node_feature[:, :MUL0]
            v = node_feature[:, MUL0:].reshape(N, MUL1, 3)
            skip_s = s @ W_skip0
            skip_v = jnp.einsum('nmi,mk->nki', v, W_skip1)
            s = s @ W_nl0
            v = jnp.einsum('nmi,mk->nki', v, W_nl1)
            rhat = edge_attr / jnp.linalg.norm(edge_attr, axis=-1, keepdims=True)
            sh1 = SQRT3 * rhat
            w = jax.nn.relu(edge_feature @ W_fc1) @ W_fc2
            w0, w1, w2, w3, w4 = jnp.split(w, [64, 128, 160, 192], axis=-1)
            src, dst = (edge_index[0], edge_index[1])
            xs = s[dst]
            xv = v[dst]
            out0a = w0 * xs
            out0b = w3 * (jnp.einsum('emi,ei->em', xv, sh1) * INV_SQRT3)
            out1a = (w1 * xs)[:, :, None] * sh1[:, None, :]
            out1b = w2[:, :, None] * xv
            out1c = w4[:, :, None] * (jnp.cross(xv, sh1[:, None, :]) * INV_SQRT2)
            tp = jnp.concatenate([out0a, out0b, out1a.reshape(E, -1), out1b.reshape(E, -1), out1c.reshape(E, -1)], axis=-1)
            agg = jax.ops.segment_sum(tp, src, num_segments=N) / DENOM
            agg_s = agg[:, :96]
            agg_v = agg[:, 96:].reshape(N, 128, 3)
            out_s = agg_s @ W_out_s + skip_s
            out_v = jnp.einsum('nmi,mk->nki', agg_v, W_out_v) + skip_v
            fs = jax.nn.silu(out_s[:, :MUL0])
            gate = jax.nn.sigmoid(out_s[:, MUL0:MUL0 + 32])
            gv = gate[:, :, None] * out_v
            return jnp.concatenate([fs, gv.reshape(N, -1)], axis=-1)
        return _forward(node_feature, edge_attr, edge_feature, W_skip0, W_skip1, W_nl0, W_nl1, W_fc1, W_fc2, W_out_s, W_out_v, edge_index)
    edge_index = jnp.stack([src, dst])
    x = _layernorm(x + _L0_gnn_ref(x, node_vec1, edge_attr_4, edge_attr_8, L0_gnn_Wsc0, L0_gnn_Wsc1, L0_gnn_Wl1_0, L0_gnn_Wl1_1, L0_gnn_Wfc1, L0_gnn_Wfc2, L0_gnn_Wfc3, L0_gnn_Wl2_s, L0_gnn_Wl2_v, L0_gnn_Wa, src, dst), axis=-1)
    x = _layernorm(x + _L1_gnn_ref(x, edge_attr_3, edge_attr_64, L1_gnn_W_skip0, L1_gnn_W_skip1, L1_gnn_W_nl0, L1_gnn_W_nl1, L1_gnn_W_fc1, L1_gnn_W_fc2, L1_gnn_W_out_s, L1_gnn_W_out_v, edge_index), axis=-1)
    return x

_drawn_inputs = setup_inputs


def setup_inputs(seed=0):
    import zlib

    import numpy as np

    out = dict(_drawn_inputs(seed))
    spreads = {}
    factors = {'edge_attr_4': 2.896,
     'edge_attr_8': 3.07,
     'L0_gnn_Wl1_0': 3.248,
     'L0_gnn_Wl1_1': 3.579,
     'L0_gnn_Wfc1': 3.228,
     'L0_gnn_Wfc2': 3.04,
     'L0_gnn_Wfc3': 3.045,
     'L0_gnn_Wl2_s': 4.572,
     'L0_gnn_Wl2_v': 3.779,
     'L0_gnn_Wa': 2.672}
    for name, (base, spread) in spreads.items():
        noise = np.random.default_rng([zlib.crc32(name.encode()), seed]).standard_normal(out[name].shape)
        drawn = base * np.exp(spread * noise) if base else spread * noise
        out[name] = jnp.asarray(drawn.astype(out[name].dtype))
    for name, factor in factors.items():
        out[name] = (out[name] * factor).astype(out[name].dtype)
    return out
```

```python
from contextlib import ExitStack

import concourse.bass as bass
from concourse import mybir
from concourse.alu_op_type import AluOpType as ALU

F32 = mybir.dt.float32
I32 = mybir.dt.int32
ACT = mybir.ActivationFunctionType
AX = mybir.AxisListType

N, E = 3125, 100000
P = 128
NT = -(-N // P)
NP = NT * P
S, V = 64, 32
D = S + 3 * V
G = 4
NGRP = -(-E // (P * G))
NGRP += NGRP % 2
TILES = NGRP * G
EP = TILES * P
GE = G * P
WIN = 24
SWEEP = -(-(N + 1) // WIN)
ACCW = max(NP, N + WIN, SWEEP * WIN)
NTAB = 4
TROWS = 26 * P
OW = 96 + 96
GW = S + 5 * V
NPAIR = TILES // 2
EPS = 1e-5


def since(eng, sem, count):
    if not isinstance(count, int) or count > 0:
        eng.wait_ge(sem, count)


def settled(eng, sem, count, passed):
    since(eng, sem, count)
    if not isinstance(count, int):
        eng.sem_inc(passed, 1)


def steps(eng, total, body, first, unroll):
    first = min(-(-first // unroll) * unroll, total)
    last = max(first, total // unroll * unroll)
    for s in range(first):
        body(s, s // unroll, s % unroll)
    if last > first:
        with eng.Fori(first // unroll, last // unroll) as j:
            for r in range(unroll):
                body(j * unroll + r, j, r)
    for s in range(last, total):
        body(s, s // unroll, s % unroll)


def lagged(s, j, r, lag, unroll):
    return s - lag, j + (r - lag) // unroll, (r - lag) % unroll


def runs(u, total):
    return not isinstance(u, int) or 0 <= u < total


def gnn_kernel(nc, t, out):
    top = ExitStack()
    with top:
        def sb(ctx, name, shape, dt=F32):
            return ctx.enter_context(nc.sbuf_tensor(name, shape, dt))

        def pb(ctx, name, shape, dt=F32):
            return ctx.enter_context(nc.psum_tensor(name, shape, dt))

        def sem(ctx, name):
            return ctx.enter_context(nc.semaphore(name))

        src_f = sb(top, "src_f", [P, TILES])
        rel_f = sb(top, "rel_f", [P, TILES])
        dst_f = sb(top, "dst_f", [P, TILES])
        src_i = sb(top, "src_i", [P, TILES], I32)
        dst_i = sb(top, "dst_i", [P, TILES], I32)
        scat_i = sb(top, "scat_i", [P, TILES], I32)
        base_i = sb(top, "base_i", [P, NGRP], I32)
        sh = sb(top, "sh", [P, TILES, 5])
        cnt = sb(top, "cnt", [P, TILES])
        lower = sb(top, "lower", [P, P])
        ident = sb(top, "ident", [P, P])
        xres = sb(top, "xres", [P, NT, D])
        a_col = sb(top, "a_col", [P, NT])
        a2_col = sb(top, "a2_col", [P, NT])
        win_ok = sb(top, "win_ok", [P, 1], I32)
        mv = sb(top, "mv", [P, NT, 2])
        rstd = sb(top, "rstd", [P, NT])
        ntmp = sb(top, "ntmp", [P, 2, NT])

        passed = sem(top, "passed")

        def rows(dram, tile):
            return dram[bass.ds(tile * P, P), :]

        with ExitStack() as c1:
            acc_zero = sb(c1, "acc_zero", [P, TROWS // P * OW])
            ea3 = sb(c1, "ea3", [P, TILES, 3])
            sq = sb(c1, "sq", [P, TILES, 3])
            nrm = sb(c1, "nrm", [P, 4, TILES])
            base_f = sb(c1, "base_f", [P, NGRP])
            rows_i = sb(c1, "rows_i", [NGRP // 2, 2, GE], I32)
            rows_f = sb(c1, "rows_f", [NGRP // 2, 2, GE])
            ones = sb(c1, "ones", [P, P])
            ext = sb(c1, "ext", [P, 4])
            w_s = sb(c1, "w_s", [S, 2, S])
            w_v = sb(c1, "w_v", [96, 2, 96])
            w_s2 = sb(c1, "w_s2", [S, 2, S])
            w_v2 = sb(c1, "w_v2", [96, 2, 96])
            xt_s = sb(c1, "xt_s", [S, 2, P])
            xt_v = sb(c1, "xt_v", [96, 2, P])
            frow = sb(c1, "frow", [P, 2, D])
            ps_n = [pb(c1, f"ps_n{i}", [P, 512]) for i in range(2)]
            ps_e = pb(c1, "ps_e", [P, 512])
            idx_in, attr_in, rows_in = sem(c1, "idx_in"), sem(c1, "attr_in"), sem(c1, "rows_in")
            wn_zero, wn_in, wn_scaled = sem(c1, "wn_zero"), sem(c1, "wn_in"), sem(c1, "wn_scaled")
            x_in, a_in = sem(c1, "x_in"), sem(c1, "a_in")
            xt_in = [sem(c1, f"xt_in{i}") for i in range(2)]
            f_out = [sem(c1, f"f_out{i}") for i in range(2)]
            consts, rowsf_done, rows_out = sem(c1, "consts"), sem(c1, "rowsf_done"), sem(c1, "rows_out")
            conv, ext_done, cnt_ps = sem(c1, "conv"), sem(c1, "ext_done"), sem(c1, "cnt_ps")
            sq_done, root_done = sem(c1, "sq_done"), sem(c1, "root_done")
            n_ready, f_ready, res_ready = sem(c1, "n_ready"), sem(c1, "f_ready"), sem(c1, "res_ready")
            zeroed, tab_out, dv = sem(c1, "zeroed"), sem(c1, "tab_out"), sem(c1, "dv")
            block = c1.enter_context(nc.Block())

            @block.sync
            def _(sp):
                sp.dma_start(src_i[:, :], t["src_col"]).then_inc(idx_in, 16)
                sp.dma_start(dst_i[:, :], t["dst_col"]).then_inc(idx_in, 16)
                sp.dma_start(base_i[:, :], t["dst_first"][0:1, :].to_broadcast([P, NGRP])).then_inc(idx_in, 16)
                sp.dma_start(rows_i[:, :, :], t["src_rows"].rearrange("(p a) e -> p a e", a=2)).then_inc(rows_in, 16)
                sp.dma_start(ea3[:, :, :], t["ea3"]).then_inc(attr_in, 16)
                sp.dma_start(xres[:, :, :], t["x_rows"]).then_inc(x_in, 16)
                sp.dma_start(a_col[:, :], t["a_col"]).then_inc(a_in, 16)
                sp.wait_ge(wn_zero, 1)
                sp.dma_start(w_s[:, 0, :], t["L0_gnn_Wl1_0"]).then_inc(wn_in, 16)
                sp.dma_start(w_s[:, 1, :], t["L0_gnn_Wsc0"]).then_inc(wn_in, 16)
                for c in range(3):
                    for k, name in enumerate(("L0_gnn_Wl1_1", "L0_gnn_Wsc1")):
                        sp.dma_start(w_v[V * c:V * c + V, k, V * c:V * c + V], t[name]).then_inc(wn_in, 16)

                def load_xt(u, j, r):
                    since(sp, n_ready, u - 1)
                    sp.dma_start(xt_s[:, r, :], t["xt"][bass.ds(u, 1), 0:S, :].squeeze(0)).then_inc(xt_in[r], 16)
                    sp.dma_start(xt_v[:, r, :], t["xt"][bass.ds(u, 1), S:D, :].squeeze(0)).then_inc(xt_in[r], 16)
                steps(sp, NT, load_xt, 2, 2)
                sp.wait_ge(rowsf_done, 1)
                sp.dma_start(t["src_rows_f"].rearrange("(p a) e -> p a e", a=2), rows_f[:, :, :]).then_inc(rows_out, 16)
                sp.wait_ge(rows_out, 16)

            @block.gpsimd
            def _(pool):
                pool.memset(w_v[:, :, :], 0.0).then_inc(wn_zero, 1)
                pool.memset(ones[:, :], 1.0).then_inc(consts, 1)
                pool.memset(lower[:, :], 1.0).then_inc(consts, 1)
                pool.memset(ident[:, :], 0.0).then_inc(consts, 1)
                pool.wait_ge(consts, 3)
                pool.affine_select(out=lower[:, :], in_=lower[:, :], compare_op=ALU.is_ge, fill=0.0,
                                   base=-1, pattern=[[-1, P]], channel_multiplier=1).then_inc(consts, 1)
                pool.affine_select(out=ident[:, :], in_=ident[:, :], compare_op=ALU.not_equal, fill=1.0,
                                   base=0, pattern=[[-1, P]], channel_multiplier=1).then_inc(consts, 1)
                pool.memset(acc_zero[:, :], 0.0).then_inc(zeroed, 1)
                pool.wait_ge(consts, 5)

            @block.tensor
            def _(pe):
                pe.wait_ge(wn_scaled, 2)

                def project(u, j, r):
                    pe.wait_ge(xt_in[r], 32 * (j + 1))
                    since(pe, f_ready, u - 1)
                    since(pe, res_ready, u - 1)
                    parts = ps_n[r][:, 0:320].rearrange("p (k f) -> p k f", k=2)
                    pe.matmul(parts[:, :, 0:S], xt_s[:, r, :], w_s2[:, :, :], start=True, stop=True)
                    pe.matmul(parts[:, :, S:D], xt_v[:, r, :], w_v2[:, :, :], start=True, stop=True).then_inc(n_ready, 1)
                steps(pe, NT, project, 2, 2)
                pe.wait_ge(ext_done, 1)
                pe.wait_ge(consts, 1)
                pe.matmul(ps_e[:, 0:1], ones[:, :], ext[:, 2:3], start=True, stop=True).then_inc(cnt_ps, 1)

            @block.scalar
            def _(act):
                act.wait_ge(zeroed, 1)
                for tab in t["tabs"]:
                    act.dma_start(tab.rearrange("(p a) f -> p (a f)", p=P), acc_zero[:, :]).then_inc(tab_out, 16)
                act.wait_ge(wn_in, 16 * 8)
                act.activation(w_s2[:, :, :], w_s[:, :, :], ACT.Copy, scale=1.0 / 8.0).then_inc(wn_scaled, 1)
                act.activation(w_v2[:, :, :], w_v[:, :, :], ACT.Copy, scale=float(V) ** -0.5).then_inc(wn_scaled, 1)
                act.wait_ge(a_in, 16)

                def table(u, j, r):
                    act.wait_ge(n_ready, u + 1)
                    since(act, f_out[r], 16 * j)
                    act.activation(frow[:, r, :], ps_n[r][:, 0:D], ACT.Copy,
                                   scale=a_col[:, bass.ds(u, 1)]).then_inc(f_ready, 1)
                    act.wait_ge(f_ready, u + 1)
                    act.dma_start(rows(t["f0"], u), frow[:, r, :]).then_inc(f_out[r], 16)
                steps(act, NT, table, 2, 2)
                act.wait_ge(sq_done, 1)
                act.activation(nrm[:, 1, :], nrm[:, 0, :], ACT.Sqrt).then_inc(root_done, 1)
                act.wait_ge(tab_out, 16 * NTAB)
                act.wait_ge(f_out[0], 16 * (-(-NT // 2)))
                act.wait_ge(f_out[1], 16 * (NT // 2))

            @block.vector
            def _(dve):
                done = [0]

                def link(ins):
                    done[0] += 1
                    ins.then_inc(dv, 1)
                    dve.wait_ge(dv, done[0])

                dve.wait_ge(attr_in, 16)
                link(dve.tensor_tensor(sq[:, :, :], ea3[:, :, :], ea3[:, :, :], ALU.mult))
                dve.tensor_reduce(nrm[:, 0, :], sq[:, :, :], AX.X, ALU.add).then_inc(sq_done, 1)
                dve.wait_ge(idx_in, 48)
                dve.tensor_copy(src_f[:, :], src_i[:, :]).then_inc(conv, 1)
                dve.tensor_copy(dst_f[:, :], dst_i[:, :]).then_inc(conv, 1)
                dve.tensor_copy(base_f[:, :], base_i[:, :]).then_inc(conv, 1)
                dve.wait_ge(rows_in, 16)
                dve.tensor_copy(rows_f[:, :, :], rows_i[:, :, :]).then_inc(rowsf_done, 1)
                dve.wait_ge(conv, 3)
                link(dve.tensor_tensor(rel_f[:, :].rearrange("p (g k) -> p g k", k=G),
                                       dst_f[:, :].rearrange("p (g k) -> p g k", k=G),
                                       base_f[:, :].unsqueeze(2).to_broadcast([P, NGRP, G]), ALU.subtract))
                dve.wait_ge(a_in, 16)
                dve.tensor_tensor(a2_col[:, :], a_col[:, :], a_col[:, :], ALU.mult)
                link(dve.tensor_reduce(ext[:, 0:1], rel_f[:, :], AX.X, ALU.max))
                link(dve.tensor_reduce(ext[:, 1:2], rel_f[:, :], AX.X, ALU.min))
                link(dve.tensor_scalar(ext[:, 0:1], ext[:, 0:1], float(WIN), None, ALU.is_ge))
                link(dve.tensor_scalar(ext[:, 1:2], ext[:, 1:2], 0.0, None, ALU.is_lt))
                dve.tensor_tensor(ext[:, 2:3], ext[:, 0:1], ext[:, 1:2], ALU.add).then_inc(ext_done, 1)

                dve.wait_ge(x_in, 16)

                def residual(u, j, r):
                    dve.wait_ge(f_ready, u + 1)
                    here = xres[:, bass.ds(u, 1), :].squeeze(1)
                    dve.scalar_tensor_tensor(here, ps_n[r][:, D:2 * D], a_col[:, bass.ds(u, 1)], here,
                                             ALU.mult, ALU.add).then_inc(res_ready, 1)
                steps(dve, NT, residual, 2, 2)

                dve.wait_ge(root_done, 1)
                link(dve.reciprocal(nrm[:, 2, :], nrm[:, 1, :]))
                link(dve.tensor_tensor(nrm[:, 3, :], nrm[:, 2, :], nrm[:, 2, :], ALU.mult))
                link(dve.tensor_tensor(nrm[:, 3, :], nrm[:, 3, :], nrm[:, 0, :], ALU.mult))
                link(dve.tensor_scalar(nrm[:, 3, :], nrm[:, 3, :], -0.5 * 3.0 ** 0.5, 1.5 * 3.0 ** 0.5, ALU.mult, ALU.add))
                link(dve.tensor_tensor(nrm[:, 2, :], nrm[:, 2, :], nrm[:, 3, :], ALU.mult))
                link(dve.tensor_tensor(sh[:, :, 0:3], ea3[:, :, :],
                                       nrm[:, 2, :].unsqueeze(2).to_broadcast([P, TILES, 3]), ALU.mult))
                link(dve.tensor_copy(sh[:, :, 3:5], sh[:, :, 0:2]))
                dve.wait_ge(cnt_ps, 1)
                link(dve.tensor_scalar(win_ok[:, :], ps_e[:, 0:1], 0.0, None, ALU.is_equal))

        with ExitStack() as cacc:
            acc_a = sb(cacc, "acc_a", [P, 4, ACCW])
            acc_b = sb(cacc, "acc_b", [96, 1, ACCW])
            acc_c = sb(cacc, "acc_c", [96, 3, ACCW])
            with ExitStack() as c2:
                w1 = sb(c2, "w1", [16, P])
                w2 = sb(c2, "w2", [P, P])
                w3 = sb(c2, "w3", [P, 192])
                w3raw = sb(c2, "w3raw", [P, 192])
                ea8 = sb(c2, "ea8", [16, 2, 256])
                y = sb(c2, "y", [P, TILES, 4])
                h1 = sb(c2, "h1", [P, 2, 256])
                h2 = sb(c2, "h2", [P, 2, 256])
                gat = sb(c2, "gat", [P, 2, G, D])
                src_bc = sb(c2, "src_bc", [P, 2, G, P])
                eq_junk = sb(c2, "eq_junk", [P, G, P])
                pos = sb(c2, "pos", [P, WIN])
                ohot = sb(c2, "ohot", [P, G, WIN])
                sel = sb(c2, "sel", [P, 2, G, 4, WIN])
                ta = sb(c2, "ta", [P, 2, G, 2, S])
                tb = sb(c2, "tb", [P, 2, G, 3, V])
                tc = sb(c2, "tc", [P, 2, G, 3, V])
                dcur = sb(c2, "dcur", [P, G])
                ps_h1, ps_h2 = (pb(c2, n, [P, 512])[:, 0:256] for n in ("ps_h1", "ps_h2"))
                ps_w = [pb(c2, f"ps_w{i}", [P, G, 256]) for i in range(2)]
                ps_g = [pb(c2, f"ps_g{i}", [P, 512]) for i in range(2)]
                w_in, w_zero, w3_ok, y_in = sem(c2, "w_in"), sem(c2, "w_zero"), sem(c2, "w3_ok"), sem(c2, "y_in")
                acc_ok, pos_ok = sem(c2, "acc_ok"), sem(c2, "pos_ok")
                ea8_in = [sem(c2, f"ea8_in{i}") for i in range(2)]
                srcb_in = [sem(c2, f"srcb_in{i}") for i in range(2)]
                gath = [sem(c2, f"gath{i}") for i in range(2)]
                h1_ready, g1_done, h2_ready, g2_done = (sem(c2, n) for n in ("h1_ready", "g1_done", "h2_ready", "g2_done"))
                w_ready, cnt_done, hot_done, sel_ready = (sem(c2, n) for n in ("w_ready", "cnt_done", "hot_done", "sel_ready"))
                prod_done, agg_done, acc_done, cur_done = (sem(c2, n) for n in ("prod_done", "agg_done", "acc_done", "cur_done"))
                gidx = sb(c2, "gidx", [P, 2, 2 * G], I32)
                gidx_done = sem(c2, "gidx_done")
                block = c2.enter_context(nc.Block())

                @block.sync
                def _(sp):
                    sp.wait_ge(w_zero, 2)
                    for h in range(2):
                        sp.dma_start(w1[8 * h:8 * h + 8, S * h:S * h + S], t["L0_gnn_Wfc1"]).then_inc(w_in, 16)
                        sp.dma_start(w2[S * h:S * h + S, S * h:S * h + S], t["L0_gnn_Wfc2"]).then_inc(w_in, 16)
                        sp.dma_start(w3raw[S * h:S * h + S, :], t["L0_gnn_Wfc3"]).then_inc(w_in, 16)
                    sp.dma_start(y[:, :, :], t["ea4"]).then_inc(y_in, 16)

                    def load_ea8(u, r):
                        since(sp, h1_ready, u - 1)
                        sp.dma_start(ea8[:, r, :], t["ea8"][:, bass.ds(u * 256, 256)]).then_inc(ea8_in[r], 16)

                    def load(u, j, r):
                        if not isinstance(u, int) or u + 1 < NGRP:
                            load_ea8(u + 1, (r + 1) % 2)
                        since(sp, cnt_done, G * (u - 1))
                        sp.dma_start(src_bc[:, r, :, :].rearrange("p k e -> p (k e)"),
                                     t["src_rows_f"][bass.ds(u, 1), :].to_broadcast([P, GE])).then_inc(srcb_in[r], 16)
                    load_ea8(0, 0)
                    split_steps(sp, NGRP, 0, load, 2, short=1)

                @block.gpsimd
                def _(pool):
                    pool.memset(w1[:, :], 0.0).then_inc(w_zero, 1)
                    pool.memset(w2[:, :], 0.0).then_inc(w_zero, 1)
                    pool.iota(pos[:, :], pattern=[[1, WIN]], base=0, channel_multiplier=0,
                              allow_small_or_imprecise_dtypes=True).then_inc(pos_ok, 1)

                    def gather(u, j, r):
                        if r % 2 == 0:
                            since(pool, prod_done, u - 2)
                            pool.tensor_copy(gidx[:, r // 2, :], src_i[:, bass.ds(u * G, 2 * G)]).then_inc(gidx_done, 1)
                            since(pool, gidx_done, j * 2 + r // 2 + 1)
                        since(pool, prod_done, u - 1)
                        if not isinstance(u, int):
                            pool.sem_inc(passed, 1)
                        for k in range(G):
                            at = r % 2 * G + k
                            pool.indirect_dma_start(
                                out=gat[:, r % 2, k, :], out_offset=None, in_=t["f0"],
                                in_offset=bass.IndirectOffsetOnAxis(ap=gidx[:, r // 2, at:at + 1], axis=0),
                            ).then_inc(gath[r % 2], 16)
                    steps(pool, NGRP, gather, 4, 4)

                @block.scalar
                def _(act):
                    act.wait_ge(w_in, 16 * 6)
                    act.activation(w3[:, :], w3raw[:, :], ACT.Copy, scale=1.0 / 8.0).then_inc(w3_ok, 1)

                    def gelus(u, j, r):
                        act.wait_ge(h1_ready, u + 1)
                        since(act, h2_ready, u - 1)
                        act.activation(h1[:, r, :], ps_h1[:, :], ACT.Gelu_apprx_tanh,
                                       scale=8.0 ** -0.5).then_inc(g1_done, 1)
                        act.wait_ge(h2_ready, u + 1)
                        since(act, w_ready, u - 1)
                        act.activation(h2[:, r, :], ps_h2[:, :], ACT.Gelu_apprx_tanh,
                                       scale=1.0 / 8.0).then_inc(g2_done, 1)
                    steps(act, NGRP, gelus, 4, 2)

                def window_sums(pe, r, ready):
                    for n, (lhs, hi) in enumerate(((ta, P), (tb, 96), (tc, 96))):
                        for k in range(G):
                            last = pe.matmul(ps_g[r][0:hi, n * 4 * WIN:(n + 1) * 4 * WIN],
                                             lhs[:, r, k, :, :].rearrange("p a b -> p (a b)"),
                                             sel[:, r, k, :, :].rearrange("p a b -> p (a b)"),
                                             start=k == 0, stop=k == G - 1)
                    last.then_inc(ready, 1)

                @block.tensor
                def _(pe):
                    pe.wait_ge(w_in, 16 * 6)
                    pe.wait_ge(w3_ok, 1)

                    def layer1(u, r, j):
                        pe.wait_ge(ea8_in[r], 16 * (j + 1))
                        since(pe, g1_done, u)
                        pe.matmul(ps_h1[:, :], w1[:, :], ea8[:, r, :], start=True, stop=True).then_inc(h1_ready, 1)

                    def layer2(u, r):
                        pe.wait_ge(g1_done, u + 1)
                        since(pe, g2_done, u)
                        pe.matmul(ps_h2[:, :], w2[:, :], h1[:, r, :], start=True, stop=True).then_inc(h2_ready, 1)

                    def layer3(u, r):
                        pe.wait_ge(g2_done, u + 1)
                        since(pe, prod_done, u - 1)
                        for k in range(G):
                            h = S * (k // 2)
                            last = pe.matmul(ps_w[r][:, k, 0:192], h2[h:h + S, r, P * (k % 2):P * (k % 2) + P],
                                             w3[h:h + S, :], start=True, stop=True)
                        last.then_inc(w_ready, 1)

                    def fast():
                        def step(s, j, r):
                            if runs(s, NGRP):
                                layer1(s, r, j)
                            u, _, ur = lagged(s, j, r, 3, 2)
                            if runs(u, NGRP):
                                pe.wait_ge(sel_ready, u + 1)
                                pe.wait_ge(prod_done, u + 1)
                                since(pe, acc_done, u - 1)
                                window_sums(pe, ur, agg_done)
                            if runs(s, NGRP):
                                layer2(s, r)
                            u, _, ur = lagged(s, j, r, 1, 2)
                            if runs(u, NGRP):
                                layer3(u, ur)
                        split_steps(pe, NGRP, 3, step)

                    def general():
                        def step(u, j, r):
                            layer1(u, r, j)
                            layer2(u, r)
                            layer3(u, r)
                            settled(pe, prod_done, u + 1, passed)
                            with pe.Fori(0, SWEEP) as n:
                                pe.wait_ge(sel_ready, u * SWEEP + n + 1)
                                window_sums(pe, r, agg_done)
                                settled(pe, acc_done, u * SWEEP + n + 1, passed)
                        steps(pe, NGRP, step, 4, 2)

                    ok = pe.value_load(win_ok[0:1, 0:1], min_val=0, max_val=1)
                    with pe.If(ok):
                        fast()
                    with pe.Else():
                        general()

                @block.vector
                def _(dve):
                    dve.memset(acc_a[:, :, :], 0.0).then_inc(acc_ok, 1)
                    dve.memset(acc_b[:, :, :], 0.0).then_inc(acc_ok, 1)
                    dve.memset(acc_c[:, :, :], 0.0).then_inc(acc_ok, 1)
                    dve.wait_ge(acc_ok, 3)
                    dve.wait_ge(pos_ok, 1)
                    dve.wait_ge(y_in, 16)

                    def earlier(u, j, r):
                        dve.wait_ge(srcb_in[r], 16 * (j + 1))
                        since(dve, cnt_done, u * G)
                        for k in range(G):
                            col = bass.ds(u * G + k, 1)
                            dve.scalar_tensor_tensor(eq_junk[:, k, :], src_bc[:, r, k, :], src_f[:, col], lower[:, :],
                                                     ALU.is_equal, ALU.mult,
                                                     accum_out=cnt[:, col]).then_inc(cnt_done, 1)

                    def select(u, r, rel, hot_count):
                        since(dve, sel_ready, hot_count - 1)
                        dve.tensor_tensor(ohot[:, :, :], pos[:, :].unsqueeze(1).to_broadcast([P, G, WIN]),
                                          rel.unsqueeze(2).to_broadcast([P, G, WIN]), ALU.is_equal).then_inc(hot_done, 1)
                        dve.wait_ge(hot_done, hot_count)
                        dve.tensor_tensor(sel[:, r, :, :, :], ohot[:, :, :].unsqueeze(2).to_broadcast([P, G, 4, WIN]),
                                          y[:, bass.ds(u * G, G), :].unsqueeze(3).to_broadcast([P, G, 4, WIN]),
                                          ALU.mult).then_inc(sel_ready, 1)

                    def products(u, j, r):
                        dve.wait_ge(w_ready, u + 1)
                        dve.wait_ge(gath[r], 16 * G * (j + 1))
                        dve.tensor_tensor(ta[:, r, :, :, :], ps_w[r][:, :, 0:2 * S].rearrange("p k (a s) -> p k a s", a=2),
                                          gat[:, r, :, 0:S].unsqueeze(2).to_broadcast([P, G, 2, S]), ALU.mult)
                        gv = gat[:, r, :, S:D].rearrange("p k (c u) -> p k c u", c=3)
                        for dst, at in ((tb, 2 * S), (tc, 2 * S + V)):
                            last = dve.tensor_tensor(dst[:, r, :, :, :],
                                                     ps_w[r][:, :, at:at + V].unsqueeze(2).to_broadcast([P, G, 3, V]),
                                                     gv, ALU.mult)
                        last.then_inc(prod_done, 1)

                    def add_window(r, base):
                        for acc, hi, at, n in ((acc_a, P, 0, 4), (acc_b, 96, 4 * WIN, 1), (acc_c, 96, 9 * WIN, 3)):
                            part = acc[:, :, bass.ds(base, WIN)]
                            last = dve.tensor_tensor(part, part,
                                                     ps_g[r][0:hi, at:at + n * WIN].rearrange("p (c w) -> p c w", c=n),
                                                     ALU.add)
                        last.then_inc(acc_done, 1)

                    def fast():
                        def step(s, j, r):
                            if runs(s, NGRP):
                                since(dve, agg_done, s - 1)
                                select(s, r, rel_f[:, bass.ds(s * G, G)], s + 1)
                                products(s, j, r)
                            u, _, ur = lagged(s, j, r, 2, 2)
                            if runs(s, NGRP):
                                earlier(s, j, r)
                            if runs(u, NGRP):
                                base = dve.value_load(base_i[0:1, bass.ds(u, 1)], min_val=0, max_val=N)
                                dve.wait_ge(agg_done, u + 1)
                                since(dve, acc_done, u)
                                add_window(ur, base)
                        split_steps(dve, NGRP, 2, step)

                    def general():
                        def step(u, j, r):
                            earlier(u, j, r)
                            since(dve, acc_done, u * SWEEP)
                            products(u, j, r)
                            settled(dve, cur_done, u * (SWEEP + 1), passed)
                            dve.tensor_copy(dcur[:, :], dst_f[:, bass.ds(u * G, G)]).then_inc(cur_done, 1)
                            with dve.Fori(0, SWEEP) as n:
                                dve.wait_ge(cur_done, u * (SWEEP + 1) + n + 1)
                                select(u, r, dcur[:, :], u * SWEEP + n + 1)
                                dve.wait_ge(agg_done, u * SWEEP + n + 1)
                                add_window(r, n * WIN)
                                dve.tensor_scalar(dcur[:, :], dcur[:, :], float(-WIN), None, ALU.add).then_inc(cur_done, 1)
                        steps(dve, NGRP, step, 4, 2)

                    ok = dve.value_load(win_ok[0:1, 0:1], min_val=0, max_val=1)
                    with dve.If(ok):
                        fast()
                    with dve.Else():
                        general()

            with ExitStack() as c3:
                r_raw = sb(c3, "r_raw", [P, 5, 96])
                r_s = sb(c3, "r_s", [P, 4, 65])
                r_v = sb(c3, "r_v", [P, 4, 96])
                st_a = sb(c3, "st_a", [P, 2, 4, P])
                st_b = sb(c3, "st_b", [96, 2, P])
                st_c = sb(c3, "st_c", [96, 2, 3, P])
                agg, ag_done = sb(c3, "agg", [P, 2]), sem(c3, "ag_done")
                alpha = sb(c3, "alpha", [P, 2, 1])
                bst = sb(c3, "bst", [P, 2, 6])
                colf = sb(c3, "colf", [P, TILES])
                pidx = sb(c3, "pidx", [P, 1])
                wn_s = sb(c3, "wn_s", [S, 160])
                wn_v = sb(c3, "wn_v", [96, 2, 96])
                xt2_s = sb(c3, "xt2_s", [S, 2, P])
                xt2_v = sb(c3, "xt2_v", [96, 2, P])
                yrow = sb(c3, "yrow", [P, 2, GW])
                ps_r = [pb(c3, f"ps_r{i}", [P, 512]) for i in range(2)]
                ps_x = [pb(c3, f"ps_x{i}", [P, 4, P]) for i in range(2)]
                ps_y = [pb(c3, f"ps_y{i}", [P, 512]) for i in range(2)]
                rz, r_in, r_ok = sem(c3, "rz"), sem(c3, "r_in"), sem(c3, "r_ok")
                st_act, st_dve = sem(c3, "st_act"), sem(c3, "st_dve")
                r_ready, al_done, xp_done, bs_done, mv_done = (sem(c3, n) for n in ("r_ready", "al_done", "xp_done", "bs_done", "mv_done"))
                ln_var, ln_root, x1_done = sem(c3, "ln_var"), sem(c3, "ln_root"), sem(c3, "x1_done")
                tr_done, xt2_done, y_ready, y_done, y2_done, skip_done = (sem(c3, n) for n in ("tr_done", "xt2_done", "y_ready", "y_done", "y2_done", "skip_done"))
                y_out = [sem(c3, f"y_out{i}") for i in range(2)]
                sk_out = [sem(c3, f"sk_out{i}") for i in range(2)]
                skrow = sb(c3, "skrow", [P, 2, OW])
                xres_t = [sb(c3, f"xres_t{i}", [P, D]) for i in range(2)]
                cp_done = sem(c3, "cp_done")
                pidx_ok, ch = sem(c3, "pidx_ok"), sem(c3, "ch")
                block = c3.enter_context(nc.Block())

                @block.sync
                def _(sp):
                    sp.wait_ge(rz, 4)
                    sp.dma_start(r_raw[0:S, 0, 0:S], t["L0_gnn_Wl2_s"][0:S, :]).then_inc(r_in, 16)
                    sp.dma_start(r_raw[0:S, 0, S:S + 1], t["L0_gnn_Wa"][0:S, :]).then_inc(r_in, 16)
                    sp.dma_start(r_raw[S:P, 3, 0:V], t["L0_gnn_Wl2_v"][0:S, :]).then_inc(r_in, 16)
                    for c in range(3):
                        q = slice(V * c, V * c + V)
                        sp.dma_start(r_raw[q, 1, 0:S], t["L0_gnn_Wl2_s"][S:96, :]).then_inc(r_in, 16)
                        sp.dma_start(r_raw[q, 1, S:S + 1], t["L0_gnn_Wa"][S:96, :]).then_inc(r_in, 16)
                        sp.dma_start(r_raw[q, 2, V * c:V * c + V], t["L0_gnn_Wl2_v"][S:96, :]).then_inc(r_in, 16)
                        sp.dma_start(wn_v[q, 0, V * c:V * c + V], t["L1_gnn_W_nl1"]).then_inc(r_in, 16)
                        sp.dma_start(wn_v[q, 1, V * c:V * c + V], t["L1_gnn_W_skip1"]).then_inc(r_in, 16)
                    sp.dma_start(wn_s[:, 0:S], t["L1_gnn_W_nl0"]).then_inc(r_in, 16)
                    sp.dma_start(wn_s[:, S:160], t["L1_gnn_W_skip0"]).then_inc(r_in, 16)
                    n_r_in = 3 + 15 + 2

                    def table(u, j, r):
                        sp.wait_ge(y_done, u + 1)
                        sp.wait_ge(y2_done, u + 1)
                        sp.dma_start(rows(t["f1"], u), yrow[:, r, :]).then_inc(y_out[r], 16)
                        sp.wait_ge(skip_done, u + 1)
                        sp.dma_start(rows(t["tabs"][0], u), skrow[:, r, :]).then_inc(sk_out[r], 16)
                    steps(sp, NT, table, 2, 2)
                    sp.wait_ge(y_out[0], 16 * (-(-NT // 2)))
                    sp.wait_ge(y_out[1], 16 * (NT // 2))
                    sp.wait_ge(sk_out[0], 16 * (-(-NT // 2)))
                    sp.wait_ge(sk_out[1], 16 * (NT // 2))
                    assert n_r_in == 20

                @block.gpsimd
                def _(pool):
                    pool.memset(r_raw[:, :, :], 0.0).then_inc(rz, 1)
                    pool.memset(wn_v[:, :, :], 0.0).then_inc(rz, 1)
                    pool.memset(r_s[:, :, :], 0.0).then_inc(rz, 1)
                    pool.memset(r_v[:, :, :], 0.0).then_inc(rz, 1)
                    pool.iota(pidx[:, :], pattern=[[0, 1]], base=N, channel_multiplier=1,
                              allow_small_or_imprecise_dtypes=True).then_inc(pidx_ok, 1)

                inv = 3072.0 ** -0.5

                @block.scalar
                def _(act):
                    act.wait_ge(r_in, 16 * 20)
                    act.activation(r_s[0:S, 0, :], r_raw[0:S, 0, 0:65], ACT.Copy, scale=inv).then_inc(r_ok, 1)
                    for c in range(3):
                        q = slice(V * c, V * c + V)
                        act.activation(r_s[q, 1 + c, :], r_raw[q, 1, 0:65], ACT.Copy, scale=inv * 3.0 ** -0.5).then_inc(r_ok, 1)
                        act.activation(r_v[S:P, 1 + c, V * c:V * c + V], r_raw[S:P, 3, 0:V], ACT.Copy, scale=inv).then_inc(r_ok, 1)
                    act.activation(r_v[0:96, 0, :], r_raw[0:96, 2, :], ACT.Copy, scale=inv).then_inc(r_ok, 1)

                    def stage(u, j, r):
                        since(act, r_ready, u - 1)
                        act.activation(st_a[:, r, :, :], acc_a[:, :, bass.ds(u * P, P)], ACT.Copy).then_inc(st_act, 1)
                    steps(act, NT, stage, 2, 2)
                    act.wait_ge(ln_var, 1)
                    act.activation(ntmp[:, 0, :], ntmp[:, 1, :], ACT.Sqrt).then_inc(ln_root, 1)

                    def evacuate(u, j, r):
                        act.wait_ge(tr_done, u + 1)
                        since(act, y_ready, u - 1)
                        act.activation(xt2_s[:, r, :], ps_x[r][0:S, 0, :], ACT.Copy)
                        act.activation(xt2_v[:, r, :], ps_x[r][0:96, 1, :], ACT.Copy).then_inc(xt2_done, 1)
                        act.wait_ge(y_ready, u + 1)
                        since(act, y_out[r], 16 * j)
                        act.activation(yrow[:, r, 0:D], ps_y[r][:, 0:D], ACT.Copy).then_inc(y_done, 1)
                        act.activation(yrow[:, r, D:GW], ps_y[r][:, S:S + 2 * V], ACT.Copy).then_inc(y2_done, 1)
                    steps(act, NT, evacuate, 2, 2)

                @block.tensor
                def _(pe):
                    pe.wait_ge(r_ok, 8)

                    def update(u, j, r):
                        pe.wait_ge(st_act, u + 1)
                        pe.wait_ge(st_dve, u + 1)
                        since(pe, xp_done, u - 1)
                        to_s, to_v = ps_r[r][:, 0:65], ps_r[r][:, 65:161]
                        pe.matmul(to_s, st_a[:, r, 0, :], r_s[:, 0, :], start=True, stop=False)
                        for c in range(3):
                            pe.matmul(to_s, st_c[:, r, c, :], r_s[0:96, 1 + c, :], start=False, stop=c == 2)
                        pe.matmul(to_v, st_b[:, r, :], r_v[0:96, 0, :], start=True, stop=False)
                        for c in range(3):
                            last = pe.matmul(to_v, st_a[:, r, 1 + c, :], r_v[:, 1 + c, :], start=False, stop=c == 2)
                        last.then_inc(r_ready, 1)
                    steps(pe, NT, update, 2, 2)

                    def project(s, j, r):
                        if runs(s, NT):
                            pe.wait_ge(x1_done, s + 1)
                            settled(pe, xt2_done, s - 1, passed)
                            row = xres_t[r]
                            pe.transpose(ps_x[r][0:S, 0, :], row[:, 0:S], ident[:, :])
                            pe.transpose(ps_x[r][0:96, 1, :], row[:, S:D], ident[:, :]).then_inc(tr_done, 1)
                        u, _, ur = lagged(s, j, r, 1, 2)
                        if runs(u, NT):
                            pe.wait_ge(xt2_done, u + 1)
                            since(pe, y2_done, u - 1)
                            since(pe, skip_done, u - 1)
                            pe.matmul(ps_y[ur][:, 0:S], xt2_s[:, ur, :], wn_s[:, 0:S], start=True, stop=True)
                            pe.matmul(ps_y[ur][:, D:D + 96], xt2_s[:, ur, :], wn_s[:, S:160], start=True, stop=True)
                            pe.matmul(ps_y[ur][:, S:D], xt2_v[:, ur, :], wn_v[:, 0, :], start=True, stop=True)
                            pe.matmul(ps_y[ur][:, D + 96:D + OW], xt2_v[:, ur, :], wn_v[:, 1, :], start=True,
                                      stop=True).then_inc(y_ready, 1)
                    split_steps(pe, NT, 1, project)

                @block.vector
                def _(dve):
                    done = [0]

                    def link(ins):
                        done[0] += 1
                        ins.then_inc(ch, 1)
                        dve.wait_ge(ch, done[0])

                    def update(s, j, r):
                        if runs(s, NT):
                            settled(dve, r_ready, s - 1, passed)
                            dve.tensor_copy(st_b[:, r, :], acc_b[:, 0, bass.ds(s * P, P)])
                            dve.tensor_copy(st_c[:, r, :, :], acc_c[:, :, bass.ds(s * P, P)]).then_inc(st_dve, 1)
                        u, _, ur = lagged(s, j, r, 1, 2)
                        if runs(u, NT):
                            dve.wait_ge(r_ready, u + 1)
                            dve.tensor_tensor(alpha[:, ur, :], ps_r[ur][:, S:S + 1], a2_col[:, bass.ds(u, 1)],
                                              ALU.mult).then_inc(al_done, 1)
                            dve.wait_ge(al_done, u + 1)
                            here = xres[:, bass.ds(u, 1), :].squeeze(1)
                            dve.scalar_tensor_tensor(here[:, 0:S], ps_r[ur][:, 0:S], alpha[:, ur, :], here[:, 0:S],
                                                     ALU.mult, ALU.add)
                            dve.scalar_tensor_tensor(here[:, S:D], ps_r[ur][:, 65:161], alpha[:, ur, :], here[:, S:D],
                                                     ALU.mult, ALU.add).then_inc(xp_done, 1)
                            since(dve, mv_done, u - 1)
                            settled(dve, xp_done, u + 1, passed)
                            dve.bn_stats(bst[:, ur, :], here).then_inc(bs_done, 1)
                            since(dve, mv_done, u)
                            settled(dve, bs_done, u + 1, passed)
                            dve.bn_aggr(agg[:, :], bst[:, ur, :]).then_inc(ag_done, 1)
                            settled(dve, ag_done, u + 1, passed)
                            dve.tensor_copy(mv[:, bass.ds(u, 1), :].squeeze(1), agg[:, :]).then_inc(mv_done, 1)
                    split_steps(dve, NT, 1, update)

                    dve.wait_ge(mv_done, NT)
                    layer_norm_scale(dve, link, mv, ntmp, rstd, ln_var, ln_root)

                    def normalise(s, j, r):
                        if runs(s, NT):
                            since(dve, tr_done, s - 1)
                            dve.tensor_scalar(xres_t[r][:, :], xres[:, bass.ds(s, 1), :].squeeze(1),
                                              mv[:, bass.ds(s, 1), 0:1].squeeze(1), rstd[:, bass.ds(s, 1)],
                                              ALU.subtract, ALU.mult).then_inc(x1_done, 1)
                            settled(dve, x1_done, s + 1, passed)
                            dve.tensor_copy(xres[:, bass.ds(s, 1), :].squeeze(1), xres_t[r][:, :]).then_inc(cp_done, 1)
                        u, uj, ur = lagged(s, j, r, 1, 2)
                        if runs(u, NT):
                            dve.wait_ge(y2_done, u + 1)
                            settled(dve, sk_out[ur], 16 * uj, passed)
                            dve.tensor_copy(skrow[:, ur, :], ps_y[ur][:, D:D + OW]).then_inc(skip_done, 1)
                    split_steps(dve, NT, 1, normalise)

                    dve.wait_ge(pidx_ok, 1)
                    link(dve.tensor_scalar(cnt[:, :], cnt[:, :], 1.0, None, ALU.min))
                    link(dve.tensor_scalar(colf[:, :], src_f[:, :], -1.0, pidx[:, :], ALU.mult, ALU.add))
                    link(dve.tensor_tensor(colf[:, :], colf[:, :], cnt[:, :], ALU.mult))
                    link(dve.tensor_tensor(scat_i[:, :], colf[:, :], src_f[:, :], ALU.add))

        with ExitStack() as c4:
            wf1 = sb(c4, "wf1", [P, P])
            wf2 = sb(c4, "wf2", [P, 224])
            ro_raw = sb(c4, "ro_raw", [P, 3, 96])
            ro_s = sb(c4, "ro_s", [P, 96])
            ro_v = sb(c4, "ro_v", [P, 2, 96])
            ea64 = sb(c4, "ea64", [P, 2, 256])
            hid = sb(c4, "hid", [P, 2, 256])
            src_bc = sb(c4, "src_bc4", [P, 4, 2, P])
            xg = sb(c4, "xg", [P, 4, 2, GW])
            mm = sb(c4, "mm", [P, 3, 2, 3, V])
            qq = sb(c4, "qq", [P, 2, 2, V])
            xx = sb(c4, "xx", [P, 2, 3, V])
            feat = sb(c4, "feat", [P, 2, 2, 3, P])
            featt = sb(c4, "featt", [P, 2, 2, 3, P])
            same = sb(c4, "same", [P, 4, 2, P])
            ash = sb(c4, "ash", [P, 2, 3, V])
            msg = sb(c4, "msg", [P, 2, 2, OW])
            summed = sb(c4, "summed", [P, 2, 2, OW])
            gidx = sb(c4, "gidx4", [P, 2, 8], I32)
            sidx = sb(c4, "sidx", [P, 2, 8], I32)
            gidx_done4, sidx_done = sem(c4, "gidx_done4"), sem(c4, "sidx_done")
            ps_h = pb(c4, "ps_h", [P, 512])[:, 0:256]
            ps_w = [pb(c4, f"ps_x4{i}", [P, 2, 256]) for i in range(2)]
            ps_t = pb(c4, "ps_t", [P, 2, 512])
            ps_o = pb(c4, "ps_o", [P, 2, 256])
            ps_d = pb(c4, "ps_d", [P, 2, 256])
            wz, w_in4, ro_ok, fz = sem(c4, "wz"), sem(c4, "w_in4"), sem(c4, "ro_ok"), sem(c4, "fz")
            ea_in = [sem(c4, f"ea_in{i}") for i in range(2)]
            sb_in = [sem(c4, f"sb_in{i}") for i in range(4)]
            g_in = [sem(c4, f"g_in{i}") for i in range(4)]
            tab_in = [sem(c4, f"tab_in{i}") for i in range(NTAB)]
            hid_ready, relu_done, w4_ready = (sem(c4, n) for n in ("hid_ready", "relu_done", "w4_ready"))
            m_done, xx_done, feat_done, same_done = (sem(c4, n) for n in ("m_done", "xx_done", "feat_done", "same_done"))
            t_ready, t_done, o_ready, os_done, ash_done, ov_done = (sem(c4, n) for n in ("t_ready", "t_done", "o_ready", "os_done", "ash_done", "ov_done"))
            d_ready, sum_done = sem(c4, "d_ready"), sem(c4, "sum_done")
            block = c4.enter_context(nc.Block())
            LAST = 3

            @block.sync
            def _(sp):
                sp.wait_ge(wz, 2)
                for h in range(2):
                    q = slice(S * h, S * h + S)
                    sp.dma_start(wf1[q, q], t["L1_gnn_W_fc1"]).then_inc(w_in4, 16)
                    sp.dma_start(wf2[q, :], t["L1_gnn_W_fc2"]).then_inc(w_in4, 16)
                wos, wov = t["L1_gnn_W_out_s"], t["L1_gnn_W_out_v"]
                sp.dma_start(ro_raw[0:96, 0, :], wos).then_inc(w_in4, 16)
                sp.dma_start(ro_raw[0:S, 1, 0:V], wov[0:S, :]).then_inc(w_in4, 16)
                sp.dma_start(ro_raw[S:P, 1, V:2 * V], wov[S:P, :]).then_inc(w_in4, 16)
                sp.dma_start(ro_raw[0:S, 2, 0:V], wov[S:P, :]).then_inc(w_in4, 16)
                sp.dma_start(ro_raw[S:P, 2, V:2 * V], wov[S:P, :]).then_inc(w_in4, 16)

                def load_ea64(g, slot):
                    since(sp, hid_ready, g - 1)
                    sp.dma_start(ea64[:, slot, :], t["ea64"][bass.ds(g, 1), :, :].squeeze(0)).then_inc(ea_in[slot], 16)

                def load(u, j, r):
                    if r % 2 == 0:
                        g = j * 2 + r // 2 + 1
                        if runs(g, NGRP):
                            load_ea64(g, (r // 2 + 1) % 2)
                    since(sp, same_done, u - 3)
                    sp.dma_start(src_bc[:, r, :, :].rearrange("p k e -> p (k e)"),
                                 t["src_pairs_f"][bass.ds(u, 1), :].to_broadcast([P, 2 * P])).then_inc(sb_in[r], 16)
                load_ea64(0, 0)
                split_steps(sp, NPAIR, 0, load, 4, short=4)

            @block.gpsimd
            def _(pool):
                pool.memset(wf1[:, :], 0.0).then_inc(wz, 1)
                pool.memset(ro_raw[:, :, :], 0.0).then_inc(wz, 1)

                def step(s, j, r):
                    if runs(s, NPAIR):
                        since(pool, feat_done, s - 3)
                        if r % 4 == 0:
                            pool.tensor_copy(gidx[:, r // 4, :], dst_i[:, bass.ds(s * 2, 8)]).then_inc(gidx_done4, 1)
                            since(pool, gidx_done4, j * 2 + r // 4 + 1)
                        if not isinstance(s, int):
                            pool.sem_inc(passed, 1)
                        for k in range(2):
                            at = r % 4 * 2 + k
                            pool.indirect_dma_start(
                                out=xg[:, r % 4, k, :], out_offset=None, in_=t["f1"],
                                in_offset=bass.IndirectOffsetOnAxis(ap=gidx[:, r // 4, at:at + 1], axis=0),
                            ).then_inc(g_in[r % 4], 16)
                    u, uj, ur = lagged(s, j, r, 6, 8)
                    if runs(u, NPAIR):
                        into = [(ur * 2 + k) % NTAB for k in range(2)]
                        for k in range(2):
                            since(pool, tab_in[into[k]], 16 * (uj * 4 + (ur * 2 + k) // NTAB))
                        if ur % 4 == 0:
                            pool.tensor_copy(sidx[:, ur // 4, :], scat_i[:, bass.ds(u * 2, 8)]).then_inc(sidx_done, 1)
                            since(pool, sidx_done, uj * 2 + ur // 4 + 1)
                        settled(pool, sum_done, u + 1, passed)
                        for k in range(2):
                            at = ur % 4 * 2 + k
                            pool.indirect_dma_start(
                                out=t["tabs"][into[k]],
                                out_offset=bass.IndirectOffsetOnAxis(ap=sidx[:, ur // 4, at:at + 1], axis=0),
                                in_=summed[:, ur % 2, k, :], in_offset=None, compute_op=ALU.add,
                                bounds_check=TROWS - 1,
                            ).then_inc(tab_in[into[k]], 16)
                split_steps(pool, NPAIR, 6, step, 8)
                for tab in range(NTAB):
                    pool.wait_ge(tab_in[tab], 16 * (TILES // NTAB))

            @block.scalar
            def _(act):
                act.wait_ge(w_in4, 16 * 9)
                inv = 1.0 / 32.0
                act.activation(ro_s[0:S, :], ro_raw[0:S, 0, :], ACT.Copy, scale=inv).then_inc(ro_ok, 1)
                act.activation(ro_s[S:P, :], ro_raw[S:P, 0, :], ACT.Copy, scale=inv * 3.0 ** -0.5).then_inc(ro_ok, 1)
                for k in range(2):
                    for q in range(4):
                        cross = q == 3 or (k == 1 and q == 1)
                        act.activation(ro_v[V * q:V * q + V, k, :], ro_raw[V * q:V * q + V, 1 + k, :], ACT.Copy,
                                       scale=inv * (2.0 ** -0.5 if cross else 1.0)).then_inc(ro_ok, 1)

                def step(s, j, r):
                    if r % 2 == 0:
                        g = j * 2 + r // 2 + 1
                        if runs(g, NGRP):
                            relu(g, (r // 2 + 1) % 2)
                    u, uj, ur = lagged(s, j, r, 1, 4)
                    if runs(u, NPAIR):
                        act.wait_ge(t_ready, u + 1)
                        since(act, o_ready, u - 1)
                        act.activation(featt[:, ur % 2, :, :, :].rearrange("p k a b -> p k (a b)"), ps_t[:, :, 0:384],
                                       ACT.Copy).then_inc(t_done, 1)
                    u, uj, ur = lagged(s, j, r, 2, 4)
                    if runs(u, NPAIR):
                        act.wait_ge(o_ready, u + 1)
                        since(act, d_ready, u - 1)
                        act.activation(msg[:, ur % 2, :, 0:96], ps_o[:, :, 0:96], ACT.Copy).then_inc(os_done, 1)
                    u, uj, ur = lagged(s, j, r, LAST, 4)
                    if runs(u, NPAIR):
                        act.wait_ge(d_ready, u + 1)
                        for k in range(2):
                            t2 = ((ur - 2) * 2 + k) % NTAB
                            turn = uj * 2 + (ur - 2) * 2 // NTAB + 1
                            since(act, tab_in[t2], 16 * turn)
                        act.activation(summed[:, ur % 2, :, :], ps_d[:, :, 0:OW], ACT.Copy).then_inc(sum_done, 1)

                def relu(g, slot):
                    act.wait_ge(hid_ready, g + 1)
                    since(act, w4_ready, 2 * (g - 1))
                    act.activation(hid[:, slot, :], ps_h[:, :], ACT.Relu).then_inc(relu_done, 1)
                relu(0, 0)
                split_steps(act, NPAIR, LAST, step, 4, short=2)

            @block.tensor
            def _(pe):
                pe.wait_ge(w_in4, 16 * 9)
                pe.wait_ge(ro_ok, 10)

                def hidden(g, slot, turn):
                    pe.wait_ge(ea_in[slot], 16 * (turn + 1))
                    since(pe, relu_done, g)
                    pe.matmul(ps_h[:, :], wf1[:, :], ea64[:, slot, :], start=True, stop=True).then_inc(hid_ready, 1)

                def step(s, j, r):
                    if r % 2 == 0:
                        g = j * 2 + r // 2 + 1
                        if runs(g, NGRP):
                            hidden(g, (r // 2 + 1) % 2, j + (r // 2 + 1) // 2)
                    if runs(s, NPAIR):
                        pe.wait_ge(relu_done, j * 2 + r // 2 + 1)
                        since(pe, feat_done, s - 1)
                        h = slice(S * (r % 2), S * (r % 2) + S)
                        for k in range(2):
                            last = pe.matmul(ps_w[r % 2][:, k, 0:224], hid[h, r // 2, P * k:P * k + P], wf2[h, :],
                                             start=True, stop=True)
                        last.then_inc(w4_ready, 1)
                    u, _, ur = lagged(s, j, r, 1, 4)
                    if runs(u, NPAIR):
                        pe.wait_ge(feat_done, u + 1)
                        since(pe, t_done, u)
                        for k in range(2):
                            for c in range(3):
                                last = pe.transpose(ps_t[:, k, P * c:P * c + P], feat[:, ur % 2, k, c, :], ident[:, :])
                        last.then_inc(t_ready, 1)
                    u, _, ur = lagged(s, j, r, 2, 4)
                    if runs(u, NPAIR):
                        pe.wait_ge(t_done, u + 1)
                        since(pe, ov_done, u)
                        since(pe, os_done, u)
                        for k in range(2):
                            pe.matmul(ps_o[:, k, 0:96], featt[:, ur % 2, k, 0, :], ro_s[:, :], start=True, stop=True)
                            for c in range(2):
                                last = pe.matmul(ps_o[:, k, 96 + 64 * c:192 + 64 * c], featt[:, ur % 2, k, 1 + c, :],
                                                 ro_v[:, c, :], start=True, stop=True)
                        last.then_inc(o_ready, 1)
                    u, _, ur = lagged(s, j, r, LAST, 4)
                    if runs(u, NPAIR):
                        pe.wait_ge(os_done, u + 1)
                        pe.wait_ge(ov_done, u + 1)
                        pe.wait_ge(same_done, u + 1)
                        since(pe, sum_done, u)
                        for k in range(2):
                            last = pe.matmul(ps_d[:, k, 0:OW], same[:, ur, k, :], msg[:, ur % 2, k, :],
                                             start=True, stop=True)
                        last.then_inc(d_ready, 1)
                hidden(0, 0, 0)
                split_steps(pe, NPAIR, LAST, step, 4, short=2)

            @block.vector
            def _(dve):
                dve.memset(feat[:, :, :, 0, 96:P], 0.0).then_inc(fz, 1)

                def products(u, j, r):
                    x = xg[:, r, :, :]
                    dve.wait_ge(g_in[r], 32 * (j + 1))

                    def shv(c):
                        return sh[:, bass.ds(u * 2, 2), c:c + 3].unsqueeze(3).to_broadcast([P, 2, 3, V])

                    def xv(c):
                        return x[:, :, S + V * c:S + V * c + 3 * V].rearrange("p k (c u) -> p k c u", c=3)
                    since(dve, xx_done, 3 * u)
                    dve.tensor_tensor(mm[:, 0, :, :, :], xv(0), shv(0), ALU.mult)
                    dve.tensor_tensor(mm[:, 1, :, :, :], xv(1), shv(2), ALU.mult)
                    dve.tensor_tensor(mm[:, 2, :, :, :], xv(2), shv(1), ALU.mult).then_inc(m_done, 1)
                    dve.wait_ge(m_done, u + 1)
                    since(dve, feat_done, u)
                    dve.tensor_tensor(qq[:, 0, :, :], mm[:, 0, :, 0, :], mm[:, 0, :, 1, :], ALU.add).then_inc(xx_done, 1)
                    dve.tensor_tensor(xx[:, :, :, :], mm[:, 1, :, :, :], mm[:, 2, :, :, :], ALU.subtract).then_inc(xx_done, 1)
                    dve.wait_ge(xx_done, 3 * u + 1)
                    dve.tensor_tensor(qq[:, 1, :, :], qq[:, 0, :, :], mm[:, 0, :, 2, :], ALU.add).then_inc(xx_done, 1)
                    dve.wait_ge(w4_ready, u + 1)
                    since(dve, t_ready, u - 1)
                    p = r % 2
                    w = ps_w[p]
                    dve.tensor_tensor(feat[:, p, :, 0:2, 0:S], w[:, :, 0:2 * S].rearrange("p k (a s) -> p k a s", a=2),
                                      x[:, :, 0:S].unsqueeze(2).to_broadcast([P, 2, 2, S]), ALU.mult)
                    flat = feat[:, p, :, :, :].rearrange("p k a b -> p k (a b)")
                    v_part = flat[:, :, P + S:3 * P].rearrange("p k (c x u) -> p k c x u", c=3, x=2)
                    dve.tensor_tensor(v_part[:, :, :, 0, :], w[:, :, 128:160].unsqueeze(2).to_broadcast([P, 2, 3, V]),
                                      xv(0), ALU.mult)
                    dve.wait_ge(xx_done, 3 * u + 3)
                    dve.tensor_tensor(flat[:, :, S:96], w[:, :, 160:192], qq[:, 1, :, :], ALU.mult)
                    dve.tensor_tensor(v_part[:, :, :, 1, :], w[:, :, 192:224].unsqueeze(2).to_broadcast([P, 2, 3, V]),
                                      xx[:, :, :, :], ALU.mult).then_inc(feat_done, 1)

                def equal(u, j, r):
                    dve.wait_ge(sb_in[r], 16 * (j + 1))
                    since(dve, d_ready, u - 3)
                    dve.tensor_tensor(same[:, r, :, :], src_bc[:, r, :, :],
                                      src_f[:, bass.ds(u * 2, 2)].unsqueeze(2).to_broadcast([P, 2, P]),
                                      ALU.is_equal).then_inc(same_done, 1)

                def finish(u, r):
                    dve.wait_ge(os_done, u + 1)
                    since(dve, ov_done, u)
                    dve.tensor_tensor(ash[:, :, :, :], ps_o[:, :, 96:128].unsqueeze(2).to_broadcast([P, 2, 3, V]),
                                      sh[:, bass.ds(u * 2, 2), 0:3].unsqueeze(3).to_broadcast([P, 2, 3, V]),
                                      ALU.mult).then_inc(ash_done, 1)
                    dve.wait_ge(ash_done, u + 1)
                    since(dve, d_ready, u - 1)
                    dve.tensor_tensor(msg[:, r % 2, :, 96:OW], ps_o[:, :, 128:224],
                                      ash[:, :, :, :].rearrange("p k c u -> p k (c u)"), ALU.add).then_inc(ov_done, 1)

                def step(s, j, r):
                    if runs(s, NPAIR):
                        products(s, j, r)
                        equal(s, j, r)
                    u, _, ur = lagged(s, j, r, 2, 4)
                    if runs(u, NPAIR):
                        finish(u, ur)
                split_steps(dve, NPAIR, 2, step, 4)

        with ExitStack() as c5:
            tabs = sb(c5, "tabs", [P, 2, NTAB, OW])
            tsum = sb(c5, "tsum", [P, 2, 2, OW])
            so = sb(c5, "so", [P, 2, OW])
            sg = sb(c5, "sg", [P, 2, 96])
            upd = sb(c5, "upd", [P, 2, D])
            agg5, ag5 = sb(c5, "agg5", [P, 2]), sem(c5, "ag5")
            bst5 = sb(c5, "bst5", [P, 2, 6])
            orow = sb(c5, "orow", [P, 2, D])
            tin = [sem(c5, f"tin{i}") for i in range(2)]
            o_out = [sem(c5, f"o_out{i}") for i in range(2)]
            half_done, so_done, sg_done, upd_done, res_done, bs5, mv5 = (
                sem(c5, n) for n in ("half_done", "so_done", "sg_done", "upd_done", "res_done", "bs5", "mv5"))
            lv5, lr5, on_done, ch5 = sem(c5, "lv5"), sem(c5, "lr5"), sem(c5, "on_done"), sem(c5, "ch5")
            block = c5.enter_context(nc.Block())

            @block.sync
            def _(sp):
                def load(u, j, r):
                    since(sp, half_done, u - 1)
                    for k in range(NTAB):
                        sp.dma_start(tabs[:, r, k, :], rows(t["tabs"][k], u)).then_inc(tin[r], 16)
                steps(sp, NT, load, 2, 2)

                def store(u, j, r):
                    sp.wait_ge(on_done, u + 1)
                    sp.dma_start(rows(out, u), orow[:, r, :]).then_inc(o_out[r], 16)
                steps(sp, NT, store, 2, 2)
                sp.wait_ge(o_out[0], 16 * (-(-NT // 2)))
                sp.wait_ge(o_out[1], 16 * (NT // 2))

            @block.scalar
            def _(act):
                def gates(u, j, r):
                    act.wait_ge(so_done, u + 1)
                    since(act, upd_done, u - 1)
                    act.activation(sg[:, r, :], so[:, r, 0:96], ACT.Sigmoid).then_inc(sg_done, 1)
                steps(act, NT, gates, 2, 2)
                act.wait_ge(lv5, 1)
                act.activation(ntmp[:, 0, :], ntmp[:, 1, :], ACT.Sqrt).then_inc(lr5, 1)

            @block.vector
            def _(dve):
                done = [0]

                def link(ins):
                    done[0] += 1
                    ins.then_inc(ch5, 1)
                    dve.wait_ge(ch5, done[0])

                def update(s, j, r):
                    if runs(s, NT):
                        dve.wait_ge(tin[r], 16 * NTAB * (j + 1))
                        dve.tensor_tensor(tsum[:, r, :, :], tabs[:, r, 0:2, :], tabs[:, r, 2:4, :], ALU.add).then_inc(half_done, 1)
                        dve.wait_ge(half_done, s + 1)
                        dve.tensor_tensor(so[:, r, :], tsum[:, r, 0, :], tsum[:, r, 1, :], ALU.add).then_inc(so_done, 1)
                    u, _, ur = lagged(s, j, r, 1, 2)
                    if runs(u, NT):
                        dve.wait_ge(sg_done, u + 1)
                        since(dve, res_done, u - 1)
                        dve.tensor_tensor(upd[:, ur, 0:S], so[:, ur, 0:S], sg[:, ur, 0:S], ALU.mult)
                        dve.tensor_tensor(upd[:, ur, S:D].rearrange("p (c u) -> p c u", c=3),
                                          so[:, ur, 96:OW].rearrange("p (c u) -> p c u", c=3),
                                          sg[:, ur, S:96].unsqueeze(1).to_broadcast([P, 3, V]), ALU.mult).then_inc(upd_done, 1)
                        dve.wait_ge(upd_done, u + 1)
                        here = xres[:, bass.ds(u, 1), :].squeeze(1)
                        dve.tensor_tensor(here, here, upd[:, ur, :], ALU.add).then_inc(res_done, 1)
                        since(dve, mv5, u - 1)
                        settled(dve, res_done, u + 1, passed)
                        dve.bn_stats(bst5[:, ur, :], here).then_inc(bs5, 1)
                        since(dve, mv5, u)
                        settled(dve, bs5, u + 1, passed)
                        dve.bn_aggr(agg5[:, :], bst5[:, ur, :]).then_inc(ag5, 1)
                        settled(dve, ag5, u + 1, passed)
                        dve.tensor_copy(mv[:, bass.ds(u, 1), :].squeeze(1), agg5[:, :]).then_inc(mv5, 1)
                split_steps(dve, NT, 1, update)
                dve.wait_ge(mv5, NT)
                layer_norm_scale(dve, link, mv, ntmp, rstd, lv5, lr5)

                def normalise(u, j, r):
                    since(dve, o_out[r], 16 * j)
                    here = xres[:, bass.ds(u, 1), :].squeeze(1)
                    mean, scale = mv[:, bass.ds(u, 1), 0:1].squeeze(1), rstd[:, bass.ds(u, 1)]
                    dve.tensor_scalar(orow[:, r, 0:S], here[:, 0:S], mean, scale, ALU.subtract, ALU.mult)
                    dve.tensor_scalar(orow[:, r, S:D].rearrange("p (u c) -> p c u", c=3),
                                      here[:, S:D].rearrange("p (c u) -> p c u", c=3), mean, scale,
                                      ALU.subtract, ALU.mult).then_inc(on_done, 1)
                steps(dve, NT, normalise, 2, 2)


def layer_norm_scale(dve, link, mv, ntmp, rstd, var_ready, root_ready):
    dve.tensor_scalar(ntmp[:, 1, :], mv[:, :, 1], EPS, None, ALU.add).then_inc(var_ready, 1)
    dve.wait_ge(root_ready, 1)
    link(dve.reciprocal(rstd[:, :], ntmp[:, 0, :]))
    link(dve.tensor_tensor(ntmp[:, 0, :], rstd[:, :], rstd[:, :], ALU.mult))
    link(dve.tensor_tensor(ntmp[:, 0, :], ntmp[:, 0, :], ntmp[:, 1, :], ALU.mult))
    link(dve.tensor_scalar(ntmp[:, 0, :], ntmp[:, 0, :], -0.5, 1.5, ALU.mult, ALU.add))
    link(dve.tensor_tensor(rstd[:, :], rstd[:, :], ntmp[:, 0, :], ALU.mult))


def split_steps(eng, units, lag, body, unroll=2, short=0):
    first = -(-(lag + 2) // unroll) * unroll
    last = max(first, (units - short) // unroll * unroll)
    for s in range(first):
        body(s, s // unroll, s % unroll)
    if last > first:
        with eng.Fori(first // unroll, last // unroll) as j:
            for r in range(unroll):
                body(j * unroll + r, j, r)
    for s in range(last, units + lag):
        body(s, s // unroll, s % unroll)


def kernel(**inputs):
    import numpy as np
    import concourse.bacc as bacc
    from concourse.bass_utils import run_bass_kernel_spmd

    nc = bacc.Bacc("TRN2", target_bir_lowering=False, num_devices=1)
    arr = {k: np.asarray(v) for k, v in inputs.items()}

    def pad(a, n, value):
        full = np.full((n,) + a.shape[1:], value, a.dtype)
        full[:a.shape[0]] = a
        return full

    def cols(a):
        return np.ascontiguousarray(a.reshape(-1, P, *a.shape[1:]).swapaxes(0, 1))

    x = pad(arr["x"], NP, 0)
    x = np.concatenate([x[:, :S], x[:, S:].reshape(NP, V, 3).transpose(0, 2, 1).reshape(NP, 3 * V)], 1)
    src, dst = pad(arr["src"], EP, N), pad(arr["dst"], EP, N)
    ea8, ea64 = pad(arr["edge_attr_8"], EP, 0), pad(arr["edge_attr_64"], EP, 0)
    data = {
        "x_rows": cols(x), "xt": np.ascontiguousarray(x.reshape(NT, P, D).transpose(0, 2, 1)),
        "a_col": cols(pad(arr["node_vec1"][:, 0], NP, 0)),
        "src_col": cols(src), "dst_col": cols(dst), "src_rows": src.reshape(NGRP, GE),
        "dst_first": np.ascontiguousarray(dst[::GE]).reshape(1, NGRP),
        "ea3": cols(pad(arr["edge_attr_3"], EP, 1)), "ea4": cols(pad(arr["edge_attr_4"], EP, 0)),
        "ea8": np.ascontiguousarray(ea8.reshape(NGRP, 2, 256, 8).transpose(1, 3, 0, 2)).reshape(16, NGRP * 256),
        "ea64": np.ascontiguousarray(ea64.reshape(NGRP, 2, 256, 64).transpose(0, 1, 3, 2)).reshape(NGRP, P, 256),
    }
    for name in arr:
        if name.startswith(("L0_gnn_W", "L1_gnn_W")):
            data[name] = arr[name]
    arrays, t = {}, {}
    for name, a in data.items():
        arrays["in_" + name] = np.ascontiguousarray(a)
        t[name] = nc.dram_tensor("in_" + name, a.shape, mybir.dt.from_np(a.dtype), kind="ExternalInput").ap()

    def scratch(name, shape):
        return nc.dram_tensor(name, shape, F32, kind="Internal").ap()
    t["f0"] = scratch("f0", (NP, D))
    t["f1"] = scratch("f1", (NP, GW))
    t["src_rows_f"] = scratch("src_rows_f", (NGRP, GE))
    t["src_pairs_f"] = t["src_rows_f"].rearrange("g (k e) -> (g k) e", k=2)
    t["tabs"] = [scratch(f"tab{i}", (TROWS, OW)) for i in range(NTAB)]
    out = nc.dram_tensor("out", (NP, D), F32, kind="ExternalOutput").ap()
    gnn_kernel(nc, t, out)
    r = run_bass_kernel_spmd(nc, [arrays], core_ids=[0])
    return r.results[0]["out"][:N]
```

```python
from contextlib import ExitStack

import concourse.bass as bass
from concourse import mybir
from concourse.alu_op_type import AluOpType as ALU

F32 = mybir.dt.float32
I32 = mybir.dt.int32
ACT = mybir.ActivationFunctionType
AX = mybir.AxisListType

N, E = 3125, 100000
FT = 5
P = 128
NT = -(-N // P)
NP = NT * P
NC = NT // FT
assert NT % FT == 0
S, V = 64, 32
D = S + 3 * V
G = 4
NGRP = -(-E // (P * G))
NGRP += NGRP % 2
TILES = NGRP * G
EP = TILES * P
GE = G * P
WIN = 24
SWEEP = -(-(N + 1) // WIN)
ACCW = max(NP, N + WIN, SWEEP * WIN)
NTAB = 4
ZROWS = -(-(N + P) // (NGRP // 2))
TROWS = NGRP // 2 * ZROWS
OW = 96 + 96
GW = S + 5 * V
NPAIR = TILES // 2
EPS = 1e-5


def since(eng, sem, count):
    if not isinstance(count, int) or count > 0:
        eng.wait_ge(sem, count)


def settled(eng, sem, count, passed):
    since(eng, sem, count)
    if not isinstance(count, int):
        eng.sem_inc(passed, 1)


def steps(eng, total, body, first, unroll):
    first = min(-(-first // unroll) * unroll, total)
    last = max(first, total // unroll * unroll)
    for s in range(first):
        body(s, s // unroll, s % unroll)
    if last > first:
        with eng.Fori(first // unroll, last // unroll) as j:
            for r in range(unroll):
                body(j * unroll + r, j, r)
    for s in range(last, total):
        body(s, s // unroll, s % unroll)


def lagged(s, j, r, lag, unroll):
    return s - lag, j + (r - lag) // unroll, (r - lag) % unroll


def runs(u, total):
    return not isinstance(u, int) or 0 <= u < total


def gnn_kernel(nc, t, out):
    top = ExitStack()
    with top:
        def sb(ctx, name, shape, dt=F32):
            return ctx.enter_context(nc.sbuf_tensor(name, shape, dt))

        def pb(ctx, name, shape, dt=F32):
            return ctx.enter_context(nc.psum_tensor(name, shape, dt))

        def sem(ctx, name):
            return ctx.enter_context(nc.semaphore(name))

        src_f = sb(top, "src_f", [P, TILES])
        rel_f = sb(top, "rel_f", [P, TILES])
        dst_f = sb(top, "dst_f", [P, TILES])
        src_i = sb(top, "src_i", [P, TILES], I32)
        dst_i = sb(top, "dst_i", [P, TILES], I32)
        scat_i = sb(top, "scat_i", [P, TILES], I32)
        base_i = sb(top, "base_i", [P, NGRP], I32)
        sh = sb(top, "sh", [P, TILES, 5])
        cnt = sb(top, "cnt", [P, TILES])
        lower = sb(top, "lower", [P, P])
        ident = sb(top, "ident", [P, P])
        xres = sb(top, "xres", [P, NT, D])
        a_col = sb(top, "a_col", [P, NT])
        a2_col = sb(top, "a2_col", [P, NT])
        win_ok = sb(top, "win_ok", [P, 1], I32)
        mv = sb(top, "mv", [P, NT, 2])
        rstd = sb(top, "rstd", [P, NT])
        ntmp = sb(top, "ntmp", [P, 2, NT])

        passed = sem(top, "passed")

        def rows(dram, tile):
            return dram[bass.ds(tile * P, P), :]

        def tile_rows(dram, m):
            return dram[m * FT * P:(m + 1) * FT * P, :].rearrange("(a p) f -> p a f", p=P)

        cacc = ExitStack()
        acc_a = sb(cacc, "acc_a", [P, 4, ACCW])
        acc_b = sb(cacc, "acc_b", [96, 1, ACCW])
        with ExitStack() as c1:
            ea3 = sb(c1, "ea3", [P, TILES, 3])
            sq = sh[:, :, 0:3]
            nrm = sb(c1, "nrm", [P, 4, TILES])
            base_f = sb(c1, "base_f", [P, NGRP])
            rows_i = sb(c1, "rows_i", [NGRP // 2, 2, GE], I32)
            rows_f = sb(c1, "rows_f", [NGRP // 2, 2, GE])
            ones = sb(c1, "ones", [P, P])
            ext = sb(c1, "ext", [P, 4])
            w_s = sb(c1, "w_s", [S, 2, S])
            w_v = sb(c1, "w_v", [96, 2, 96])
            w_s2 = sb(c1, "w_s2", [S, 2, S])
            w_v2 = sb(c1, "w_v2", [96, 2, 96])
            xt_s = sb(c1, "xt_s", [S, NP])
            xt_v = sb(c1, "xt_v", [96, NP])
            frow = sb(c1, "frow", [P, 2, FT, D])
            ps_n = [pb(c1, f"ps_n{i}", [P, 512]) for i in range(2)]
            ps_e = pb(c1, "ps_e", [P, 512])
            idx_in, attr_in, rows_in = sem(c1, "idx_in"), sem(c1, "attr_in"), sem(c1, "rows_in")
            wn_zero, wn_in, wn_scaled = sem(c1, "wn_zero"), sem(c1, "wn_in"), sem(c1, "wn_scaled")
            x_in, a_in = sem(c1, "x_in"), sem(c1, "a_in")
            xt_in = sem(c1, "xt_in")
            f_out = [sem(c1, f"f_out{i}") for i in range(2)]
            consts, rowsf_done, rows_out = sem(c1, "consts"), sem(c1, "rowsf_done"), sem(c1, "rows_out")
            conv, ext_done, cnt_ps = sem(c1, "conv"), sem(c1, "ext_done"), sem(c1, "cnt_ps")
            sq_done, root_done = sem(c1, "sq_done"), sem(c1, "root_done")
            n_ready, f_ready, res_ready = sem(c1, "n_ready"), sem(c1, "f_ready"), sem(c1, "res_ready")
            zeroed, dv = sem(c1, "zeroed"), sem(c1, "dv")
            block = c1.enter_context(nc.Block())

            @block.sync
            def _(sp):
                sp.dma_start(src_i[:, :], t["src_col"]).then_inc(idx_in, 16)
                sp.dma_start(dst_i[:, :], t["dst_col"]).then_inc(idx_in, 16)
                sp.dma_start(base_i[:, :], t["dst_first"][0:1, :].to_broadcast([P, NGRP])).then_inc(idx_in, 16)
                sp.dma_start(rows_i[:, :, :], t["src_rows"].rearrange("(p a) e -> p a e", a=2)).then_inc(rows_in, 16)
                sp.dma_start(ea3[:, :, :], t["ea3"]).then_inc(attr_in, 16)
                sp.wait_ge(wn_zero, 1)
                sp.dma_start(w_s[:, 0, :], t["L0_gnn_Wl1_0"]).then_inc(wn_in, 16)
                sp.dma_start(w_s[:, 1, :], t["L0_gnn_Wsc0"]).then_inc(wn_in, 16)
                for c in range(3):
                    for k, name in enumerate(("L0_gnn_Wl1_1", "L0_gnn_Wsc1")):
                        sp.dma_start(w_v[V * c:V * c + V, k, V * c:V * c + V], t[name]).then_inc(wn_in, 16)
                sp.dma_start(xres[:, :, :], t["x_rows"]).then_inc(x_in, 16)
                sp.wait_ge(rowsf_done, 1)
                sp.dma_start(t["src_rows_f"].rearrange("(p a) e -> p a e", a=2), rows_f[:, :, :]).then_inc(rows_out, 16)
                sp.wait_ge(rows_out, 16)

            @block.gpsimd
            def _(pool):
                pool.memset(w_v[:, :, :], 0.0).then_inc(wn_zero, 1)
                pool.memset(ones[:, :], 1.0).then_inc(consts, 1)
                pool.memset(lower[:, :], 1.0).then_inc(consts, 1)
                pool.memset(ident[:, :], 0.0).then_inc(consts, 1)
                pool.wait_ge(consts, 3)
                pool.affine_select(out=lower[:, :], in_=lower[:, :], compare_op=ALU.is_ge, fill=0.0,
                                   base=-1, pattern=[[-1, P]], channel_multiplier=1).then_inc(consts, 1)
                pool.affine_select(out=ident[:, :], in_=ident[:, :], compare_op=ALU.not_equal, fill=1.0,
                                   base=0, pattern=[[-1, P]], channel_multiplier=1).then_inc(consts, 1)
                pool.memset(acc_a[:, :, :], 0.0).then_inc(zeroed, 1)
                pool.memset(acc_b[:, :, :], 0.0).then_inc(zeroed, 1)
                pool.wait_ge(consts, 5)
                pool.wait_ge(zeroed, 2)

            @block.tensor
            def _(pe):
                pe.wait_ge(wn_scaled, 2)

                pe.wait_ge(xt_in, 32)
                for u in range(NT):
                    r = u % 2
                    since(pe, f_ready, u - 1)
                    since(pe, res_ready, u - 1)
                    parts = ps_n[r][:, 0:320].rearrange("p (k f) -> p k f", k=2)
                    here = slice(u * P, u * P + P)
                    pe.matmul(parts[:, :, 0:S], xt_s[:, here], w_s2[:, :, :], start=True, stop=True)
                    pe.matmul(parts[:, :, S:D], xt_v[:, here], w_v2[:, :, :], start=True, stop=True).then_inc(n_ready, 1)
                pe.wait_ge(ext_done, 1)
                pe.wait_ge(consts, 1)
                pe.matmul(ps_e[:, 0:1], ones[:, :], ext[:, 2:3], start=True, stop=True).then_inc(cnt_ps, 1)

            @block.scalar
            def _(act):
                act.dma_start(xt_s[:, :], t["xt"][0:S, :]).then_inc(xt_in, 16)
                act.dma_start(xt_v[:, :], t["xt"][S:D, :]).then_inc(xt_in, 16)
                act.dma_start(a_col[:, :], t["a_col"]).then_inc(a_in, 16)
                act.wait_ge(wn_in, 16 * 8)
                act.activation(w_s2[:, :, :], w_s[:, :, :], ACT.Copy, scale=1.0 / 8.0).then_inc(wn_scaled, 1)
                act.activation(w_v2[:, :, :], w_v[:, :, :], ACT.Copy, scale=float(V) ** -0.5).then_inc(wn_scaled, 1)
                act.wait_ge(sq_done, 1)
                act.activation(nrm[:, 1, :], nrm[:, 0, :], ACT.Sqrt).then_inc(root_done, 1)
                act.wait_ge(a_in, 16)
                for u in range(NT):
                    m, at = divmod(u, FT)
                    act.wait_ge(n_ready, u + 1)
                    if at == 0 and m >= 2:
                        act.wait_ge(f_out[m % 2], 16 * (m // 2))
                    act.activation(frow[:, m % 2, at, :], ps_n[u % 2][:, 0:D], ACT.Copy,
                                   scale=a_col[:, u:u + 1]).then_inc(f_ready, 1)
                    if at == FT - 1:
                        act.wait_ge(f_ready, u + 1)
                        act.dma_start(tile_rows(t["f0"], m),
                                      frow[:, m % 2, :, :]).then_inc(f_out[m % 2], 16)
                act.wait_ge(f_out[0], 16 * (-(-NT // FT // 2)))
                act.wait_ge(f_out[1], 16 * (NT // FT // 2))

            @block.vector
            def _(dve):
                done = [0]

                def link(ins):
                    done[0] += 1
                    ins.then_inc(dv, 1)
                    dve.wait_ge(dv, done[0])

                dve.wait_ge(attr_in, 16)
                link(dve.tensor_tensor(sq, ea3[:, :, :], ea3[:, :, :], ALU.mult))
                dve.tensor_reduce(nrm[:, 0, :], sq, AX.X, ALU.add).then_inc(sq_done, 1)
                dve.wait_ge(idx_in, 48)
                dve.tensor_copy(src_f[:, :], src_i[:, :]).then_inc(conv, 1)
                dve.tensor_copy(dst_f[:, :], dst_i[:, :]).then_inc(conv, 1)
                dve.tensor_copy(base_f[:, :], base_i[:, :]).then_inc(conv, 1)
                dve.wait_ge(rows_in, 16)
                dve.tensor_copy(rows_f[:, :, :], rows_i[:, :, :]).then_inc(rowsf_done, 1)
                dve.wait_ge(conv, 3)
                link(dve.tensor_tensor(rel_f[:, :].rearrange("p (g k) -> p g k", k=G),
                                       dst_f[:, :].rearrange("p (g k) -> p g k", k=G),
                                       base_f[:, :].unsqueeze(2).to_broadcast([P, NGRP, G]), ALU.subtract))
                dve.wait_ge(a_in, 16)
                dve.tensor_tensor(a2_col[:, :], a_col[:, :], a_col[:, :], ALU.mult)
                link(dve.tensor_reduce(ext[:, 0:1], rel_f[:, :], AX.X, ALU.max))
                link(dve.tensor_reduce(ext[:, 1:2], rel_f[:, :], AX.X, ALU.min))
                link(dve.tensor_scalar(ext[:, 0:1], ext[:, 0:1], float(WIN), None, ALU.is_ge))
                link(dve.tensor_scalar(ext[:, 1:2], ext[:, 1:2], 0.0, None, ALU.is_lt))
                dve.tensor_tensor(ext[:, 2:3], ext[:, 0:1], ext[:, 1:2], ALU.add).then_inc(ext_done, 1)

                dve.wait_ge(x_in, 16)

                for u in range(NT):
                    dve.wait_ge(f_ready, u + 1)
                    dve.scalar_tensor_tensor(xres[:, u, :], ps_n[u % 2][:, D:2 * D], a_col[:, u:u + 1], xres[:, u, :],
                                             ALU.mult, ALU.add).then_inc(res_ready, 1)

                dve.wait_ge(root_done, 1)
                link(dve.reciprocal(nrm[:, 2, :], nrm[:, 1, :]))
                link(dve.tensor_tensor(nrm[:, 3, :], nrm[:, 2, :], nrm[:, 2, :], ALU.mult))
                link(dve.tensor_tensor(nrm[:, 3, :], nrm[:, 3, :], nrm[:, 0, :], ALU.mult))
                link(dve.tensor_scalar(nrm[:, 3, :], nrm[:, 3, :], -0.5 * 3.0 ** 0.5, 1.5 * 3.0 ** 0.5, ALU.mult, ALU.add))
                link(dve.tensor_tensor(nrm[:, 2, :], nrm[:, 2, :], nrm[:, 3, :], ALU.mult))
                link(dve.tensor_tensor(sh[:, :, 0:3], ea3[:, :, :],
                                       nrm[:, 2, :].unsqueeze(2).to_broadcast([P, TILES, 3]), ALU.mult))
                link(dve.tensor_copy(sh[:, :, 3:5], sh[:, :, 0:2]))
                dve.wait_ge(cnt_ps, 1)
                link(dve.tensor_scalar(win_ok[:, :], ps_e[:, 0:1], 0.0, None, ALU.is_equal))

        with cacc:
            acc_c = sb(cacc, "acc_c", [96, 3, ACCW])
            with ExitStack() as c2:
                w1 = sb(c2, "w1", [16, P])
                w2 = sb(c2, "w2", [P, P])
                w3 = sb(c2, "w3", [P, 192])
                w3raw = sb(c2, "w3raw", [P, 192])
                ea8 = sb(c2, "ea8", [16, 2, 256])
                y = sb(c2, "y", [P, TILES, 4])
                h1 = sb(c2, "h1", [P, 2, 256])
                h2 = sb(c2, "h2", [P, 2, 256])
                gat = sb(c2, "gat", [P, 2, G, D])
                src_bc = sb(c2, "src_bc", [P, 2, G, P])
                eq_junk = sb(c2, "eq_junk", [P, G, P])
                pos = sb(c2, "pos", [P, WIN])
                ohot = sb(c2, "ohot", [P, G, WIN])
                sel = sb(c2, "sel", [P, 2, G, 4, WIN])
                ta = sb(c2, "ta", [P, 2, G, 2, S])
                tb = sb(c2, "tb", [P, 2, G, 3, V])
                tc = sb(c2, "tc", [P, 2, G, 3, V])
                dcur = sb(c2, "dcur", [P, G])
                ps_h1, ps_h2 = (pb(c2, n, [P, 512])[:, 0:256] for n in ("ps_h1", "ps_h2"))
                ps_w = [pb(c2, f"ps_w{i}", [P, G, 256]) for i in range(2)]
                ps_g = [pb(c2, f"ps_g{i}", [P, 512]) for i in range(2)]
                w_in, w_zero, w3_ok, y_in = sem(c2, "w_in"), sem(c2, "w_zero"), sem(c2, "w3_ok"), sem(c2, "y_in")
                acc_ok, pos_ok = sem(c2, "acc_ok"), sem(c2, "pos_ok")
                zrow = sb(c2, "zrow", [ZROWS, OW])
                z_ok, tab_out = sem(c2, "z_ok"), sem(c2, "tab_out")
                ea8_in = [sem(c2, f"ea8_in{i}") for i in range(2)]
                srcb_in = [sem(c2, f"srcb_in{i}") for i in range(2)]
                gath = [sem(c2, f"gath{i}") for i in range(2)]
                h1_ready, g1_done, h2_ready, g2_done = (sem(c2, n) for n in ("h1_ready", "g1_done", "h2_ready", "g2_done"))
                w_ready, cnt_done, hot_done, sel_ready = (sem(c2, n) for n in ("w_ready", "cnt_done", "hot_done", "sel_ready"))
                prod_done, agg_done, acc_done, cur_done = (sem(c2, n) for n in ("prod_done", "agg_done", "acc_done", "cur_done"))
                gidx = sb(c2, "gidx", [P, 2, 2 * G], I32)
                gidx_done = sem(c2, "gidx_done")
                block = c2.enter_context(nc.Block())

                @block.sync
                def _(sp):
                    sp.wait_ge(w_zero, 2)
                    for h in range(2):
                        sp.dma_start(w1[8 * h:8 * h + 8, S * h:S * h + S], t["L0_gnn_Wfc1"]).then_inc(w_in, 16)
                        sp.dma_start(w2[S * h:S * h + S, S * h:S * h + S], t["L0_gnn_Wfc2"]).then_inc(w_in, 16)
                        sp.dma_start(w3raw[S * h:S * h + S, :], t["L0_gnn_Wfc3"]).then_inc(w_in, 16)
                    sp.dma_start(y[:, :, :], t["ea4"]).then_inc(y_in, 16)

                    def load_ea8(u, r):
                        since(sp, h1_ready, u - 1)
                        sp.dma_start(ea8[:, r, :], t["ea8"][:, bass.ds(u * 256, 256)]).then_inc(ea8_in[r], 16)

                    def load(u, j, r):
                        if r == 0:
                            for tab in t["tabs"]:
                                sp.dma_start(tab[bass.ds(j * ZROWS, ZROWS), :], zrow[:, :]).then_inc(tab_out, 16)
                        if not isinstance(u, int) or u + 1 < NGRP:
                            load_ea8(u + 1, (r + 1) % 2)
                        since(sp, cnt_done, G * (u - 1))
                        sp.dma_start(src_bc[:, r, :, :].rearrange("p k e -> p (k e)"),
                                     t["src_rows_f"][bass.ds(u, 1), :].to_broadcast([P, GE])).then_inc(srcb_in[r], 16)
                    load_ea8(0, 0)
                    sp.wait_ge(z_ok, 1)
                    split_steps(sp, NGRP, 0, load, 2, short=1)
                    sp.wait_ge(tab_out, 16 * NTAB * (NGRP // 2))

                @block.gpsimd
                def _(pool):
                    pool.memset(w1[:, :], 0.0).then_inc(w_zero, 1)
                    pool.memset(w2[:, :], 0.0).then_inc(w_zero, 1)
                    pool.memset(zrow[:, :], 0.0).then_inc(z_ok, 1)
                    pool.iota(pos[:, :], pattern=[[1, WIN]], base=0, channel_multiplier=0,
                              allow_small_or_imprecise_dtypes=True).then_inc(pos_ok, 1)

                    def gather(u, j, r):
                        if r % 2 == 0:
                            since(pool, prod_done, u - 2)
                            pool.tensor_copy(gidx[:, r // 2, :], src_i[:, bass.ds(u * G, 2 * G)]).then_inc(gidx_done, 1)
                            since(pool, gidx_done, j * 2 + r // 2 + 1)
                        since(pool, prod_done, u - 1)
                        if not isinstance(u, int):
                            pool.sem_inc(passed, 1)
                        for k in range(G):
                            at = r % 2 * G + k
                            pool.indirect_dma_start(
                                out=gat[:, r % 2, k, :], out_offset=None, in_=t["f0"],
                                in_offset=bass.IndirectOffsetOnAxis(ap=gidx[:, r // 2, at:at + 1], axis=0),
                            ).then_inc(gath[r % 2], 16)
                    steps(pool, NGRP, gather, 4, 4)

                @block.scalar
                def _(act):
                    act.activation(acc_c[:, :, :], acc_a[0:96, 0:3, :], ACT.Copy).then_inc(acc_ok, 1)
                    act.wait_ge(w_in, 16 * 6)
                    act.activation(w3[:, :], w3raw[:, :], ACT.Copy, scale=1.0 / 8.0).then_inc(w3_ok, 1)

                    def gelus(u, j, r):
                        act.wait_ge(h1_ready, u + 1)
                        since(act, h2_ready, u - 1)
                        act.activation(h1[:, r, :], ps_h1[:, :], ACT.Gelu_apprx_tanh,
                                       scale=8.0 ** -0.5).then_inc(g1_done, 1)
                        act.wait_ge(h2_ready, u + 1)
                        since(act, w_ready, u - 1)
                        act.activation(h2[:, r, :], ps_h2[:, :], ACT.Gelu_apprx_tanh,
                                       scale=1.0 / 8.0).then_inc(g2_done, 1)
                    steps(act, NGRP, gelus, 4, 2)

                def window_sums(pe, r, ready):
                    for n, (lhs, hi) in enumerate(((ta, P), (tb, 96), (tc, 96))):
                        for k in range(G):
                            last = pe.matmul(ps_g[r][0:hi, n * 4 * WIN:(n + 1) * 4 * WIN],
                                             lhs[:, r, k, :, :].rearrange("p a b -> p (a b)"),
                                             sel[:, r, k, :, :].rearrange("p a b -> p (a b)"),
                                             start=k == 0, stop=k == G - 1)
                    last.then_inc(ready, 1)

                @block.tensor
                def _(pe):
                    pe.wait_ge(w_in, 16 * 6)
                    pe.wait_ge(w3_ok, 1)

                    def layer1(u, r, j):
                        pe.wait_ge(ea8_in[r], 16 * (j + 1))
                        since(pe, g1_done, u)
                        pe.matmul(ps_h1[:, :], w1[:, :], ea8[:, r, :], start=True, stop=True).then_inc(h1_ready, 1)

                    def layer2(u, r):
                        pe.wait_ge(g1_done, u + 1)
                        since(pe, g2_done, u)
                        pe.matmul(ps_h2[:, :], w2[:, :], h1[:, r, :], start=True, stop=True).then_inc(h2_ready, 1)

                    def layer3(u, r):
                        pe.wait_ge(g2_done, u + 1)
                        since(pe, prod_done, u - 1)
                        for k in range(G):
                            h = S * (k // 2)
                            last = pe.matmul(ps_w[r][:, k, 0:192], h2[h:h + S, r, P * (k % 2):P * (k % 2) + P],
                                             w3[h:h + S, :], start=True, stop=True)
                        last.then_inc(w_ready, 1)

                    def fast():
                        def step(s, j, r):
                            if runs(s, NGRP):
                                layer1(s, r, j)
                            u, _, ur = lagged(s, j, r, 3, 2)
                            if runs(u, NGRP):
                                pe.wait_ge(sel_ready, u + 1)
                                pe.wait_ge(prod_done, u + 1)
                                since(pe, acc_done, u - 1)
                                window_sums(pe, ur, agg_done)
                            if runs(s, NGRP):
                                layer2(s, r)
                            u, _, ur = lagged(s, j, r, 1, 2)
                            if runs(u, NGRP):
                                layer3(u, ur)
                        split_steps(pe, NGRP, 3, step)

                    def general():
                        def step(u, j, r):
                            layer1(u, r, j)
                            layer2(u, r)
                            layer3(u, r)
                            settled(pe, prod_done, u + 1, passed)
                            with pe.Fori(0, SWEEP) as n:
                                pe.wait_ge(sel_ready, u * SWEEP + n + 1)
                                window_sums(pe, r, agg_done)
                                settled(pe, acc_done, u * SWEEP + n + 1, passed)
                        steps(pe, NGRP, step, 4, 2)

                    ok = pe.value_load(win_ok[0:1, 0:1], min_val=0, max_val=1)
                    with pe.If(ok):
                        fast()
                    with pe.Else():
                        general()

                @block.vector
                def _(dve):
                    dve.wait_ge(acc_ok, 1)
                    dve.wait_ge(pos_ok, 1)
                    dve.wait_ge(y_in, 16)

                    def earlier(u, j, r):
                        dve.wait_ge(srcb_in[r], 16 * (j + 1))
                        since(dve, cnt_done, u * G)
                        for k in range(G):
                            col = bass.ds(u * G + k, 1)
                            dve.scalar_tensor_tensor(eq_junk[:, k, :], src_bc[:, r, k, :], src_f[:, col], lower[:, :],
                                                     ALU.is_equal, ALU.mult,
                                                     accum_out=cnt[:, col]).then_inc(cnt_done, 1)

                    def select(u, r, rel, hot_count):
                        since(dve, sel_ready, hot_count - 1)
                        dve.tensor_tensor(ohot[:, :, :], pos[:, :].unsqueeze(1).to_broadcast([P, G, WIN]),
                                          rel.unsqueeze(2).to_broadcast([P, G, WIN]), ALU.is_equal).then_inc(hot_done, 1)
                        dve.wait_ge(hot_done, hot_count)
                        dve.tensor_tensor(sel[:, r, :, :, :], ohot[:, :, :].unsqueeze(2).to_broadcast([P, G, 4, WIN]),
                                          y[:, bass.ds(u * G, G), :].unsqueeze(3).to_broadcast([P, G, 4, WIN]),
                                          ALU.mult).then_inc(sel_ready, 1)

                    def products(u, j, r):
                        dve.wait_ge(w_ready, u + 1)
                        dve.wait_ge(gath[r], 16 * G * (j + 1))
                        dve.tensor_tensor(ta[:, r, :, :, :], ps_w[r][:, :, 0:2 * S].rearrange("p k (a s) -> p k a s", a=2),
                                          gat[:, r, :, 0:S].unsqueeze(2).to_broadcast([P, G, 2, S]), ALU.mult)
                        gv = gat[:, r, :, S:D].rearrange("p k (c u) -> p k c u", c=3)
                        for dst, at in ((tb, 2 * S), (tc, 2 * S + V)):
                            last = dve.tensor_tensor(dst[:, r, :, :, :],
                                                     ps_w[r][:, :, at:at + V].unsqueeze(2).to_broadcast([P, G, 3, V]),
                                                     gv, ALU.mult)
                        last.then_inc(prod_done, 1)

                    def add_window(r, base):
                        for acc, hi, at, n in ((acc_a, P, 0, 4), (acc_b, 96, 4 * WIN, 1), (acc_c, 96, 9 * WIN, 3)):
                            part = acc[:, :, bass.ds(base, WIN)]
                            last = dve.tensor_tensor(part, part,
                                                     ps_g[r][0:hi, at:at + n * WIN].rearrange("p (c w) -> p c w", c=n),
                                                     ALU.add)
                        last.then_inc(acc_done, 1)

                    def fast():
                        def step(s, j, r):
                            if runs(s, NGRP):
                                since(dve, agg_done, s - 1)
                                select(s, r, rel_f[:, bass.ds(s * G, G)], s + 1)
                                products(s, j, r)
                            u, _, ur = lagged(s, j, r, 2, 2)
                            if runs(s, NGRP):
                                earlier(s, j, r)
                            if runs(u, NGRP):
                                base = dve.value_load(base_i[0:1, bass.ds(u, 1)], min_val=0, max_val=N)
                                dve.wait_ge(agg_done, u + 1)
                                since(dve, acc_done, u)
                                add_window(ur, base)
                        split_steps(dve, NGRP, 2, step)

                    def general():
                        def step(u, j, r):
                            earlier(u, j, r)
                            since(dve, acc_done, u * SWEEP)
                            products(u, j, r)
                            settled(dve, cur_done, u * (SWEEP + 1), passed)
                            dve.tensor_copy(dcur[:, :], dst_f[:, bass.ds(u * G, G)]).then_inc(cur_done, 1)
                            with dve.Fori(0, SWEEP) as n:
                                dve.wait_ge(cur_done, u * (SWEEP + 1) + n + 1)
                                select(u, r, dcur[:, :], u * SWEEP + n + 1)
                                dve.wait_ge(agg_done, u * SWEEP + n + 1)
                                add_window(r, n * WIN)
                                dve.tensor_scalar(dcur[:, :], dcur[:, :], float(-WIN), None, ALU.add).then_inc(cur_done, 1)
                        steps(dve, NGRP, step, 4, 2)

                    ok = dve.value_load(win_ok[0:1, 0:1], min_val=0, max_val=1)
                    with dve.If(ok):
                        fast()
                    with dve.Else():
                        general()

            with ExitStack() as c3:
                r_raw = sb(c3, "r_raw", [P, 5, 96])
                r_s = sb(c3, "r_s", [P, 4, 65])
                r_v = sb(c3, "r_v", [P, 4, 96])
                st_a = sb(c3, "st_a", [P, 2, 4, P])
                st_b = sb(c3, "st_b", [96, 2, P])
                st_c = sb(c3, "st_c", [96, 2, 3, P])
                agg, ag_done = sb(c3, "agg", [P, 2]), sem(c3, "ag_done")
                alpha = sb(c3, "alpha", [P, 2, 1])
                bst = sb(c3, "bst", [P, 2, 6])
                colf = sb(c3, "colf", [P, TILES])
                pidx = sb(c3, "pidx", [P, 1])
                wn_s = sb(c3, "wn_s", [S, 160])
                wn_v = sb(c3, "wn_v", [96, 2, 96])
                xt2_s = sb(c3, "xt2_s", [S, 2, P])
                xt2_v = sb(c3, "xt2_v", [96, 2, P])
                yrow = sb(c3, "yrow", [P, 2, GW])
                ps_r = [pb(c3, f"ps_r{i}", [P, 512]) for i in range(2)]
                ps_x = [pb(c3, f"ps_x{i}", [P, 4, P]) for i in range(2)]
                ps_y = [pb(c3, f"ps_y{i}", [P, 512]) for i in range(2)]
                rz, r_in, r_ok = sem(c3, "rz"), sem(c3, "r_in"), sem(c3, "r_ok")
                st_act, st_dve = sem(c3, "st_act"), sem(c3, "st_dve")
                r_ready, al_done, xp_done, bs_done, mv_done = (sem(c3, n) for n in ("r_ready", "al_done", "xp_done", "bs_done", "mv_done"))
                ln_var, ln_root, x1_done = sem(c3, "ln_var"), sem(c3, "ln_root"), sem(c3, "x1_done")
                tr_done, xt2_done, y_ready, y_done, y2_done, skip_done = (sem(c3, n) for n in ("tr_done", "xt2_done", "y_ready", "y_done", "y2_done", "skip_done"))
                y_out = [sem(c3, f"y_out{i}") for i in range(2)]
                sk_out = [sem(c3, f"sk_out{i}") for i in range(2)]
                skrow = sb(c3, "skrow", [P, 2, OW])
                xres_t = [sb(c3, f"xres_t{i}", [P, D]) for i in range(2)]
                cp_done = sem(c3, "cp_done")
                pidx_ok, ch = sem(c3, "pidx_ok"), sem(c3, "ch")
                block = c3.enter_context(nc.Block())

                @block.sync
                def _(sp):
                    sp.wait_ge(rz, 4)
                    sp.dma_start(r_raw[0:S, 0, 0:S], t["L0_gnn_Wl2_s"][0:S, :]).then_inc(r_in, 16)
                    sp.dma_start(r_raw[0:S, 0, S:S + 1], t["L0_gnn_Wa"][0:S, :]).then_inc(r_in, 16)
                    sp.dma_start(r_raw[S:P, 3, 0:V], t["L0_gnn_Wl2_v"][0:S, :]).then_inc(r_in, 16)
                    for c in range(3):
                        q = slice(V * c, V * c + V)
                        sp.dma_start(r_raw[q, 1, 0:S], t["L0_gnn_Wl2_s"][S:96, :]).then_inc(r_in, 16)
                        sp.dma_start(r_raw[q, 1, S:S + 1], t["L0_gnn_Wa"][S:96, :]).then_inc(r_in, 16)
                        sp.dma_start(r_raw[q, 2, V * c:V * c + V], t["L0_gnn_Wl2_v"][S:96, :]).then_inc(r_in, 16)
                        sp.dma_start(wn_v[q, 0, V * c:V * c + V], t["L1_gnn_W_nl1"]).then_inc(r_in, 16)
                        sp.dma_start(wn_v[q, 1, V * c:V * c + V], t["L1_gnn_W_skip1"]).then_inc(r_in, 16)
                    sp.dma_start(wn_s[:, 0:S], t["L1_gnn_W_nl0"]).then_inc(r_in, 16)
                    sp.dma_start(wn_s[:, S:160], t["L1_gnn_W_skip0"]).then_inc(r_in, 16)
                    n_r_in = 3 + 15 + 2

                    def table(u, j, r):
                        sp.wait_ge(y_done, u + 1)
                        sp.wait_ge(y2_done, u + 1)
                        sp.dma_start(rows(t["f1"], u), yrow[:, r, :]).then_inc(y_out[r], 16)
                        sp.wait_ge(skip_done, u + 1)
                        sp.dma_start(rows(t["tabs"][0], u), skrow[:, r, :]).then_inc(sk_out[r], 16)
                    steps(sp, NT, table, 2, 2)
                    sp.wait_ge(y_out[0], 16 * (-(-NT // 2)))
                    sp.wait_ge(y_out[1], 16 * (NT // 2))
                    sp.wait_ge(sk_out[0], 16 * (-(-NT // 2)))
                    sp.wait_ge(sk_out[1], 16 * (NT // 2))
                    assert n_r_in == 20

                @block.gpsimd
                def _(pool):
                    pool.memset(r_raw[:, :, :], 0.0).then_inc(rz, 1)
                    pool.memset(wn_v[:, :, :], 0.0).then_inc(rz, 1)
                    pool.memset(r_s[:, :, :], 0.0).then_inc(rz, 1)
                    pool.memset(r_v[:, :, :], 0.0).then_inc(rz, 1)
                    pool.iota(pidx[:, :], pattern=[[0, 1]], base=N, channel_multiplier=1,
                              allow_small_or_imprecise_dtypes=True).then_inc(pidx_ok, 1)

                inv = 3072.0 ** -0.5

                @block.scalar
                def _(act):
                    act.wait_ge(r_in, 16 * 20)
                    act.activation(r_s[0:S, 0, :], r_raw[0:S, 0, 0:65], ACT.Copy, scale=inv).then_inc(r_ok, 1)
                    for c in range(3):
                        q = slice(V * c, V * c + V)
                        act.activation(r_s[q, 1 + c, :], r_raw[q, 1, 0:65], ACT.Copy, scale=inv * 3.0 ** -0.5).then_inc(r_ok, 1)
                        act.activation(r_v[S:P, 1 + c, V * c:V * c + V], r_raw[S:P, 3, 0:V], ACT.Copy, scale=inv).then_inc(r_ok, 1)
                    act.activation(r_v[0:96, 0, :], r_raw[0:96, 2, :], ACT.Copy, scale=inv).then_inc(r_ok, 1)

                    def stage(u, j, r):
                        since(act, r_ready, u - 1)
                        act.activation(st_a[:, r, :, :], acc_a[:, :, bass.ds(u * P, P)], ACT.Copy).then_inc(st_act, 1)
                    steps(act, NT, stage, 2, 2)
                    act.wait_ge(ln_var, 1)
                    act.activation(ntmp[:, 0, :], ntmp[:, 1, :], ACT.Sqrt).then_inc(ln_root, 1)

                    def evacuate(u, j, r):
                        act.wait_ge(tr_done, u + 1)
                        since(act, y_ready, u - 1)
                        act.activation(xt2_s[:, r, :], ps_x[r][0:S, 0, :], ACT.Copy)
                        act.activation(xt2_v[:, r, :], ps_x[r][0:96, 1, :], ACT.Copy).then_inc(xt2_done, 1)
                        act.wait_ge(y_ready, u + 1)
                        since(act, y_out[r], 16 * j)
                        act.activation(yrow[:, r, 0:D], ps_y[r][:, 0:D], ACT.Copy).then_inc(y_done, 1)
                        act.activation(yrow[:, r, D:GW], ps_y[r][:, S:S + 2 * V], ACT.Copy).then_inc(y2_done, 1)
                    steps(act, NT, evacuate, 2, 2)

                @block.tensor
                def _(pe):
                    pe.wait_ge(r_ok, 8)

                    def update(u, j, r):
                        pe.wait_ge(st_act, u + 1)
                        pe.wait_ge(st_dve, u + 1)
                        since(pe, xp_done, u - 1)
                        to_s, to_v = ps_r[r][:, 0:65], ps_r[r][:, 65:161]
                        pe.matmul(to_s, st_a[:, r, 0, :], r_s[:, 0, :], start=True, stop=False)
                        for c in range(3):
                            pe.matmul(to_s, st_c[:, r, c, :], r_s[0:96, 1 + c, :], start=False, stop=c == 2)
                        pe.matmul(to_v, st_b[:, r, :], r_v[0:96, 0, :], start=True, stop=False)
                        for c in range(3):
                            last = pe.matmul(to_v, st_a[:, r, 1 + c, :], r_v[:, 1 + c, :], start=False, stop=c == 2)
                        last.then_inc(r_ready, 1)
                    steps(pe, NT, update, 2, 2)

                    def project(s, j, r):
                        if runs(s, NT):
                            pe.wait_ge(x1_done, s + 1)
                            settled(pe, xt2_done, s - 1, passed)
                            row = xres_t[r]
                            pe.transpose(ps_x[r][0:S, 0, :], row[:, 0:S], ident[:, :])
                            pe.transpose(ps_x[r][0:96, 1, :], row[:, S:D], ident[:, :]).then_inc(tr_done, 1)
                        u, _, ur = lagged(s, j, r, 1, 2)
                        if runs(u, NT):
                            pe.wait_ge(xt2_done, u + 1)
                            since(pe, y2_done, u - 1)
                            since(pe, skip_done, u - 1)
                            pe.matmul(ps_y[ur][:, 0:S], xt2_s[:, ur, :], wn_s[:, 0:S], start=True, stop=True)
                            pe.matmul(ps_y[ur][:, D:D + 96], xt2_s[:, ur, :], wn_s[:, S:160], start=True, stop=True)
                            pe.matmul(ps_y[ur][:, S:D], xt2_v[:, ur, :], wn_v[:, 0, :], start=True, stop=True)
                            pe.matmul(ps_y[ur][:, D + 96:D + OW], xt2_v[:, ur, :], wn_v[:, 1, :], start=True,
                                      stop=True).then_inc(y_ready, 1)
                    split_steps(pe, NT, 1, project)

                @block.vector
                def _(dve):
                    done = [0]

                    def link(ins):
                        done[0] += 1
                        ins.then_inc(ch, 1)
                        dve.wait_ge(ch, done[0])

                    def update(s, j, r):
                        if runs(s, NT):
                            settled(dve, r_ready, s - 1, passed)
                            dve.tensor_copy(st_b[:, r, :], acc_b[:, 0, bass.ds(s * P, P)])
                            dve.tensor_copy(st_c[:, r, :, :], acc_c[:, :, bass.ds(s * P, P)]).then_inc(st_dve, 1)
                        u, _, ur = lagged(s, j, r, 1, 2)
                        if runs(u, NT):
                            dve.wait_ge(r_ready, u + 1)
                            dve.tensor_tensor(alpha[:, ur, :], ps_r[ur][:, S:S + 1], a2_col[:, bass.ds(u, 1)],
                                              ALU.mult).then_inc(al_done, 1)
                            dve.wait_ge(al_done, u + 1)
                            here = xres[:, bass.ds(u, 1), :].squeeze(1)
                            dve.scalar_tensor_tensor(here[:, 0:S], ps_r[ur][:, 0:S], alpha[:, ur, :], here[:, 0:S],
                                                     ALU.mult, ALU.add)
                            dve.scalar_tensor_tensor(here[:, S:D], ps_r[ur][:, 65:161], alpha[:, ur, :], here[:, S:D],
                                                     ALU.mult, ALU.add).then_inc(xp_done, 1)
                            since(dve, mv_done, u - 1)
                            settled(dve, xp_done, u + 1, passed)
                            dve.bn_stats(bst[:, ur, :], here).then_inc(bs_done, 1)
                            since(dve, mv_done, u)
                            settled(dve, bs_done, u + 1, passed)
                            dve.bn_aggr(agg[:, :], bst[:, ur, :]).then_inc(ag_done, 1)
                            settled(dve, ag_done, u + 1, passed)
                            dve.tensor_copy(mv[:, bass.ds(u, 1), :].squeeze(1), agg[:, :]).then_inc(mv_done, 1)
                    split_steps(dve, NT, 1, update)

                    dve.wait_ge(mv_done, NT)
                    layer_norm_scale(dve, link, mv, ntmp, rstd, ln_var, ln_root)

                    def normalise(s, j, r):
                        if runs(s, NT):
                            since(dve, tr_done, s - 1)
                            dve.tensor_scalar(xres_t[r][:, :], xres[:, bass.ds(s, 1), :].squeeze(1),
                                              mv[:, bass.ds(s, 1), 0:1].squeeze(1), rstd[:, bass.ds(s, 1)],
                                              ALU.subtract, ALU.mult).then_inc(x1_done, 1)
                            settled(dve, x1_done, s + 1, passed)
                            dve.tensor_copy(xres[:, bass.ds(s, 1), :].squeeze(1), xres_t[r][:, :]).then_inc(cp_done, 1)
                        u, uj, ur = lagged(s, j, r, 1, 2)
                        if runs(u, NT):
                            dve.wait_ge(y2_done, u + 1)
                            settled(dve, sk_out[ur], 16 * uj, passed)
                            dve.tensor_copy(skrow[:, ur, :], ps_y[ur][:, D:D + OW]).then_inc(skip_done, 1)
                    split_steps(dve, NT, 1, normalise)

                    dve.wait_ge(pidx_ok, 1)
                    link(dve.tensor_scalar(cnt[:, :], cnt[:, :], 1.0, None, ALU.min))
                    link(dve.tensor_scalar(colf[:, :], src_f[:, :], -1.0, pidx[:, :], ALU.mult, ALU.add))
                    link(dve.tensor_tensor(colf[:, :], colf[:, :], cnt[:, :], ALU.mult))
                    link(dve.tensor_tensor(scat_i[:, :], colf[:, :], src_f[:, :], ALU.add))

        with ExitStack() as c4:
            wf1 = sb(c4, "wf1", [P, P])
            wf2 = sb(c4, "wf2", [P, 224])
            ro_raw = sb(c4, "ro_raw", [P, 3, 96])
            ro_s = sb(c4, "ro_s", [P, 96])
            ro_v = sb(c4, "ro_v", [P, 2, 96])
            ea64 = sb(c4, "ea64", [P, 2, 256])
            hid = sb(c4, "hid", [P, 2, 256])
            src_bc = sb(c4, "src_bc4", [P, 4, 2, P])
            xg = sb(c4, "xg", [P, 4, 2, GW])
            mm = sb(c4, "mm", [P, 3, 2, 3, V])
            qq = sb(c4, "qq", [P, 2, 2, V])
            xx = sb(c4, "xx", [P, 2, 3, V])
            feat = sb(c4, "feat", [P, 2, 2, 3, P])
            featt = sb(c4, "featt", [P, 2, 2, 3, P])
            same = sb(c4, "same", [P, 4, 2, P])
            ash = sb(c4, "ash", [P, 2, 3, V])
            msg = sb(c4, "msg", [P, 2, 2, OW])
            summed = sb(c4, "summed", [P, 2, 2, OW])
            gidx = sb(c4, "gidx4", [P, 2, 8], I32)
            sidx = sb(c4, "sidx", [P, 2, 8], I32)
            gidx_done4, sidx_done = sem(c4, "gidx_done4"), sem(c4, "sidx_done")
            ps_h = pb(c4, "ps_h", [P, 512])[:, 0:256]
            ps_w = [pb(c4, f"ps_x4{i}", [P, 2, 256]) for i in range(2)]
            ps_t = pb(c4, "ps_t", [P, 2, 512])
            ps_o = pb(c4, "ps_o", [P, 2, 256])
            ps_d = pb(c4, "ps_d", [P, 2, 256])
            wz, w_in4, ro_ok, fz = sem(c4, "wz"), sem(c4, "w_in4"), sem(c4, "ro_ok"), sem(c4, "fz")
            ea_in = [sem(c4, f"ea_in{i}") for i in range(2)]
            sb_in = [sem(c4, f"sb_in{i}") for i in range(4)]
            g_in = [sem(c4, f"g_in{i}") for i in range(4)]
            tab_in = [sem(c4, f"tab_in{i}") for i in range(NTAB)]
            hid_ready, relu_done, w4_ready = (sem(c4, n) for n in ("hid_ready", "relu_done", "w4_ready"))
            m_done, xx_done, feat_done, same_done = (sem(c4, n) for n in ("m_done", "xx_done", "feat_done", "same_done"))
            t_ready, t_done, o_ready, os_done, ash_done, ov_done = (sem(c4, n) for n in ("t_ready", "t_done", "o_ready", "os_done", "ash_done", "ov_done"))
            d_ready, sum_done = sem(c4, "d_ready"), sem(c4, "sum_done")
            block = c4.enter_context(nc.Block())
            LAST = 3

            @block.sync
            def _(sp):
                sp.wait_ge(wz, 2)
                for h in range(2):
                    q = slice(S * h, S * h + S)
                    sp.dma_start(wf1[q, q], t["L1_gnn_W_fc1"]).then_inc(w_in4, 16)
                    sp.dma_start(wf2[q, :], t["L1_gnn_W_fc2"]).then_inc(w_in4, 16)
                wos, wov = t["L1_gnn_W_out_s"], t["L1_gnn_W_out_v"]
                sp.dma_start(ro_raw[0:96, 0, :], wos).then_inc(w_in4, 16)
                sp.dma_start(ro_raw[0:S, 1, 0:V], wov[0:S, :]).then_inc(w_in4, 16)
                sp.dma_start(ro_raw[S:P, 1, V:2 * V], wov[S:P, :]).then_inc(w_in4, 16)
                sp.dma_start(ro_raw[0:S, 2, 0:V], wov[S:P, :]).then_inc(w_in4, 16)
                sp.dma_start(ro_raw[S:P, 2, V:2 * V], wov[S:P, :]).then_inc(w_in4, 16)

                def load_ea64(g, slot):
                    since(sp, hid_ready, g - 1)
                    sp.dma_start(ea64[:, slot, :], t["ea64"][bass.ds(g, 1), :, :].squeeze(0)).then_inc(ea_in[slot], 16)

                def load(u, j, r):
                    if r % 2 == 0:
                        g = j * 2 + r // 2 + 1
                        if runs(g, NGRP):
                            load_ea64(g, (r // 2 + 1) % 2)
                    since(sp, same_done, u - 3)
                    sp.dma_start(src_bc[:, r, :, :].rearrange("p k e -> p (k e)"),
                                 t["src_pairs_f"][bass.ds(u, 1), :].to_broadcast([P, 2 * P])).then_inc(sb_in[r], 16)
                load_ea64(0, 0)
                split_steps(sp, NPAIR, 0, load, 4, short=4)

            @block.gpsimd
            def _(pool):
                pool.memset(wf1[:, :], 0.0).then_inc(wz, 1)
                pool.memset(ro_raw[:, :, :], 0.0).then_inc(wz, 1)

                def step(s, j, r):
                    if runs(s, NPAIR):
                        since(pool, feat_done, s - 3)
                        if r % 4 == 0:
                            pool.tensor_copy(gidx[:, r // 4, :], dst_i[:, bass.ds(s * 2, 8)]).then_inc(gidx_done4, 1)
                            since(pool, gidx_done4, j * 2 + r // 4 + 1)
                        if not isinstance(s, int):
                            pool.sem_inc(passed, 1)
                        for k in range(2):
                            at = r % 4 * 2 + k
                            pool.indirect_dma_start(
                                out=xg[:, r % 4, k, :], out_offset=None, in_=t["f1"],
                                in_offset=bass.IndirectOffsetOnAxis(ap=gidx[:, r // 4, at:at + 1], axis=0),
                            ).then_inc(g_in[r % 4], 16)
                    u, uj, ur = lagged(s, j, r, 6, 8)
                    if runs(u, NPAIR):
                        into = [(ur * 2 + k) % NTAB for k in range(2)]
                        for k in range(2):
                            since(pool, tab_in[into[k]], 16 * (uj * 4 + (ur * 2 + k) // NTAB))
                        if ur % 4 == 0:
                            pool.tensor_copy(sidx[:, ur // 4, :], scat_i[:, bass.ds(u * 2, 8)]).then_inc(sidx_done, 1)
                            since(pool, sidx_done, uj * 2 + ur // 4 + 1)
                        settled(pool, sum_done, u + 1, passed)
                        for k in range(2):
                            at = ur % 4 * 2 + k
                            pool.indirect_dma_start(
                                out=t["tabs"][into[k]],
                                out_offset=bass.IndirectOffsetOnAxis(ap=sidx[:, ur // 4, at:at + 1], axis=0),
                                in_=summed[:, ur % 2, k, :], in_offset=None, compute_op=ALU.add,
                                bounds_check=TROWS - 1,
                            ).then_inc(tab_in[into[k]], 16)
                split_steps(pool, NPAIR, 6, step, 8)
                for tab in range(NTAB):
                    pool.wait_ge(tab_in[tab], 16 * (TILES // NTAB))

            @block.scalar
            def _(act):
                act.wait_ge(w_in4, 16 * 9)
                inv = 1.0 / 32.0
                act.activation(ro_s[0:S, :], ro_raw[0:S, 0, :], ACT.Copy, scale=inv).then_inc(ro_ok, 1)
                act.activation(ro_s[S:P, :], ro_raw[S:P, 0, :], ACT.Copy, scale=inv * 3.0 ** -0.5).then_inc(ro_ok, 1)
                for k in range(2):
                    for q in range(4):
                        cross = q == 3 or (k == 1 and q == 1)
                        act.activation(ro_v[V * q:V * q + V, k, :], ro_raw[V * q:V * q + V, 1 + k, :], ACT.Copy,
                                       scale=inv * (2.0 ** -0.5 if cross else 1.0)).then_inc(ro_ok, 1)

                def step(s, j, r):
                    if r % 2 == 0:
                        g = j * 2 + r // 2 + 1
                        if runs(g, NGRP):
                            relu(g, (r // 2 + 1) % 2)
                    u, uj, ur = lagged(s, j, r, 1, 4)
                    if runs(u, NPAIR):
                        act.wait_ge(t_ready, u + 1)
                        since(act, o_ready, u - 1)
                        act.activation(featt[:, ur % 2, :, :, :].rearrange("p k a b -> p k (a b)"), ps_t[:, :, 0:384],
                                       ACT.Copy).then_inc(t_done, 1)
                    u, uj, ur = lagged(s, j, r, 2, 4)
                    if runs(u, NPAIR):
                        act.wait_ge(o_ready, u + 1)
                        since(act, d_ready, u - 1)
                        act.activation(msg[:, ur % 2, :, 0:96], ps_o[:, :, 0:96], ACT.Copy).then_inc(os_done, 1)
                    u, uj, ur = lagged(s, j, r, LAST, 4)
                    if runs(u, NPAIR):
                        act.wait_ge(d_ready, u + 1)
                        for k in range(2):
                            t2 = ((ur - 2) * 2 + k) % NTAB
                            turn = uj * 2 + (ur - 2) * 2 // NTAB + 1
                            since(act, tab_in[t2], 16 * turn)
                        act.activation(summed[:, ur % 2, :, :], ps_d[:, :, 0:OW], ACT.Copy).then_inc(sum_done, 1)

                def relu(g, slot):
                    act.wait_ge(hid_ready, g + 1)
                    since(act, w4_ready, 2 * (g - 1))
                    act.activation(hid[:, slot, :], ps_h[:, :], ACT.Relu).then_inc(relu_done, 1)
                relu(0, 0)
                split_steps(act, NPAIR, LAST, step, 4, short=2)

            @block.tensor
            def _(pe):
                pe.wait_ge(w_in4, 16 * 9)
                pe.wait_ge(ro_ok, 10)

                def hidden(g, slot, turn):
                    pe.wait_ge(ea_in[slot], 16 * (turn + 1))
                    since(pe, relu_done, g)
                    pe.matmul(ps_h[:, :], wf1[:, :], ea64[:, slot, :], start=True, stop=True).then_inc(hid_ready, 1)

                def step(s, j, r):
                    if r % 2 == 0:
                        g = j * 2 + r // 2 + 1
                        if runs(g, NGRP):
                            hidden(g, (r // 2 + 1) % 2, j + (r // 2 + 1) // 2)
                    if runs(s, NPAIR):
                        pe.wait_ge(relu_done, j * 2 + r // 2 + 1)
                        since(pe, feat_done, s - 1)
                        h = slice(S * (r % 2), S * (r % 2) + S)
                        for k in range(2):
                            last = pe.matmul(ps_w[r % 2][:, k, 0:224], hid[h, r // 2, P * k:P * k + P], wf2[h, :],
                                             start=True, stop=True)
                        last.then_inc(w4_ready, 1)
                    u, _, ur = lagged(s, j, r, 1, 4)
                    if runs(u, NPAIR):
                        pe.wait_ge(feat_done, u + 1)
                        since(pe, t_done, u)
                        for k in range(2):
                            for c in range(3):
                                last = pe.transpose(ps_t[:, k, P * c:P * c + P], feat[:, ur % 2, k, c, :], ident[:, :])
                        last.then_inc(t_ready, 1)
                    u, _, ur = lagged(s, j, r, 2, 4)
                    if runs(u, NPAIR):
                        pe.wait_ge(t_done, u + 1)
                        since(pe, ov_done, u)
                        since(pe, os_done, u)
                        for k in range(2):
                            pe.matmul(ps_o[:, k, 0:96], featt[:, ur % 2, k, 0, :], ro_s[:, :], start=True, stop=True)
                            for c in range(2):
                                last = pe.matmul(ps_o[:, k, 96 + 64 * c:192 + 64 * c], featt[:, ur % 2, k, 1 + c, :],
                                                 ro_v[:, c, :], start=True, stop=True)
                        last.then_inc(o_ready, 1)
                    u, _, ur = lagged(s, j, r, LAST, 4)
                    if runs(u, NPAIR):
                        pe.wait_ge(os_done, u + 1)
                        pe.wait_ge(ov_done, u + 1)
                        pe.wait_ge(same_done, u + 1)
                        since(pe, sum_done, u)
                        for k in range(2):
                            last = pe.matmul(ps_d[:, k, 0:OW], same[:, ur, k, :], msg[:, ur % 2, k, :],
                                             start=True, stop=True)
                        last.then_inc(d_ready, 1)
                hidden(0, 0, 0)
                split_steps(pe, NPAIR, LAST, step, 4, short=2)

            @block.vector
            def _(dve):
                dve.memset(feat[:, :, :, 0, 96:P], 0.0).then_inc(fz, 1)

                def products(u, j, r):
                    x = xg[:, r, :, :]
                    dve.wait_ge(g_in[r], 32 * (j + 1))

                    def shv(c):
                        return sh[:, bass.ds(u * 2, 2), c:c + 3].unsqueeze(3).to_broadcast([P, 2, 3, V])

                    def xv(c):
                        return x[:, :, S + V * c:S + V * c + 3 * V].rearrange("p k (c u) -> p k c u", c=3)
                    since(dve, xx_done, 3 * u)
                    dve.tensor_tensor(mm[:, 0, :, :, :], xv(0), shv(0), ALU.mult)
                    dve.tensor_tensor(mm[:, 1, :, :, :], xv(1), shv(2), ALU.mult)
                    dve.tensor_tensor(mm[:, 2, :, :, :], xv(2), shv(1), ALU.mult).then_inc(m_done, 1)
                    dve.wait_ge(m_done, u + 1)
                    since(dve, feat_done, u)
                    dve.tensor_tensor(qq[:, 0, :, :], mm[:, 0, :, 0, :], mm[:, 0, :, 1, :], ALU.add).then_inc(xx_done, 1)
                    dve.tensor_tensor(xx[:, :, :, :], mm[:, 1, :, :, :], mm[:, 2, :, :, :], ALU.subtract).then_inc(xx_done, 1)
                    dve.wait_ge(xx_done, 3 * u + 1)
                    dve.tensor_tensor(qq[:, 1, :, :], qq[:, 0, :, :], mm[:, 0, :, 2, :], ALU.add).then_inc(xx_done, 1)
                    dve.wait_ge(w4_ready, u + 1)
                    since(dve, t_ready, u - 1)
                    p = r % 2
                    w = ps_w[p]
                    dve.tensor_tensor(feat[:, p, :, 0:2, 0:S], w[:, :, 0:2 * S].rearrange("p k (a s) -> p k a s", a=2),
                                      x[:, :, 0:S].unsqueeze(2).to_broadcast([P, 2, 2, S]), ALU.mult)
                    flat = feat[:, p, :, :, :].rearrange("p k a b -> p k (a b)")
                    v_part = flat[:, :, P + S:3 * P].rearrange("p k (c x u) -> p k c x u", c=3, x=2)
                    dve.tensor_tensor(v_part[:, :, :, 0, :], w[:, :, 128:160].unsqueeze(2).to_broadcast([P, 2, 3, V]),
                                      xv(0), ALU.mult)
                    dve.wait_ge(xx_done, 3 * u + 3)
                    dve.tensor_tensor(flat[:, :, S:96], w[:, :, 160:192], qq[:, 1, :, :], ALU.mult)
                    dve.tensor_tensor(v_part[:, :, :, 1, :], w[:, :, 192:224].unsqueeze(2).to_broadcast([P, 2, 3, V]),
                                      xx[:, :, :, :], ALU.mult).then_inc(feat_done, 1)

                def equal(u, j, r):
                    dve.wait_ge(sb_in[r], 16 * (j + 1))
                    since(dve, d_ready, u - 3)
                    dve.tensor_tensor(same[:, r, :, :], src_bc[:, r, :, :],
                                      src_f[:, bass.ds(u * 2, 2)].unsqueeze(2).to_broadcast([P, 2, P]),
                                      ALU.is_equal).then_inc(same_done, 1)

                def finish(u, r):
                    dve.wait_ge(os_done, u + 1)
                    since(dve, ov_done, u)
                    dve.tensor_tensor(ash[:, :, :, :], ps_o[:, :, 96:128].unsqueeze(2).to_broadcast([P, 2, 3, V]),
                                      sh[:, bass.ds(u * 2, 2), 0:3].unsqueeze(3).to_broadcast([P, 2, 3, V]),
                                      ALU.mult).then_inc(ash_done, 1)
                    dve.wait_ge(ash_done, u + 1)
                    since(dve, d_ready, u - 1)
                    dve.tensor_tensor(msg[:, r % 2, :, 96:OW], ps_o[:, :, 128:224],
                                      ash[:, :, :, :].rearrange("p k c u -> p k (c u)"), ALU.add).then_inc(ov_done, 1)

                def step(s, j, r):
                    if runs(s, NPAIR):
                        products(s, j, r)
                        equal(s, j, r)
                    u, _, ur = lagged(s, j, r, 2, 4)
                    if runs(u, NPAIR):
                        finish(u, ur)
                split_steps(dve, NPAIR, 2, step, 4)

        with ExitStack() as c5:
            tabs = sb(c5, "tabs", [P, NC, NTAB, FT, OW])
            tsum = sb(c5, "tsum", [P, 2, 2, FT, OW])
            so = sb(c5, "so", [P, 2, FT, OW])
            sg = sb(c5, "sg", [P, 2, FT, 96])
            upd = sb(c5, "upd", [P, 2, FT, D])
            bst5 = sb(c5, "bst5", [P, NT, 6])
            orow = sb(c5, "orow", [P, NC, FT, D])
            tin = [sem(c5, f"tin{i}") for i in range(NC)]
            half_done, half2_done, so_done, sg_done, upd_done, res_done, bs5, mv5 = (
                sem(c5, n) for n in ("half_done", "half2_done", "so_done", "sg_done", "upd_done", "res_done", "bs5", "mv5"))
            lv5, lr5, on_done, ch5, o_out = sem(c5, "lv5"), sem(c5, "lr5"), sem(c5, "on_done"), sem(c5, "ch5"), sem(c5, "o_out")
            block = c5.enter_context(nc.Block())

            @block.sync
            def _(sp):
                for m in range(NC):
                    for k in range(2):
                        sp.dma_start(tabs[:, m, k, :, :], tile_rows(t["tabs"][k], m)).then_inc(tin[m], 16)
                for m in range(NC):
                    sp.wait_ge(on_done, m + 1)
                    sp.dma_start(tile_rows(out, m), orow[:, m, :, :]).then_inc(o_out, 16)
                sp.wait_ge(o_out, 16 * NC)

            @block.gpsimd
            def _(pool):
                for m in range(NC):
                    pool.wait_ge(tin[m], 16 * NTAB)
                    since(pool, so_done, m - 1)
                    pool.tensor_tensor(tsum[:, m % 2, 1, :, :], tabs[:, m, 2, :, :], tabs[:, m, 3, :, :],
                                       ALU.add).then_inc(half2_done, 1)

            @block.scalar
            def _(act):
                for m in range(NC):
                    for k in range(2, NTAB):
                        act.dma_start(tabs[:, m, k, :, :], tile_rows(t["tabs"][k], m)).then_inc(tin[m], 16)
                for m in range(NC):
                    act.wait_ge(so_done, m + 1)
                    since(act, upd_done, m - 1)
                    act.activation(sg[:, m % 2, :, :], so[:, m % 2, :, 0:96], ACT.Sigmoid).then_inc(sg_done, 1)
                act.wait_ge(lv5, 1)
                act.activation(ntmp[:, 0, :], ntmp[:, 1, :], ACT.Sqrt).then_inc(lr5, 1)

            @block.vector
            def _(dve):
                done = [0]

                def link(ins):
                    done[0] += 1
                    ins.then_inc(ch5, 1)
                    dve.wait_ge(ch5, done[0])

                def sums(m):
                    r = m % 2
                    dve.wait_ge(tin[m], 16 * NTAB)
                    dve.tensor_tensor(tsum[:, r, 0, :, :], tabs[:, m, 0, :, :], tabs[:, m, 1, :, :], ALU.add).then_inc(half_done, 1)
                    dve.wait_ge(half_done, m + 1)
                    dve.wait_ge(half2_done, m + 1)
                    dve.tensor_tensor(so[:, r, :, :], tsum[:, r, 0, :, :], tsum[:, r, 1, :, :], ALU.add).then_inc(so_done, 1)

                def update(m):
                    r = m % 2
                    dve.wait_ge(sg_done, m + 1)
                    dve.tensor_tensor(upd[:, r, :, 0:S], so[:, r, :, 0:S], sg[:, r, :, 0:S], ALU.mult)
                    dve.tensor_tensor(upd[:, r, :, S:D].rearrange("p a (c u) -> p a c u", c=3),
                                      so[:, r, :, 96:OW].rearrange("p a (c u) -> p a c u", c=3),
                                      sg[:, r, :, S:96].unsqueeze(2).to_broadcast([P, FT, 3, V]), ALU.mult).then_inc(upd_done, 1)
                    dve.wait_ge(upd_done, m + 1)
                    here = xres[:, m * FT:(m + 1) * FT, :]
                    dve.tensor_tensor(here, here, upd[:, r, :, :], ALU.add).then_inc(res_done, 1)
                    dve.wait_ge(res_done, m + 1)
                    for u in range(m * FT, (m + 1) * FT):
                        dve.bn_stats(bst5[:, u, :], xres[:, u, :]).then_inc(bs5, 1)
                    for u in range(m * FT, (m + 1) * FT):
                        dve.wait_ge(bs5, u + 1)
                        dve.bn_aggr(mv[:, u, :], bst5[:, u, :]).then_inc(mv5, 1)

                for m in range(NC + 1):
                    if m < NC:
                        sums(m)
                    if m:
                        update(m - 1)
                dve.wait_ge(mv5, NT)
                layer_norm_scale(dve, link, mv, ntmp, rstd, lv5, lr5)
                for u in range(NT):
                    m, at = divmod(u, FT)
                    mean, scale = mv[:, u, 0:1], rstd[:, u:u + 1]
                    dve.tensor_scalar(orow[:, m, at, 0:S], xres[:, u, 0:S], mean, scale, ALU.subtract, ALU.mult)
                    last = dve.tensor_scalar(orow[:, m, at, S:D].rearrange("p (u c) -> p c u", c=3),
                                             xres[:, u, S:D].rearrange("p (c u) -> p c u", c=3), mean, scale,
                                             ALU.subtract, ALU.mult)
                    if at == FT - 1:
                        last.then_inc(on_done, 1)


def layer_norm_scale(dve, link, mv, ntmp, rstd, var_ready, root_ready):
    dve.tensor_scalar(ntmp[:, 1, :], mv[:, :, 1], EPS, None, ALU.add).then_inc(var_ready, 1)
    dve.wait_ge(root_ready, 1)
    link(dve.reciprocal(rstd[:, :], ntmp[:, 0, :]))
    link(dve.tensor_tensor(ntmp[:, 0, :], rstd[:, :], rstd[:, :], ALU.mult))
    link(dve.tensor_tensor(ntmp[:, 0, :], ntmp[:, 0, :], ntmp[:, 1, :], ALU.mult))
    link(dve.tensor_scalar(ntmp[:, 0, :], ntmp[:, 0, :], -0.5, 1.5, ALU.mult, ALU.add))
    link(dve.tensor_tensor(rstd[:, :], rstd[:, :], ntmp[:, 0, :], ALU.mult))


def split_steps(eng, units, lag, body, unroll=2, short=0):
    first = -(-(lag + 2) // unroll) * unroll
    last = max(first, (units - short) // unroll * unroll)
    for s in range(first):
        body(s, s // unroll, s % unroll)
    if last > first:
        with eng.Fori(first // unroll, last // unroll) as j:
            for r in range(unroll):
                body(j * unroll + r, j, r)
    for s in range(last, units + lag):
        body(s, s // unroll, s % unroll)


def kernel(**inputs):
    import numpy as np
    import concourse.bacc as bacc
    from concourse.bass_utils import run_bass_kernel_spmd

    nc = bacc.Bacc("TRN2", target_bir_lowering=False, num_devices=1)
    arr = {k: np.asarray(v) for k, v in inputs.items()}

    def pad(a, n, value):
        full = np.full((n,) + a.shape[1:], value, a.dtype)
        full[:a.shape[0]] = a
        return full

    def cols(a):
        return np.ascontiguousarray(a.reshape(-1, P, *a.shape[1:]).swapaxes(0, 1))

    x = pad(arr["x"], NP, 0)
    x = np.concatenate([x[:, :S], x[:, S:].reshape(NP, V, 3).transpose(0, 2, 1).reshape(NP, 3 * V)], 1)
    src, dst = pad(arr["src"], EP, N), pad(arr["dst"], EP, N)
    ea8, ea64 = pad(arr["edge_attr_8"], EP, 0), pad(arr["edge_attr_64"], EP, 0)
    data = {
        "x_rows": cols(x), "xt": np.ascontiguousarray(x.T),
        "a_col": cols(pad(arr["node_vec1"][:, 0], NP, 0)),
        "src_col": cols(src), "dst_col": cols(dst), "src_rows": src.reshape(NGRP, GE),
        "dst_first": np.ascontiguousarray(dst[::GE]).reshape(1, NGRP),
        "ea3": cols(pad(arr["edge_attr_3"], EP, 1)), "ea4": cols(pad(arr["edge_attr_4"], EP, 0)),
        "ea8": np.ascontiguousarray(ea8.reshape(NGRP, 2, 256, 8).transpose(1, 3, 0, 2)).reshape(16, NGRP * 256),
        "ea64": np.ascontiguousarray(ea64.reshape(NGRP, 2, 256, 64).transpose(0, 1, 3, 2)).reshape(NGRP, P, 256),
    }
    for name in arr:
        if name.startswith(("L0_gnn_W", "L1_gnn_W")):
            data[name] = arr[name]
    arrays, t = {}, {}
    for name, a in data.items():
        arrays["in_" + name] = np.ascontiguousarray(a)
        t[name] = nc.dram_tensor("in_" + name, a.shape, mybir.dt.from_np(a.dtype), kind="ExternalInput").ap()

    def scratch(name, shape):
        return nc.dram_tensor(name, shape, F32, kind="Internal").ap()
    t["f0"] = scratch("f0", (NP, D))
    t["f1"] = scratch("f1", (NP, GW))
    t["src_rows_f"] = scratch("src_rows_f", (NGRP, GE))
    t["src_pairs_f"] = t["src_rows_f"].rearrange("g (k e) -> (g k) e", k=2)
    t["tabs"] = [scratch(f"tab{i}", (TROWS, OW)) for i in range(NTAB)]
    out = nc.dram_tensor("out", (NP, D), F32, kind="ExternalOutput").ap()
    gnn_kernel(nc, t, out)
    r = run_bass_kernel_spmd(nc, [arrays], core_ids=[0])
    return r.results[0]["out"][:N]
```

```python
from contextlib import ExitStack

import concourse.bass as bass
from concourse import mybir
from concourse.alu_op_type import AluOpType as ALU

F32 = mybir.dt.float32
I32 = mybir.dt.int32
ACT = mybir.ActivationFunctionType
AX = mybir.AxisListType

N, E = 3125, 100000
FT = 5
P = 128
NT = -(-N // P)
NP = NT * P
NC = NT // FT
assert NT % FT == 0
S, V = 64, 32
D = S + 3 * V
G = 4
NGRP = -(-E // (P * G))
NGRP += NGRP % 2
TILES = NGRP * G
EP = TILES * P
GE = G * P
WIN = 24
SWEEP = -(-(N + 1) // WIN)
ACCW = max(NP, N + WIN, SWEEP * WIN)
NTAB = 4
ZROWS = -(-(N + P) // (NGRP // 2))
TROWS = NGRP // 2 * ZROWS
OW = 96 + 96
GW = S + 5 * V
NPAIR = TILES // 2
EPS = 1e-5


def since(eng, sem, count):
    if not isinstance(count, int) or count > 0:
        eng.wait_ge(sem, count)


def settled(eng, sem, count, passed):
    since(eng, sem, count)
    if not isinstance(count, int):
        eng.sem_inc(passed, 1)


def steps(eng, total, body, first, unroll):
    first = min(-(-first // unroll) * unroll, total)
    last = max(first, total // unroll * unroll)
    for s in range(first):
        body(s, s // unroll, s % unroll)
    if last > first:
        with eng.Fori(first // unroll, last // unroll) as j:
            for r in range(unroll):
                body(j * unroll + r, j, r)
    for s in range(last, total):
        body(s, s // unroll, s % unroll)


def lagged(s, j, r, lag, unroll):
    return s - lag, j + (r - lag) // unroll, (r - lag) % unroll


def runs(u, total):
    return not isinstance(u, int) or 0 <= u < total


def gnn_kernel(nc, t, out):
    top = ExitStack()
    with top:
        def sb(ctx, name, shape, dt=F32):
            return ctx.enter_context(nc.sbuf_tensor(name, shape, dt))

        def pb(ctx, name, shape, dt=F32):
            return ctx.enter_context(nc.psum_tensor(name, shape, dt))

        def sem(ctx, name):
            return ctx.enter_context(nc.semaphore(name))

        src_f = sb(top, "src_f", [P, TILES])
        rel_f = sb(top, "rel_f", [P, TILES])
        dst_f = sb(top, "dst_f", [P, TILES])
        src_i = sb(top, "src_i", [P, TILES], I32)
        dst_i = sb(top, "dst_i", [P, TILES], I32)
        scat_i = sb(top, "scat_i", [P, TILES], I32)
        base_i = sb(top, "base_i", [P, NGRP], I32)
        sh = sb(top, "sh", [P, TILES, 5])
        cnt = sb(top, "cnt", [P, TILES])
        lower = sb(top, "lower", [P, P])
        ident = sb(top, "ident", [P, P])
        xres = sb(top, "xres", [P, NT, D])
        a_col = sb(top, "a_col", [P, NT])
        a2_col = sb(top, "a2_col", [P, NT])
        win_ok = sb(top, "win_ok", [P, 1], I32)
        mv = sb(top, "mv", [P, NT, 2])
        rstd = sb(top, "rstd", [P, NT])
        ntmp = sb(top, "ntmp", [P, 2, NT])

        wf1 = sb(top, "wf1", [P, P])
        wf2 = sb(top, "wf2", [P, 224])
        ro_raw = sb(top, "ro_raw", [P, 3, 96])
        ro_s = sb(top, "ro_s", [P, 96])
        ro_v = sb(top, "ro_v", [P, 2, 96])

        passed = sem(top, "passed")

        def rows(dram, tile):
            return dram[bass.ds(tile * P, P), :]

        def tile_rows(dram, m):
            return dram[m * FT * P:(m + 1) * FT * P, :].rearrange("(a p) f -> p a f", p=P)

        cacc = ExitStack()
        acc_a = sb(cacc, "acc_a", [P, 4, ACCW])
        acc_b = sb(cacc, "acc_b", [96, 1, ACCW])
        acc_c = sb(cacc, "acc_c", [96, 3, ACCW])
        with ExitStack() as c1:
            base_f = sb(c1, "base_f", [P, NGRP])
            rows_i = sb(c1, "rows_i", [NGRP // 2, 2, GE], I32)
            rows_f = sb(c1, "rows_f", [NGRP // 2, 2, GE])
            ones = sb(c1, "ones", [P, P])
            ext = sb(c1, "ext", [P, 4])
            w_s = sb(c1, "w_s", [S, 2, S])
            w_v = sb(c1, "w_v", [96, 2, 96])
            w_s2 = sb(c1, "w_s2", [S, 2, S])
            w_v2 = sb(c1, "w_v2", [96, 2, 96])
            xt_s = sb(c1, "xt_s", [S, NP])
            xt_v = sb(c1, "xt_v", [96, NP])
            frow = sb(c1, "frow", [P, 2, FT, D])
            ps_n = [pb(c1, f"ps_n{i}", [P, 512]) for i in range(2)]
            ps_e = pb(c1, "ps_e", [P, 512])
            idx_in, rows_in = sem(c1, "idx_in"), sem(c1, "rows_in")
            wn_zero, wn_in, wn_scaled = sem(c1, "wn_zero"), sem(c1, "wn_in"), sem(c1, "wn_scaled")
            x_in, a_in = sem(c1, "x_in"), sem(c1, "a_in")
            xt_in = sem(c1, "xt_in")
            f_out = [sem(c1, f"f_out{i}") for i in range(2)]
            consts, rowsf_done, rows_out = sem(c1, "consts"), sem(c1, "rowsf_done"), sem(c1, "rows_out")
            conv, ext_done, cnt_ps = sem(c1, "conv"), sem(c1, "ext_done"), sem(c1, "cnt_ps")
            n_ready, f_ready, res_ready = sem(c1, "n_ready"), sem(c1, "f_ready"), sem(c1, "res_ready")
            zeroed, dv = sem(c1, "zeroed"), sem(c1, "dv")
            block = c1.enter_context(nc.Block())

            @block.sync
            def _(sp):
                sp.dma_start(src_i[:, :], t["src_col"]).then_inc(idx_in, 16)
                sp.dma_start(dst_i[:, :], t["dst_col"]).then_inc(idx_in, 16)
                sp.dma_start(base_i[:, :], t["dst_first"][0:1, :].to_broadcast([P, NGRP])).then_inc(idx_in, 16)
                sp.dma_start(rows_i[:, :, :], t["src_rows"].rearrange("(p a) e -> p a e", a=2)).then_inc(rows_in, 16)
                sp.wait_ge(wn_zero, 1)
                sp.dma_start(w_s[:, 0, :], t["L0_gnn_Wl1_0"]).then_inc(wn_in, 16)
                sp.dma_start(w_s[:, 1, :], t["L0_gnn_Wsc0"]).then_inc(wn_in, 16)
                for c in range(3):
                    for k, name in enumerate(("L0_gnn_Wl1_1", "L0_gnn_Wsc1")):
                        sp.dma_start(w_v[V * c:V * c + V, k, V * c:V * c + V], t[name]).then_inc(wn_in, 16)
                sp.dma_start(xres[:, :, :], t["x_rows"]).then_inc(x_in, 16)
                sp.wait_ge(rowsf_done, 1)
                sp.dma_start(t["src_rows_f"].rearrange("(p a) e -> p a e", a=2), rows_f[:, :, :]).then_inc(rows_out, 16)
                sp.wait_ge(rows_out, 16)

            @block.gpsimd
            def _(pool):
                pool.memset(w_v[:, :, :], 0.0).then_inc(wn_zero, 1)
                pool.memset(ones[:, :], 1.0).then_inc(consts, 1)
                pool.memset(lower[:, :], 1.0).then_inc(consts, 1)
                pool.memset(ident[:, :], 0.0).then_inc(consts, 1)
                pool.wait_ge(consts, 3)
                pool.affine_select(out=lower[:, :], in_=lower[:, :], compare_op=ALU.is_ge, fill=0.0,
                                   base=-1, pattern=[[-1, P]], channel_multiplier=1).then_inc(consts, 1)
                pool.affine_select(out=ident[:, :], in_=ident[:, :], compare_op=ALU.not_equal, fill=1.0,
                                   base=0, pattern=[[-1, P]], channel_multiplier=1).then_inc(consts, 1)
                pool.memset(acc_a[:, :, :], 0.0).then_inc(zeroed, 1)
                pool.memset(acc_b[:, :, :], 0.0).then_inc(zeroed, 1)
                pool.memset(acc_c[:, :, :], 0.0).then_inc(zeroed, 1)
                pool.wait_ge(consts, 5)
                pool.wait_ge(zeroed, 3)

            @block.tensor
            def _(pe):
                pe.wait_ge(wn_scaled, 2)

                pe.wait_ge(xt_in, 32)
                for u in range(NT):
                    r = u % 2
                    since(pe, f_ready, u - 1)
                    since(pe, res_ready, u - 1)
                    parts = ps_n[r][:, 0:320].rearrange("p (k f) -> p k f", k=2)
                    here = slice(u * P, u * P + P)
                    pe.matmul(parts[:, :, 0:S], xt_s[:, here], w_s2[:, :, :], start=True, stop=True)
                    pe.matmul(parts[:, :, S:D], xt_v[:, here], w_v2[:, :, :], start=True, stop=True).then_inc(n_ready, 1)
                pe.wait_ge(ext_done, 1)
                pe.wait_ge(consts, 1)
                pe.matmul(ps_e[:, 0:1], ones[:, :], ext[:, 2:3], start=True, stop=True).then_inc(cnt_ps, 1)

            @block.scalar
            def _(act):
                act.dma_start(xt_s[:, :], t["xt"][0:S, :]).then_inc(xt_in, 16)
                act.dma_start(xt_v[:, :], t["xt"][S:D, :]).then_inc(xt_in, 16)
                act.dma_start(a_col[:, :], t["a_col"]).then_inc(a_in, 16)
                act.wait_ge(wn_in, 16 * 8)
                act.activation(w_s2[:, :, :], w_s[:, :, :], ACT.Copy, scale=1.0 / 8.0).then_inc(wn_scaled, 1)
                act.activation(w_v2[:, :, :], w_v[:, :, :], ACT.Copy, scale=float(V) ** -0.5).then_inc(wn_scaled, 1)
                act.wait_ge(a_in, 16)
                for u in range(NT):
                    m, at = divmod(u, FT)
                    act.wait_ge(n_ready, u + 1)
                    if at == 0 and m >= 2:
                        act.wait_ge(f_out[m % 2], 16 * (m // 2))
                    act.activation(frow[:, m % 2, at, :], ps_n[u % 2][:, 0:D], ACT.Copy,
                                   scale=a_col[:, u:u + 1]).then_inc(f_ready, 1)
                    if at == FT - 1:
                        act.wait_ge(f_ready, u + 1)
                        act.dma_start(tile_rows(t["f0"], m),
                                      frow[:, m % 2, :, :]).then_inc(f_out[m % 2], 16)
                act.wait_ge(f_out[0], 16 * (-(-NT // FT // 2)))
                act.wait_ge(f_out[1], 16 * (NT // FT // 2))

            @block.vector
            def _(dve):
                done = [0]

                def link(ins):
                    done[0] += 1
                    ins.then_inc(dv, 1)
                    dve.wait_ge(dv, done[0])

                dve.wait_ge(idx_in, 48)
                dve.tensor_copy(src_f[:, :], src_i[:, :]).then_inc(conv, 1)
                dve.tensor_copy(dst_f[:, :], dst_i[:, :]).then_inc(conv, 1)
                dve.tensor_copy(base_f[:, :], base_i[:, :]).then_inc(conv, 1)
                dve.wait_ge(rows_in, 16)
                dve.tensor_copy(rows_f[:, :, :], rows_i[:, :, :]).then_inc(rowsf_done, 1)
                dve.wait_ge(conv, 3)
                link(dve.tensor_tensor(rel_f[:, :].rearrange("p (g k) -> p g k", k=G),
                                       dst_f[:, :].rearrange("p (g k) -> p g k", k=G),
                                       base_f[:, :].unsqueeze(2).to_broadcast([P, NGRP, G]), ALU.subtract))
                dve.wait_ge(a_in, 16)
                dve.tensor_tensor(a2_col[:, :], a_col[:, :], a_col[:, :], ALU.mult)
                link(dve.tensor_reduce(ext[:, 0:1], rel_f[:, :], AX.X, ALU.max))
                link(dve.tensor_reduce(ext[:, 1:2], rel_f[:, :], AX.X, ALU.min))
                link(dve.tensor_scalar(ext[:, 0:1], ext[:, 0:1], float(WIN), None, ALU.is_ge))
                link(dve.tensor_scalar(ext[:, 1:2], ext[:, 1:2], 0.0, None, ALU.is_lt))
                dve.tensor_tensor(ext[:, 2:3], ext[:, 0:1], ext[:, 1:2], ALU.add).then_inc(ext_done, 1)

                dve.wait_ge(x_in, 16)

                for u in range(NT):
                    dve.wait_ge(f_ready, u + 1)
                    dve.scalar_tensor_tensor(xres[:, u, :], ps_n[u % 2][:, D:2 * D], a_col[:, u:u + 1], xres[:, u, :],
                                             ALU.mult, ALU.add).then_inc(res_ready, 1)

                dve.wait_ge(cnt_ps, 1)
                link(dve.tensor_scalar(win_ok[:, :], ps_e[:, 0:1], 0.0, None, ALU.is_equal))

        with cacc:
            r_raw = sb(cacc, "r_raw", [P, 5, 96])
            r_s = sb(cacc, "r_s", [P, 2, 65])
            r_v = sb(cacc, "r_v", [P, 4, 96])
            with ExitStack() as c2:
                w1 = sb(c2, "w1", [16, P])
                w2 = sb(c2, "w2", [P, P])
                w3 = sb(c2, "w3", [P, 192])
                w3raw = ro_raw[:, 0:2, :].rearrange("p a b -> p (a b)")
                ea8 = sb(c2, "ea8", [16, 2, 256])
                y = sb(c2, "y", [P, TILES, 4])
                h1 = sb(c2, "h1", [P, 2, 256])
                h2 = sb(c2, "h2", [P, 2, 256])
                gat = sb(c2, "gat", [P, 2, G, D])
                src_bc = sb(c2, "src_bc", [P, 2, G, P])
                eq_junk = sb(c2, "eq_junk", [P, G, P])
                pos = sb(c2, "pos", [P, WIN])
                ohot = sb(c2, "ohot", [P, G, WIN])
                sel = sb(c2, "sel", [P, 2, G, 4, WIN])
                ta = sb(c2, "ta", [P, 2, G, 2, S])
                tb = sb(c2, "tb", [P, 2, G, 3, V])
                tc = sb(c2, "tc", [P, 2, G, 3, V])
                dcur = sb(c2, "dcur", [P, G])
                ps_h1, ps_h2 = (pb(c2, n, [P, 512])[:, 0:256] for n in ("ps_h1", "ps_h2"))
                ps_w = [pb(c2, f"ps_w{i}", [P, G, 256]) for i in range(2)]
                ps_g = [pb(c2, f"ps_g{i}", [P, 512]) for i in range(2)]
                w_in, w_zero, w3_ok, y_in = sem(c2, "w_in"), sem(c2, "w_zero"), sem(c2, "w3_ok"), sem(c2, "y_in")
                pos_ok = sem(c2, "pos_ok")
                zrow = r_v[0:ZROWS, 0:2, :].rearrange("p a b -> p (a b)")
                rz, r_in, r_ok = sem(c2, "rz"), sem(c2, "r_in"), sem(c2, "r_ok")
                z_ok, tab_out = sem(c2, "z_ok"), sem(c2, "tab_out")
                ea8_in = [sem(c2, f"ea8_in{i}") for i in range(2)]
                srcb_in = [sem(c2, f"srcb_in{i}") for i in range(2)]
                gath = [sem(c2, f"gath{i}") for i in range(2)]
                h1_ready, g1_done, h2_ready, g2_done = (sem(c2, n) for n in ("h1_ready", "g1_done", "h2_ready", "g2_done"))
                w_ready, cnt_done, hot_done, sel_ready = (sem(c2, n) for n in ("w_ready", "cnt_done", "hot_done", "sel_ready"))
                prod_done, agg_done, acc_done, cur_done = (sem(c2, n) for n in ("prod_done", "agg_done", "acc_done", "cur_done"))
                gidx = sb(c2, "gidx", [P, 2, 2 * G], I32)
                gidx_done = sem(c2, "gidx_done")
                block = c2.enter_context(nc.Block())

                @block.sync
                def _(sp):
                    sp.wait_ge(w_zero, 2)
                    for h in range(2):
                        sp.dma_start(w1[8 * h:8 * h + 8, S * h:S * h + S], t["L0_gnn_Wfc1"]).then_inc(w_in, 16)
                        sp.dma_start(w2[S * h:S * h + S, S * h:S * h + S], t["L0_gnn_Wfc2"]).then_inc(w_in, 16)
                        sp.dma_start(w3raw[S * h:S * h + S, :], t["L0_gnn_Wfc3"]).then_inc(w_in, 16)
                    sp.dma_start(y[:, :, :], t["ea4"]).then_inc(y_in, 16)

                    def load_ea8(u, r):
                        since(sp, h1_ready, u - 1)
                        sp.dma_start(ea8[:, r, :], t["ea8"][:, bass.ds(u * 256, 256)]).then_inc(ea8_in[r], 16)

                    def load(u, j, r):
                        if r == 0:
                            for tab in t["tabs"]:
                                sp.dma_start(tab[bass.ds(j * ZROWS, ZROWS), :], zrow[:, :]).then_inc(tab_out, 16)
                        if not isinstance(u, int) or u + 1 < NGRP:
                            load_ea8(u + 1, (r + 1) % 2)
                        since(sp, cnt_done, G * (u - 1))
                        sp.dma_start(src_bc[:, r, :, :].rearrange("p k e -> p (k e)"),
                                     t["src_rows_f"][bass.ds(u, 1), :].to_broadcast([P, GE])).then_inc(srcb_in[r], 16)
                    load_ea8(0, 0)
                    sp.wait_ge(z_ok, 1)
                    split_steps(sp, NGRP, 0, load, 2, short=1)
                    sp.wait_ge(rz, 2)
                    sp.dma_start(r_raw[0:S, 0, 0:S], t["L0_gnn_Wl2_s"][0:S, :]).then_inc(r_in, 16)
                    sp.dma_start(r_raw[0:S, 0, S:S + 1], t["L0_gnn_Wa"][0:S, :]).then_inc(r_in, 16)
                    sp.dma_start(r_raw[S:P, 3, 0:V], t["L0_gnn_Wl2_v"][0:S, :]).then_inc(r_in, 16)
                    for c in range(3):
                        q = slice(V * c, V * c + V)
                        sp.dma_start(r_raw[q, 1, 0:S], t["L0_gnn_Wl2_s"][S:96, :]).then_inc(r_in, 16)
                        sp.dma_start(r_raw[q, 1, S:S + 1], t["L0_gnn_Wa"][S:96, :]).then_inc(r_in, 16)
                        sp.dma_start(r_raw[q, 2, V * c:V * c + V], t["L0_gnn_Wl2_v"][S:96, :]).then_inc(r_in, 16)
                    sp.wait_ge(tab_out, 16 * NTAB * (NGRP // 2))

                @block.gpsimd
                def _(pool):
                    pool.memset(w1[:, :], 0.0).then_inc(w_zero, 1)
                    pool.memset(w2[:, :], 0.0).then_inc(w_zero, 1)
                    pool.memset(r_v[:, :, :], 0.0).then_inc(z_ok, 1)
                    pool.memset(r_raw[:, :, :], 0.0).then_inc(rz, 1)
                    pool.memset(r_s[:, :, :], 0.0).then_inc(rz, 1)
                    pool.iota(pos[:, :], pattern=[[1, WIN]], base=0, channel_multiplier=0,
                              allow_small_or_imprecise_dtypes=True).then_inc(pos_ok, 1)

                    def gather(u, j, r):
                        if r % 2 == 0:
                            since(pool, prod_done, u - 2)
                            pool.tensor_copy(gidx[:, r // 2, :], src_i[:, bass.ds(u * G, 2 * G)]).then_inc(gidx_done, 1)
                            since(pool, gidx_done, j * 2 + r // 2 + 1)
                        since(pool, prod_done, u - 1)
                        if not isinstance(u, int):
                            pool.sem_inc(passed, 1)
                        for k in range(G):
                            at = r % 2 * G + k
                            pool.indirect_dma_start(
                                out=gat[:, r % 2, k, :], out_offset=None, in_=t["f0"],
                                in_offset=bass.IndirectOffsetOnAxis(ap=gidx[:, r // 2, at:at + 1], axis=0),
                            ).then_inc(gath[r % 2], 16)
                    steps(pool, NGRP, gather, 4, 4)

                @block.scalar
                def _(act):
                    act.wait_ge(w_in, 16 * 6)
                    act.activation(w3[:, :], w3raw[:, :], ACT.Copy, scale=1.0 / 8.0).then_inc(w3_ok, 1)

                    def gelus(u, j, r):
                        act.wait_ge(h1_ready, u + 1)
                        since(act, h2_ready, u - 1)
                        act.activation(h1[:, r, :], ps_h1[:, :], ACT.Gelu_apprx_tanh,
                                       scale=8.0 ** -0.5).then_inc(g1_done, 1)
                        act.wait_ge(h2_ready, u + 1)
                        since(act, w_ready, u - 1)
                        act.activation(h2[:, r, :], ps_h2[:, :], ACT.Gelu_apprx_tanh,
                                       scale=1.0 / 8.0).then_inc(g2_done, 1)
                    steps(act, NGRP, gelus, 4, 2)
                    act.wait_ge(r_in, 16 * 12)
                    act.wait_ge(tab_out, 16 * NTAB * (NGRP // 2))
                    inv = 3072.0 ** -0.5
                    act.activation(r_s[0:S, 0, :], r_raw[0:S, 0, 0:65], ACT.Copy, scale=inv).then_inc(r_ok, 1)
                    act.activation(r_s[0:96, 1, :], r_raw[0:96, 1, 0:65], ACT.Copy, scale=inv * 3.0 ** -0.5).then_inc(r_ok, 1)
                    for c in range(3):
                        act.activation(r_v[S:P, 1 + c, V * c:V * c + V], r_raw[S:P, 3, 0:V], ACT.Copy, scale=inv).then_inc(r_ok, 1)
                    act.activation(r_v[0:96, 0, :], r_raw[0:96, 2, :], ACT.Copy, scale=inv).then_inc(r_ok, 1)
                    act.wait_ge(r_ok, 6)

                def window_sums(pe, r, ready):
                    for n, (lhs, hi) in enumerate(((ta, P), (tb, 96), (tc, 96))):
                        for k in range(G):
                            last = pe.matmul(ps_g[r][0:hi, n * 4 * WIN:(n + 1) * 4 * WIN],
                                             lhs[:, r, k, :, :].rearrange("p a b -> p (a b)"),
                                             sel[:, r, k, :, :].rearrange("p a b -> p (a b)"),
                                             start=k == 0, stop=k == G - 1)
                    last.then_inc(ready, 1)

                @block.tensor
                def _(pe):
                    pe.wait_ge(w_in, 16 * 6)
                    pe.wait_ge(w3_ok, 1)

                    def layer1(u, r, j):
                        pe.wait_ge(ea8_in[r], 16 * (j + 1))
                        since(pe, g1_done, u)
                        pe.matmul(ps_h1[:, :], w1[:, :], ea8[:, r, :], start=True, stop=True).then_inc(h1_ready, 1)

                    def layer2(u, r):
                        pe.wait_ge(g1_done, u + 1)
                        since(pe, g2_done, u)
                        pe.matmul(ps_h2[:, :], w2[:, :], h1[:, r, :], start=True, stop=True).then_inc(h2_ready, 1)

                    def layer3(u, r):
                        pe.wait_ge(g2_done, u + 1)
                        since(pe, prod_done, u - 1)
                        for k in range(G):
                            h = S * (k // 2)
                            last = pe.matmul(ps_w[r][:, k, 0:192], h2[h:h + S, r, P * (k % 2):P * (k % 2) + P],
                                             w3[h:h + S, :], start=True, stop=True)
                        last.then_inc(w_ready, 1)

                    def fast():
                        def step(s, j, r):
                            if runs(s, NGRP):
                                layer1(s, r, j)
                            u, _, ur = lagged(s, j, r, 3, 2)
                            if runs(u, NGRP):
                                pe.wait_ge(sel_ready, u + 1)
                                pe.wait_ge(prod_done, u + 1)
                                since(pe, acc_done, u - 1)
                                window_sums(pe, ur, agg_done)
                            if runs(s, NGRP):
                                layer2(s, r)
                            u, _, ur = lagged(s, j, r, 1, 2)
                            if runs(u, NGRP):
                                layer3(u, ur)
                        split_steps(pe, NGRP, 3, step)

                    def general():
                        def step(u, j, r):
                            layer1(u, r, j)
                            layer2(u, r)
                            layer3(u, r)
                            settled(pe, prod_done, u + 1, passed)
                            with pe.Fori(0, SWEEP) as n:
                                pe.wait_ge(sel_ready, u * SWEEP + n + 1)
                                window_sums(pe, r, agg_done)
                                settled(pe, acc_done, u * SWEEP + n + 1, passed)
                        steps(pe, NGRP, step, 4, 2)

                    ok = pe.value_load(win_ok[0:1, 0:1], min_val=0, max_val=1)
                    with pe.If(ok):
                        fast()
                    with pe.Else():
                        general()

                @block.vector
                def _(dve):
                    dve.wait_ge(pos_ok, 1)
                    dve.wait_ge(y_in, 16)

                    def earlier(u, j, r):
                        dve.wait_ge(srcb_in[r], 16 * (j + 1))
                        since(dve, cnt_done, u * G)
                        for k in range(G):
                            col = bass.ds(u * G + k, 1)
                            dve.scalar_tensor_tensor(eq_junk[:, k, :], src_bc[:, r, k, :], src_f[:, col], lower[:, :],
                                                     ALU.is_equal, ALU.mult,
                                                     accum_out=cnt[:, col]).then_inc(cnt_done, 1)

                    def select(u, r, rel, hot_count):
                        since(dve, sel_ready, hot_count - 1)
                        dve.tensor_tensor(ohot[:, :, :], pos[:, :].unsqueeze(1).to_broadcast([P, G, WIN]),
                                          rel.unsqueeze(2).to_broadcast([P, G, WIN]), ALU.is_equal).then_inc(hot_done, 1)
                        dve.wait_ge(hot_done, hot_count)
                        dve.tensor_tensor(sel[:, r, :, :, :], ohot[:, :, :].unsqueeze(2).to_broadcast([P, G, 4, WIN]),
                                          y[:, bass.ds(u * G, G), :].unsqueeze(3).to_broadcast([P, G, 4, WIN]),
                                          ALU.mult).then_inc(sel_ready, 1)

                    def products(u, j, r):
                        dve.wait_ge(w_ready, u + 1)
                        dve.wait_ge(gath[r], 16 * G * (j + 1))
                        dve.tensor_tensor(ta[:, r, :, :, :], ps_w[r][:, :, 0:2 * S].rearrange("p k (a s) -> p k a s", a=2),
                                          gat[:, r, :, 0:S].unsqueeze(2).to_broadcast([P, G, 2, S]), ALU.mult)
                        gv = gat[:, r, :, S:D].rearrange("p k (c u) -> p k c u", c=3)
                        for dst, at in ((tb, 2 * S), (tc, 2 * S + V)):
                            last = dve.tensor_tensor(dst[:, r, :, :, :],
                                                     ps_w[r][:, :, at:at + V].unsqueeze(2).to_broadcast([P, G, 3, V]),
                                                     gv, ALU.mult)
                        last.then_inc(prod_done, 1)

                    def add_window(r, base):
                        for acc, hi, at, n in ((acc_a, P, 0, 4), (acc_b, 96, 4 * WIN, 1), (acc_c, 96, 9 * WIN, 3)):
                            part = acc[:, :, bass.ds(base, WIN)]
                            last = dve.tensor_tensor(part, part,
                                                     ps_g[r][0:hi, at:at + n * WIN].rearrange("p (c w) -> p c w", c=n),
                                                     ALU.add)
                        last.then_inc(acc_done, 1)

                    def fast():
                        def step(s, j, r):
                            if runs(s, NGRP):
                                since(dve, agg_done, s - 1)
                                select(s, r, rel_f[:, bass.ds(s * G, G)], s + 1)
                                products(s, j, r)
                            u, _, ur = lagged(s, j, r, 2, 2)
                            if runs(s, NGRP):
                                earlier(s, j, r)
                            if runs(u, NGRP):
                                base = dve.value_load(base_i[0:1, bass.ds(u, 1)], min_val=0, max_val=N)
                                dve.wait_ge(agg_done, u + 1)
                                since(dve, acc_done, u)
                                add_window(ur, base)
                        split_steps(dve, NGRP, 2, step)

                    def general():
                        def step(u, j, r):
                            earlier(u, j, r)
                            since(dve, acc_done, u * SWEEP)
                            products(u, j, r)
                            settled(dve, cur_done, u * (SWEEP + 1), passed)
                            dve.tensor_copy(dcur[:, :], dst_f[:, bass.ds(u * G, G)]).then_inc(cur_done, 1)
                            with dve.Fori(0, SWEEP) as n:
                                dve.wait_ge(cur_done, u * (SWEEP + 1) + n + 1)
                                select(u, r, dcur[:, :], u * SWEEP + n + 1)
                                dve.wait_ge(agg_done, u * SWEEP + n + 1)
                                add_window(r, n * WIN)
                                dve.tensor_scalar(dcur[:, :], dcur[:, :], float(-WIN), None, ALU.add).then_inc(cur_done, 1)
                        steps(dve, NGRP, step, 4, 2)

                    ok = dve.value_load(win_ok[0:1, 0:1], min_val=0, max_val=1)
                    with dve.If(ok):
                        fast()
                    with dve.Else():
                        general()

            with ExitStack() as c3:
                bst = sb(c3, "bst", [P, NT, 6])
                wn_s = sb(c3, "wn_s", [S, 160])
                wn_v = sb(c3, "wn_v", [96, 2, 96])
                ea3 = sb(c3, "ea3", [P, TILES, 3])
                nrm = sb(c3, "nrm", [P, 3, TILES])
                attr_in, sq_done, root_done = sem(c3, "attr_in"), sem(c3, "sq_done"), sem(c3, "root_done")
                wnz, wn_in2 = sem(c3, "wnz"), sem(c3, "wn_in2")
                alpha = sb(c3, "alpha", [P, NT])
                colf = sb(c3, "colf", [P, TILES])
                pidx = sb(c3, "pidx", [P, 1])
                xt2_s = sb(c3, "xt2_s", [S, 2, P])
                xt2_v = sb(c3, "xt2_v", [96, 2, P])
                yrow = sb(c3, "yrow", [P, 2, FT, GW])
                skrow = sb(c3, "skrow", [P, 2, FT, OW])
                ps_r = [pb(c3, f"ps_r{i}", [P, 512]) for i in range(3)]
                ps_x = [pb(c3, f"ps_x{i}", [P, 4, P]) for i in range(2)]
                ps_y = [pb(c3, f"ps_y{i}", [P, 512]) for i in range(2)]
                r_ready, al_done, xp_done, bs_done, mv_done = (sem(c3, n) for n in ("r_ready", "al_done", "xp_done", "bs_done", "mv_done"))
                ln_var, ln_root, x1_done = sem(c3, "ln_var"), sem(c3, "ln_root"), sem(c3, "x1_done")
                tr_done, xt2_done, y_ready, y_done = (sem(c3, n) for n in ("tr_done", "xt2_done", "y_ready", "y_done"))
                y_out = [sem(c3, f"y_out{i}") for i in range(2)]
                wz, w_in4, ro_ok = sem(c3, "wz"), sem(c3, "w_in4"), sem(c3, "ro_ok")
                diag_done = sem(c3, "diag_done")
                pidx_ok, ch = sem(c3, "pidx_ok"), sem(c3, "ch")
                block = c3.enter_context(nc.Block())

                @block.sync
                def _(sp):
                    sp.wait_ge(wnz, 1)
                    sp.dma_start(wn_s[:, 0:S], t["L1_gnn_W_nl0"]).then_inc(wn_in2, 16)
                    sp.dma_start(wn_s[:, S:160], t["L1_gnn_W_skip0"]).then_inc(wn_in2, 16)
                    for c in range(3):
                        q = slice(V * c, V * c + V)
                        sp.dma_start(wn_v[q, 0, V * c:V * c + V], t["L1_gnn_W_nl1"]).then_inc(wn_in2, 16)
                        sp.dma_start(wn_v[q, 1, V * c:V * c + V], t["L1_gnn_W_skip1"]).then_inc(wn_in2, 16)
                    sp.dma_start(ea3[:, :, :], t["ea3"]).then_inc(attr_in, 16)
                    sp.wait_ge(wz, 2)
                    for h in range(2):
                        q = slice(S * h, S * h + S)
                        sp.dma_start(wf1[q, q], t["L1_gnn_W_fc1"]).then_inc(w_in4, 16)
                        sp.dma_start(wf2[q, :], t["L1_gnn_W_fc2"]).then_inc(w_in4, 16)
                    wos, wov = t["L1_gnn_W_out_s"], t["L1_gnn_W_out_v"]
                    sp.dma_start(ro_raw[0:96, 0, :], wos).then_inc(w_in4, 16)
                    sp.dma_start(ro_raw[0:S, 1, 0:V], wov[0:S, :]).then_inc(w_in4, 16)
                    sp.dma_start(ro_raw[S:P, 1, V:2 * V], wov[S:P, :]).then_inc(w_in4, 16)
                    sp.dma_start(ro_raw[0:S, 2, 0:V], wov[S:P, :]).then_inc(w_in4, 16)
                    sp.dma_start(ro_raw[S:P, 2, V:2 * V], wov[S:P, :]).then_inc(w_in4, 16)
                    for m in range(NC):
                        sp.wait_ge(y_done, (m + 1) * FT)
                        sp.dma_start(tile_rows(t["f1"], m), yrow[:, m % 2, :, :]).then_inc(y_out[m % 2], 16)
                        sp.dma_start(tile_rows(t["tabs"][0], m), skrow[:, m % 2, :, :]).then_inc(y_out[m % 2], 16)
                    sp.wait_ge(y_out[0], 32 * (-(-NC // 2)))
                    sp.wait_ge(y_out[1], 32 * (NC // 2))

                @block.gpsimd
                def _(pool):
                    pool.memset(wn_v[:, :, :], 0.0).then_inc(wnz, 1)
                    pool.memset(wf1[:, :], 0.0).then_inc(wz, 1)
                    pool.memset(ro_raw[:, :, :], 0.0).then_inc(wz, 1)
                    pool.iota(pidx[:, :], pattern=[[0, 1]], base=N, channel_multiplier=1,
                              allow_small_or_imprecise_dtypes=True).then_inc(pidx_ok, 1)

                @block.scalar
                def _(act):
                    def out_rows(u):
                        m, at = divmod(u, FT)
                        act.wait_ge(y_ready, u + 1)
                        if at == 0 and m >= 2:
                            act.wait_ge(y_out[m % 2], 32 * (m // 2))
                        act.activation(yrow[:, m % 2, at, 0:D], ps_y[u % 2][:, 0:D], ACT.Copy)
                        act.activation(yrow[:, m % 2, at, D:GW], ps_y[u % 2][:, S:S + 2 * V], ACT.Copy)
                        act.activation(skrow[:, m % 2, at, :], ps_y[u % 2][:, D:D + OW], ACT.Copy).then_inc(y_done, 1)

                    for m in range(NC):
                        cols = slice(m * FT * P, (m + 1) * FT * P)
                        for c in range(1, 3):
                            q = slice(V * c, V * c + V)
                            act.activation(acc_c[q, 0, cols], acc_c[q, c, cols], ACT.Copy).then_inc(diag_done, 1)
                    for m in range(NC):
                        if m == 1:
                            act.wait_ge(sq_done, 1)
                            act.activation(nrm[:, 1, :], nrm[:, 0, :], ACT.Sqrt).then_inc(root_done, 1)
                        tiles = slice(m * FT, (m + 1) * FT)
                        act.wait_ge(ln_var, m + 1)
                        act.activation(ntmp[:, 0, tiles], ntmp[:, 1, tiles], ACT.Sqrt).then_inc(ln_root, 1)
                        for u in range(m * FT, (m + 1) * FT):
                            act.wait_ge(tr_done, u + 1)
                            since(act, y_ready, u - 1)
                            act.activation(xt2_s[:, u % 2, :], ps_x[u % 2][0:S, 0, :], ACT.Copy)
                            act.activation(xt2_v[:, u % 2, :], ps_x[u % 2][0:96, 1, :], ACT.Copy).then_inc(xt2_done, 1)
                            if u > m * FT:
                                out_rows(u - 1)
                        out_rows((m + 1) * FT - 1)
                    act.wait_ge(w_in4, 16 * 9)
                    inv = 1.0 / 32.0
                    act.activation(ro_s[0:S, :], ro_raw[0:S, 0, :], ACT.Copy, scale=inv).then_inc(ro_ok, 1)
                    act.activation(ro_s[S:P, :], ro_raw[S:P, 0, :], ACT.Copy, scale=inv * 3.0 ** -0.5).then_inc(ro_ok, 1)
                    for k in range(2):
                        for q in range(4):
                            cross = q == 3 or (k == 1 and q == 1)
                            act.activation(ro_v[V * q:V * q + V, k, :], ro_raw[V * q:V * q + V, 1 + k, :], ACT.Copy,
                                           scale=inv * (2.0 ** -0.5 if cross else 1.0)).then_inc(ro_ok, 1)
                    act.wait_ge(ro_ok, 10)

                @block.tensor
                def _(pe):
                    def update(u):
                        since(pe, xp_done, u - 2)
                        here = slice(u * P, u * P + P)
                        to_s, to_v = ps_r[u % 3][:, 0:65], ps_r[u % 3][:, 65:161]
                        pe.matmul(to_s, acc_a[:, 0, here], r_s[:, 0, :], start=True, stop=False)
                        pe.matmul(to_s, acc_c[:, 0, here], r_s[0:96, 1, :], start=False, stop=True)
                        pe.matmul(to_v, acc_b[:, 0, here], r_v[0:96, 0, :], start=True, stop=False)
                        for c in range(3):
                            last = pe.matmul(to_v, acc_a[:, 1 + c, here], r_v[:, 1 + c, :], start=False, stop=c == 2)
                        last.then_inc(r_ready, 1)

                    def turn(u):
                        pe.wait_ge(x1_done, u + 1)
                        since(pe, xt2_done, u - 1)
                        pe.transpose(ps_x[u % 2][0:S, 0, :], xres[:, u, 0:S], ident[:, :])
                        pe.transpose(ps_x[u % 2][0:96, 1, :], xres[:, u, S:D], ident[:, :]).then_inc(tr_done, 1)

                    def project(u):
                        r = u % 2
                        pe.wait_ge(xt2_done, u + 1)
                        since(pe, y_done, u - 1)
                        pe.matmul(ps_y[r][:, 0:S], xt2_s[:, r, :], wn_s[:, 0:S], start=True, stop=True)
                        pe.matmul(ps_y[r][:, D:D + 96], xt2_s[:, r, :], wn_s[:, S:160], start=True, stop=True)
                        pe.matmul(ps_y[r][:, S:D], xt2_v[:, r, :], wn_v[:, 0, :], start=True, stop=True)
                        pe.matmul(ps_y[r][:, D + 96:D + OW], xt2_v[:, r, :], wn_v[:, 1, :], start=True,
                                  stop=True).then_inc(y_ready, 1)

                    for m in range(NC + 1):
                        if m < NC:
                            pe.wait_ge(diag_done, 2 * (m + 1))
                            for u in range(m * FT, (m + 1) * FT):
                                update(u)
                        if m == 1:
                            pe.wait_ge(wn_in2, 16 * 8)
                        if m:
                            for u in range((m - 1) * FT, m * FT):
                                turn(u)
                                if u > (m - 1) * FT:
                                    project(u - 1)
                            project(m * FT - 1)

                @block.vector
                def _(dve):
                    done = [0]

                    def link(ins):
                        done[0] += 1
                        ins.then_inc(ch, 1)
                        dve.wait_ge(ch, done[0])

                    dve.wait_ge(pidx_ok, 1)
                    link(dve.tensor_scalar(cnt[:, :], cnt[:, :], 1.0, None, ALU.min))
                    link(dve.tensor_scalar(colf[:, :], src_f[:, :], -1.0, pidx[:, :], ALU.mult, ALU.add))
                    link(dve.tensor_tensor(colf[:, :], colf[:, :], cnt[:, :], ALU.mult))
                    link(dve.tensor_tensor(scat_i[:, :], colf[:, :], src_f[:, :], ALU.add))

                    def updated(u):
                        here, ps = xres[:, u, :], ps_r[u % 3]
                        dve.wait_ge(r_ready, u + 1)
                        dve.tensor_tensor(alpha[:, u:u + 1], ps[:, S:S + 1], a2_col[:, u:u + 1], ALU.mult).then_inc(al_done, 1)
                        dve.wait_ge(al_done, u + 1)
                        dve.scalar_tensor_tensor(here[:, 0:S], ps[:, 0:S], alpha[:, u:u + 1], here[:, 0:S],
                                                 ALU.mult, ALU.add)
                        dve.scalar_tensor_tensor(here[:, S:D], ps[:, 65:161], alpha[:, u:u + 1], here[:, S:D],
                                                 ALU.mult, ALU.add).then_inc(xp_done, 1)
                        dve.wait_ge(xp_done, u + 1)
                        dve.bn_stats(bst[:, u, :], here).then_inc(bs_done, 1)

                    def squares():
                        dve.wait_ge(attr_in, 16)
                        link(dve.tensor_tensor(sh[:, :, 0:3], ea3[:, :, :], ea3[:, :, :], ALU.mult))
                        dve.tensor_reduce(nrm[:, 0, :], sh[:, :, 0:3], AX.X, ALU.add).then_inc(sq_done, 1)

                    def inverse():
                        dve.wait_ge(root_done, 1)
                        link(dve.reciprocal(nrm[:, 2, :], nrm[:, 1, :]))

                    def newton():
                        link(dve.tensor_tensor(colf[:, :], nrm[:, 2, :], nrm[:, 2, :], ALU.mult))
                        link(dve.tensor_tensor(colf[:, :], colf[:, :], nrm[:, 0, :], ALU.mult))
                        link(dve.tensor_scalar(colf[:, :], colf[:, :], -0.5 * 3.0 ** 0.5, 1.5 * 3.0 ** 0.5, ALU.mult, ALU.add))
                        link(dve.tensor_tensor(nrm[:, 2, :], nrm[:, 2, :], colf[:, :], ALU.mult))

                    def directions():
                        link(dve.tensor_tensor(sh[:, :, 0:3], ea3[:, :, :],
                                               nrm[:, 2, :].unsqueeze(2).to_broadcast([P, TILES, 3]), ALU.mult))
                        link(dve.tensor_copy(sh[:, :, 3:5], sh[:, :, 0:2]))

                    parts = (squares, inverse, newton, directions)
                    for m in range(NC):
                        chunk = range(m * FT, (m + 1) * FT)
                        for u in chunk:
                            updated(u)
                        for u in chunk:
                            dve.wait_ge(bs_done, u + 1)
                            dve.bn_aggr(mv[:, u, :], bst[:, u, :]).then_inc(mv_done, 1)
                        dve.wait_ge(mv_done, (m + 1) * FT)
                        layer_norm_scale(dve, link, mv, ntmp, rstd, ln_var, ln_root, slice(m * FT, (m + 1) * FT), m + 1)
                        for u in chunk:
                            dve.tensor_scalar(xres[:, u, :], xres[:, u, :], mv[:, u, 0:1], rstd[:, u:u + 1],
                                              ALU.subtract, ALU.mult).then_inc(x1_done, 1)
                        if m < len(parts):
                            parts[m]()

        with ExitStack() as c4:
            ea64 = sb(c4, "ea64", [P, 2, 256])
            hid = sb(c4, "hid", [P, 2, 256])
            src_bc = sb(c4, "src_bc4", [P, 4, 2, P])
            xg = sb(c4, "xg", [P, 4, 2, GW])
            mm = sb(c4, "mm", [P, 3, 2, 3, V])
            qq = sb(c4, "qq", [P, 2, 2, V])
            xx = sb(c4, "xx", [P, 2, 3, V])
            feat = sb(c4, "feat", [P, 2, 2, 3, P])
            featt = sb(c4, "featt", [P, 2, 2, 3, P])
            same = sb(c4, "same", [P, 4, 2, P])
            ash = sb(c4, "ash", [P, 2, 3, V])
            msg = sb(c4, "msg", [P, 2, 2, OW])
            summed = sb(c4, "summed", [P, 2, 2, OW])
            gidx = sb(c4, "gidx4", [P, 2, 8], I32)
            sidx = sb(c4, "sidx", [P, 2, 8], I32)
            gidx_done4, sidx_done = sem(c4, "gidx_done4"), sem(c4, "sidx_done")
            ps_h = pb(c4, "ps_h", [P, 512])[:, 0:256]
            ps_w = [pb(c4, f"ps_x4{i}", [P, 2, 256]) for i in range(2)]
            ps_t = pb(c4, "ps_t", [P, 2, 512])
            ps_o = pb(c4, "ps_o", [P, 2, 256])
            ps_d = pb(c4, "ps_d", [P, 2, 256])
            fz = sem(c4, "fz")
            ea_in = [sem(c4, f"ea_in{i}") for i in range(2)]
            sb_in = [sem(c4, f"sb_in{i}") for i in range(4)]
            g_in = [sem(c4, f"g_in{i}") for i in range(4)]
            tab_in = [sem(c4, f"tab_in{i}") for i in range(NTAB)]
            hid_ready, relu_done, w4_ready = (sem(c4, n) for n in ("hid_ready", "relu_done", "w4_ready"))
            m_done, xx_done, feat_done, same_done = (sem(c4, n) for n in ("m_done", "xx_done", "feat_done", "same_done"))
            t_ready, t_done, o_ready, os_done, ash_done, ov_done = (sem(c4, n) for n in ("t_ready", "t_done", "o_ready", "os_done", "ash_done", "ov_done"))
            d_ready, sum_done = sem(c4, "d_ready"), sem(c4, "sum_done")
            block = c4.enter_context(nc.Block())
            LAST = 3

            @block.sync
            def _(sp):
                def load_ea64(g, slot):
                    since(sp, hid_ready, g - 1)
                    sp.dma_start(ea64[:, slot, :], t["ea64"][bass.ds(g, 1), :, :].squeeze(0)).then_inc(ea_in[slot], 16)

                def load(u, j, r):
                    if r % 2 == 0:
                        g = j * 2 + r // 2 + 1
                        if runs(g, NGRP):
                            load_ea64(g, (r // 2 + 1) % 2)
                    since(sp, same_done, u - 3)
                    sp.dma_start(src_bc[:, r, :, :].rearrange("p k e -> p (k e)"),
                                 t["src_pairs_f"][bass.ds(u, 1), :].to_broadcast([P, 2 * P])).then_inc(sb_in[r], 16)
                load_ea64(0, 0)
                split_steps(sp, NPAIR, 0, load, 4, short=4)

            @block.gpsimd
            def _(pool):
                def step(s, j, r):
                    if runs(s, NPAIR):
                        since(pool, feat_done, s - 3)
                        if r % 4 == 0:
                            pool.tensor_copy(gidx[:, r // 4, :], dst_i[:, bass.ds(s * 2, 8)]).then_inc(gidx_done4, 1)
                            since(pool, gidx_done4, j * 2 + r // 4 + 1)
                        if not isinstance(s, int):
                            pool.sem_inc(passed, 1)
                        for k in range(2):
                            at = r % 4 * 2 + k
                            pool.indirect_dma_start(
                                out=xg[:, r % 4, k, :], out_offset=None, in_=t["f1"],
                                in_offset=bass.IndirectOffsetOnAxis(ap=gidx[:, r // 4, at:at + 1], axis=0),
                            ).then_inc(g_in[r % 4], 16)
                    u, uj, ur = lagged(s, j, r, 6, 8)
                    if runs(u, NPAIR):
                        into = [(ur * 2 + k) % NTAB for k in range(2)]
                        for k in range(2):
                            since(pool, tab_in[into[k]], 16 * (uj * 4 + (ur * 2 + k) // NTAB))
                        if ur % 4 == 0:
                            pool.tensor_copy(sidx[:, ur // 4, :], scat_i[:, bass.ds(u * 2, 8)]).then_inc(sidx_done, 1)
                            since(pool, sidx_done, uj * 2 + ur // 4 + 1)
                        settled(pool, sum_done, u + 1, passed)
                        for k in range(2):
                            at = ur % 4 * 2 + k
                            pool.indirect_dma_start(
                                out=t["tabs"][into[k]],
                                out_offset=bass.IndirectOffsetOnAxis(ap=sidx[:, ur // 4, at:at + 1], axis=0),
                                in_=summed[:, ur % 2, k, :], in_offset=None, compute_op=ALU.add,
                                bounds_check=TROWS - 1,
                            ).then_inc(tab_in[into[k]], 16)
                split_steps(pool, NPAIR, 6, step, 8)
                for tab in range(NTAB):
                    pool.wait_ge(tab_in[tab], 16 * (TILES // NTAB))

            @block.scalar
            def _(act):
                def step(s, j, r):
                    if r % 2 == 0:
                        g = j * 2 + r // 2 + 1
                        if runs(g, NGRP):
                            relu(g, (r // 2 + 1) % 2)
                    u, uj, ur = lagged(s, j, r, 1, 4)
                    if runs(u, NPAIR):
                        act.wait_ge(t_ready, u + 1)
                        since(act, o_ready, u - 1)
                        act.activation(featt[:, ur % 2, :, :, :].rearrange("p k a b -> p k (a b)"), ps_t[:, :, 0:384],
                                       ACT.Copy).then_inc(t_done, 1)
                    u, uj, ur = lagged(s, j, r, 2, 4)
                    if runs(u, NPAIR):
                        act.wait_ge(o_ready, u + 1)
                        since(act, d_ready, u - 1)
                        act.activation(msg[:, ur % 2, :, 0:96], ps_o[:, :, 0:96], ACT.Copy).then_inc(os_done, 1)
                    u, uj, ur = lagged(s, j, r, LAST, 4)
                    if runs(u, NPAIR):
                        act.wait_ge(d_ready, u + 1)
                        for k in range(2):
                            t2 = ((ur - 2) * 2 + k) % NTAB
                            turn = uj * 2 + (ur - 2) * 2 // NTAB + 1
                            since(act, tab_in[t2], 16 * turn)
                        act.activation(summed[:, ur % 2, :, :], ps_d[:, :, 0:OW], ACT.Copy).then_inc(sum_done, 1)

                def relu(g, slot):
                    act.wait_ge(hid_ready, g + 1)
                    since(act, w4_ready, 2 * (g - 1))
                    act.activation(hid[:, slot, :], ps_h[:, :], ACT.Relu).then_inc(relu_done, 1)
                relu(0, 0)
                split_steps(act, NPAIR, LAST, step, 4, short=2)

            @block.tensor
            def _(pe):
                def hidden(g, slot, turn):
                    pe.wait_ge(ea_in[slot], 16 * (turn + 1))
                    since(pe, relu_done, g)
                    pe.matmul(ps_h[:, :], wf1[:, :], ea64[:, slot, :], start=True, stop=True).then_inc(hid_ready, 1)

                def step(s, j, r):
                    if r % 2 == 0:
                        g = j * 2 + r // 2 + 1
                        if runs(g, NGRP):
                            hidden(g, (r // 2 + 1) % 2, j + (r // 2 + 1) // 2)
                    if runs(s, NPAIR):
                        pe.wait_ge(relu_done, j * 2 + r // 2 + 1)
                        since(pe, feat_done, s - 1)
                        h = slice(S * (r % 2), S * (r % 2) + S)
                        for k in range(2):
                            last = pe.matmul(ps_w[r % 2][:, k, 0:224], hid[h, r // 2, P * k:P * k + P], wf2[h, :],
                                             start=True, stop=True)
                        last.then_inc(w4_ready, 1)
                    u, _, ur = lagged(s, j, r, 1, 4)
                    if runs(u, NPAIR):
                        pe.wait_ge(feat_done, u + 1)
                        since(pe, t_done, u)
                        for k in range(2):
                            for c in range(3):
                                last = pe.transpose(ps_t[:, k, P * c:P * c + P], feat[:, ur % 2, k, c, :], ident[:, :])
                        last.then_inc(t_ready, 1)
                    u, _, ur = lagged(s, j, r, 2, 4)
                    if runs(u, NPAIR):
                        pe.wait_ge(t_done, u + 1)
                        since(pe, ov_done, u)
                        since(pe, os_done, u)
                        for k in range(2):
                            pe.matmul(ps_o[:, k, 0:96], featt[:, ur % 2, k, 0, :], ro_s[:, :], start=True, stop=True)
                            for c in range(2):
                                last = pe.matmul(ps_o[:, k, 96 + 64 * c:192 + 64 * c], featt[:, ur % 2, k, 1 + c, :],
                                                 ro_v[:, c, :], start=True, stop=True)
                        last.then_inc(o_ready, 1)
                    u, _, ur = lagged(s, j, r, LAST, 4)
                    if runs(u, NPAIR):
                        pe.wait_ge(os_done, u + 1)
                        pe.wait_ge(ov_done, u + 1)
                        pe.wait_ge(same_done, u + 1)
                        since(pe, sum_done, u)
                        for k in range(2):
                            last = pe.matmul(ps_d[:, k, 0:OW], same[:, ur, k, :], msg[:, ur % 2, k, :],
                                             start=True, stop=True)
                        last.then_inc(d_ready, 1)
                hidden(0, 0, 0)
                split_steps(pe, NPAIR, LAST, step, 4, short=2)

            @block.vector
            def _(dve):
                dve.memset(feat[:, :, :, 0, 96:P], 0.0).then_inc(fz, 1)

                def products(u, j, r):
                    x = xg[:, r, :, :]
                    dve.wait_ge(g_in[r], 32 * (j + 1))

                    def shv(c):
                        return sh[:, bass.ds(u * 2, 2), c:c + 3].unsqueeze(3).to_broadcast([P, 2, 3, V])

                    def xv(c):
                        return x[:, :, S + V * c:S + V * c + 3 * V].rearrange("p k (c u) -> p k c u", c=3)
                    since(dve, xx_done, 3 * u)
                    dve.tensor_tensor(mm[:, 0, :, :, :], xv(0), shv(0), ALU.mult)
                    dve.tensor_tensor(mm[:, 1, :, :, :], xv(1), shv(2), ALU.mult)
                    dve.tensor_tensor(mm[:, 2, :, :, :], xv(2), shv(1), ALU.mult).then_inc(m_done, 1)
                    dve.wait_ge(m_done, u + 1)
                    since(dve, feat_done, u)
                    dve.tensor_tensor(qq[:, 0, :, :], mm[:, 0, :, 0, :], mm[:, 0, :, 1, :], ALU.add).then_inc(xx_done, 1)
                    dve.tensor_tensor(xx[:, :, :, :], mm[:, 1, :, :, :], mm[:, 2, :, :, :], ALU.subtract).then_inc(xx_done, 1)
                    dve.wait_ge(xx_done, 3 * u + 1)
                    dve.tensor_tensor(qq[:, 1, :, :], qq[:, 0, :, :], mm[:, 0, :, 2, :], ALU.add).then_inc(xx_done, 1)
                    dve.wait_ge(w4_ready, u + 1)
                    since(dve, t_ready, u - 1)
                    p = r % 2
                    w = ps_w[p]
                    dve.tensor_tensor(feat[:, p, :, 0:2, 0:S], w[:, :, 0:2 * S].rearrange("p k (a s) -> p k a s", a=2),
                                      x[:, :, 0:S].unsqueeze(2).to_broadcast([P, 2, 2, S]), ALU.mult)
                    flat = feat[:, p, :, :, :].rearrange("p k a b -> p k (a b)")
                    v_part = flat[:, :, P + S:3 * P].rearrange("p k (c x u) -> p k c x u", c=3, x=2)
                    dve.tensor_tensor(v_part[:, :, :, 0, :], w[:, :, 128:160].unsqueeze(2).to_broadcast([P, 2, 3, V]),
                                      xv(0), ALU.mult)
                    dve.wait_ge(xx_done, 3 * u + 3)
                    dve.tensor_tensor(flat[:, :, S:96], w[:, :, 160:192], qq[:, 1, :, :], ALU.mult)
                    dve.tensor_tensor(v_part[:, :, :, 1, :], w[:, :, 192:224].unsqueeze(2).to_broadcast([P, 2, 3, V]),
                                      xx[:, :, :, :], ALU.mult).then_inc(feat_done, 1)

                def equal(u, j, r):
                    dve.wait_ge(sb_in[r], 16 * (j + 1))
                    since(dve, d_ready, u - 3)
                    dve.tensor_tensor(same[:, r, :, :], src_bc[:, r, :, :],
                                      src_f[:, bass.ds(u * 2, 2)].unsqueeze(2).to_broadcast([P, 2, P]),
                                      ALU.is_equal).then_inc(same_done, 1)

                def finish(u, r):
                    dve.wait_ge(os_done, u + 1)
                    since(dve, ov_done, u)
                    dve.tensor_tensor(ash[:, :, :, :], ps_o[:, :, 96:128].unsqueeze(2).to_broadcast([P, 2, 3, V]),
                                      sh[:, bass.ds(u * 2, 2), 0:3].unsqueeze(3).to_broadcast([P, 2, 3, V]),
                                      ALU.mult).then_inc(ash_done, 1)
                    dve.wait_ge(ash_done, u + 1)
                    since(dve, d_ready, u - 1)
                    dve.tensor_tensor(msg[:, r % 2, :, 96:OW], ps_o[:, :, 128:224],
                                      ash[:, :, :, :].rearrange("p k c u -> p k (c u)"), ALU.add).then_inc(ov_done, 1)

                def step(s, j, r):
                    if runs(s, NPAIR):
                        products(s, j, r)
                        equal(s, j, r)
                    u, _, ur = lagged(s, j, r, 2, 4)
                    if runs(u, NPAIR):
                        finish(u, ur)
                split_steps(dve, NPAIR, 2, step, 4)

        with ExitStack() as c5:
            tabs = sb(c5, "tabs", [P, NC, NTAB, FT, OW])
            tsum = sb(c5, "tsum", [P, 2, 2, FT, OW])
            so = sb(c5, "so", [P, 2, FT, OW])
            sg = sb(c5, "sg", [P, 2, FT, 96])
            upd = sb(c5, "upd", [P, 2, FT, D])
            bst5 = sb(c5, "bst5", [P, NT, 6])
            orow = sb(c5, "orow", [P, NC, FT, D])
            tin = [sem(c5, f"tin{i}") for i in range(NC)]
            half_done, half2_done, so_done, sg_done, upd_done, res_done, bs5, mv5 = (
                sem(c5, n) for n in ("half_done", "half2_done", "so_done", "sg_done", "upd_done", "res_done", "bs5", "mv5"))
            lv5, lr5, on_done, ch5, o_out = sem(c5, "lv5"), sem(c5, "lr5"), sem(c5, "on_done"), sem(c5, "ch5"), sem(c5, "o_out")
            block = c5.enter_context(nc.Block())

            @block.sync
            def _(sp):
                for m in range(NC):
                    for k in range(2):
                        sp.dma_start(tabs[:, m, k, :, :], tile_rows(t["tabs"][k], m)).then_inc(tin[m], 16)
                for m in range(NC):
                    sp.wait_ge(on_done, m + 1)
                    sp.dma_start(tile_rows(out, m), orow[:, m, :, :]).then_inc(o_out, 16)
                sp.wait_ge(o_out, 16 * NC)

            @block.gpsimd
            def _(pool):
                for m in range(NC):
                    pool.wait_ge(tin[m], 16 * NTAB)
                    since(pool, so_done, m - 1)
                    pool.tensor_tensor(tsum[:, m % 2, 1, :, :], tabs[:, m, 2, :, :], tabs[:, m, 3, :, :],
                                       ALU.add).then_inc(half2_done, 1)

            @block.scalar
            def _(act):
                for m in range(NC):
                    for k in range(2, NTAB):
                        act.dma_start(tabs[:, m, k, :, :], tile_rows(t["tabs"][k], m)).then_inc(tin[m], 16)
                for m in range(NC):
                    act.wait_ge(so_done, m + 1)
                    since(act, upd_done, m - 1)
                    act.activation(sg[:, m % 2, :, :], so[:, m % 2, :, 0:96], ACT.Sigmoid).then_inc(sg_done, 1)
                act.wait_ge(lv5, 1)
                act.activation(ntmp[:, 0, :], ntmp[:, 1, :], ACT.Sqrt).then_inc(lr5, 1)

            @block.vector
            def _(dve):
                done = [0]

                def link(ins):
                    done[0] += 1
                    ins.then_inc(ch5, 1)
                    dve.wait_ge(ch5, done[0])

                def sums(m):
                    r = m % 2
                    dve.wait_ge(tin[m], 16 * NTAB)
                    dve.tensor_tensor(tsum[:, r, 0, :, :], tabs[:, m, 0, :, :], tabs[:, m, 1, :, :], ALU.add).then_inc(half_done, 1)
                    dve.wait_ge(half_done, m + 1)
                    dve.wait_ge(half2_done, m + 1)
                    dve.tensor_tensor(so[:, r, :, :], tsum[:, r, 0, :, :], tsum[:, r, 1, :, :], ALU.add).then_inc(so_done, 1)

                def update(m):
                    r = m % 2
                    dve.wait_ge(sg_done, m + 1)
                    dve.tensor_tensor(upd[:, r, :, 0:S], so[:, r, :, 0:S], sg[:, r, :, 0:S], ALU.mult)
                    dve.tensor_tensor(upd[:, r, :, S:D].rearrange("p a (c u) -> p a c u", c=3),
                                      so[:, r, :, 96:OW].rearrange("p a (c u) -> p a c u", c=3),
                                      sg[:, r, :, S:96].unsqueeze(2).to_broadcast([P, FT, 3, V]), ALU.mult).then_inc(upd_done, 1)
                    dve.wait_ge(upd_done, m + 1)
                    here = xres[:, m * FT:(m + 1) * FT, :]
                    dve.tensor_tensor(here, here, upd[:, r, :, :], ALU.add).then_inc(res_done, 1)
                    dve.wait_ge(res_done, m + 1)
                    for u in range(m * FT, (m + 1) * FT):
                        dve.bn_stats(bst5[:, u, :], xres[:, u, :]).then_inc(bs5, 1)
                    for u in range(m * FT, (m + 1) * FT):
                        dve.wait_ge(bs5, u + 1)
                        dve.bn_aggr(mv[:, u, :], bst5[:, u, :]).then_inc(mv5, 1)

                for m in range(NC + 1):
                    if m < NC:
                        sums(m)
                    if m:
                        update(m - 1)
                dve.wait_ge(mv5, NT)
                layer_norm_scale(dve, link, mv, ntmp, rstd, lv5, lr5, slice(0, NT), 1)
                for u in range(NT):
                    m, at = divmod(u, FT)
                    mean, scale = mv[:, u, 0:1], rstd[:, u:u + 1]
                    dve.tensor_scalar(orow[:, m, at, 0:S], xres[:, u, 0:S], mean, scale, ALU.subtract, ALU.mult)
                    last = dve.tensor_scalar(orow[:, m, at, S:D].rearrange("p (u c) -> p c u", c=3),
                                             xres[:, u, S:D].rearrange("p (c u) -> p c u", c=3), mean, scale,
                                             ALU.subtract, ALU.mult)
                    if at == FT - 1:
                        last.then_inc(on_done, 1)


def layer_norm_scale(dve, link, mv, ntmp, rstd, var_ready, root_ready, tiles, turn):
    root, var, scale = ntmp[:, 0, tiles], ntmp[:, 1, tiles], rstd[:, tiles]
    dve.tensor_scalar(var, mv[:, tiles, 1], EPS, None, ALU.add).then_inc(var_ready, 1)
    dve.wait_ge(root_ready, turn)
    link(dve.reciprocal(scale, root))
    link(dve.tensor_tensor(root, scale, scale, ALU.mult))
    link(dve.tensor_tensor(root, root, var, ALU.mult))
    link(dve.tensor_scalar(root, root, -0.5, 1.5, ALU.mult, ALU.add))
    link(dve.tensor_tensor(scale, scale, root, ALU.mult))


def split_steps(eng, units, lag, body, unroll=2, short=0):
    first = -(-(lag + 2) // unroll) * unroll
    last = max(first, (units - short) // unroll * unroll)
    for s in range(first):
        body(s, s // unroll, s % unroll)
    if last > first:
        with eng.Fori(first // unroll, last // unroll) as j:
            for r in range(unroll):
                body(j * unroll + r, j, r)
    for s in range(last, units + lag):
        body(s, s // unroll, s % unroll)


def kernel(**inputs):
    import numpy as np
    import concourse.bacc as bacc
    from concourse.bass_utils import run_bass_kernel_spmd

    nc = bacc.Bacc("TRN2", target_bir_lowering=False, num_devices=1)
    arr = {k: np.asarray(v) for k, v in inputs.items()}

    def pad(a, n, value):
        full = np.full((n,) + a.shape[1:], value, a.dtype)
        full[:a.shape[0]] = a
        return full

    def cols(a):
        return np.ascontiguousarray(a.reshape(-1, P, *a.shape[1:]).swapaxes(0, 1))

    x = pad(arr["x"], NP, 0)
    x = np.concatenate([x[:, :S], x[:, S:].reshape(NP, V, 3).transpose(0, 2, 1).reshape(NP, 3 * V)], 1)
    src, dst = pad(arr["src"], EP, N), pad(arr["dst"], EP, N)
    ea8, ea64 = pad(arr["edge_attr_8"], EP, 0), pad(arr["edge_attr_64"], EP, 0)
    data = {
        "x_rows": cols(x), "xt": np.ascontiguousarray(x.T),
        "a_col": cols(pad(arr["node_vec1"][:, 0], NP, 0)),
        "src_col": cols(src), "dst_col": cols(dst), "src_rows": src.reshape(NGRP, GE),
        "dst_first": np.ascontiguousarray(dst[::GE]).reshape(1, NGRP),
        "ea3": cols(pad(arr["edge_attr_3"], EP, 1)), "ea4": cols(pad(arr["edge_attr_4"], EP, 0)),
        "ea8": np.ascontiguousarray(ea8.reshape(NGRP, 2, 256, 8).transpose(1, 3, 0, 2)).reshape(16, NGRP * 256),
        "ea64": np.ascontiguousarray(ea64.reshape(NGRP, 2, 256, 64).transpose(0, 1, 3, 2)).reshape(NGRP, P, 256),
    }
    for name in arr:
        if name.startswith(("L0_gnn_W", "L1_gnn_W")):
            data[name] = arr[name]
    arrays, t = {}, {}
    for name, a in data.items():
        arrays["in_" + name] = np.ascontiguousarray(a)
        t[name] = nc.dram_tensor("in_" + name, a.shape, mybir.dt.from_np(a.dtype), kind="ExternalInput").ap()

    def scratch(name, shape):
        return nc.dram_tensor(name, shape, F32, kind="Internal").ap()
    t["f0"] = scratch("f0", (NP, D))
    t["f1"] = scratch("f1", (NP, GW))
    t["src_rows_f"] = scratch("src_rows_f", (NGRP, GE))
    t["src_pairs_f"] = t["src_rows_f"].rearrange("g (k e) -> (g k) e", k=2)
    t["tabs"] = [scratch(f"tab{i}", (TROWS, OW)) for i in range(NTAB)]
    out = nc.dram_tensor("out", (NP, D), F32, kind="ExternalOutput").ap()
    gnn_kernel(nc, t, out)
    r = run_bass_kernel_spmd(nc, [arrays], core_ids=[0])
    return r.results[0]["out"][:N]
```
